# Optimizing a Trainium2 kernel written in Bass

```python
import numpy as np
import jax
import jax.numpy as jnp

def _softmax(x, axis=-1):
    return jax.nn.softmax(x, axis=axis)

def _gelu(x):
    return jax.nn.gelu(x, approximate=True)

def _silu(x):
    return jax.nn.silu(x)

def _sigmoid(x):
    return jax.nn.sigmoid(x)

def _layernorm(x, axis=-1, eps=1e-05):
    m = jnp.mean(x, axis=axis, keepdims=True)
    v = jnp.var(x, axis=axis, keepdims=True)
    return (x - m) / jnp.sqrt(v + eps)

def _scatter_add(tgt, idx, src, axis=0):
    return tgt.at[idx].add(src)

def _segment_sum(src, seg, n):
    return jax.ops.segment_sum(src, seg, n)
kernel_name = 'mk_gnn_ffn_d1_gnn_r8_33d9b1'

def setup_inputs(seed: int=0):
    np.random.seed(seed)
    _w = jnp.asarray

    def _rec_inputs():
        import jax
        import jax.numpy as jnp
        _gk = jax.random.key(seed)
        x = -0.0002117 + 1 * jax.random.normal(jax.random.fold_in(_gk, 1), (6250, 512), jnp.float32)
        _s = jax.random.randint(jax.random.fold_in(_gk, 2), (50000,), 0, 6250, jnp.int32)
        _d = jax.random.randint(jax.random.fold_in(_gk, 3), (50000,), 0, 6250, jnp.int32)
        _loop = jnp.arange(6250, dtype=jnp.int32)
        src = jnp.concatenate([_s, _d, _loop])
        dst = jnp.concatenate([_d, _s, _loop])
        _o = jnp.argsort(dst, stable=True)
        src = src[_o]
        dst = dst[_o]
        return (x, src, dst)
    x, src, dst = _rec_inputs()

    def _L0_gnn_setup():
        import jax, jax.numpy as jnp
        import numpy as np
        N, E, D = (6250, 50000, 512)
        EPS = 1e-05
        key = jax.random.key(seed)
        ks = jax.random.split(key, 5)
        scale = 1.0 / np.sqrt(D)
        x = jax.random.normal(ks[0], (N, D), dtype=jnp.float32)
        edge_index = jax.random.randint(ks[1], (2, E), 0, N, dtype=jnp.int32)
        W_l = jax.random.normal(ks[2], (D, D), dtype=jnp.float32) * scale
        b_l = jnp.zeros((D,), dtype=jnp.float32)
        W_r = jax.random.normal(ks[3], (D, D), dtype=jnp.float32) * scale
        gamma = jnp.ones((D,), dtype=jnp.float32)
        beta = jnp.zeros((D,), dtype=jnp.float32)
        return {'x': x, 'edge_index': edge_index, 'W_l': W_l, 'b_l': b_l, 'W_r': W_r, 'gamma': gamma, 'beta': beta}
    _L0_gnn_all = _L0_gnn_setup()
    _L0_gnn_in = {k: v for k, v in _L0_gnn_all.items() if k in ('W_l', 'b_l', 'W_r', 'gamma', 'beta')}
    del _L0_gnn_all

    def _L0_ffn_setup():
        import jax, jax.numpy as jnp
        import numpy as np
        D, H, E, K = (512, 256, 8, 2)
        EPS = 1e-05

        def _ln(x, g, b):
            m = jnp.mean(x, axis=-1, keepdims=True)
            v = jnp.var(x, axis=-1, keepdims=True)
            return (x - m) * jax.lax.rsqrt(v + EPS) * g + b
        key = jax.random.key(seed)
        ks = jax.random.split(key, 12)
        s = 0.02
        return {'x': jax.random.normal(ks[0], (2, 256, D), jnp.float32), 'Wg1': jax.random.normal(ks[1], (D, 2 * E), jnp.float32) * s, 'bg1': jnp.zeros((2 * E,), jnp.float32), 'Wg2': jax.random.normal(ks[2], (2 * E, E), jnp.float32) * s, 'bg2': jnp.zeros((E,), jnp.float32), 'W1': jax.random.normal(ks[3], (E, D, H), jnp.float32) * s, 'b1': jnp.zeros((E, H), jnp.float32), 'g1': jnp.ones((E, H), jnp.float32), 'be1': jnp.zeros((E, H), jnp.float32), 'W2': jax.random.normal(ks[4], (E, H, H), jnp.float32) * s, 'b2': jnp.zeros((E, H), jnp.float32), 'g2': jnp.ones((E, H), jnp.float32), 'be2': jnp.zeros((E, H), jnp.float32), 'W3': jax.random.normal(ks[5], (E, H, D), jnp.float32) * s, 'b3': jnp.zeros((E, D), jnp.float32)}
    _L0_ffn_all = _L0_ffn_setup()
    _L0_ffn_in = {k: v for k, v in _L0_ffn_all.items() if k in ('Wg1', 'bg1', 'Wg2', 'bg2', 'W1', 'b1', 'g1', 'be1', 'W2', 'b2', 'g2', 'be2', 'W3', 'b3')}
    del _L0_ffn_all
    return {'x': x, 'src': src, 'dst': dst, 'L0_gnn_W_l': _L0_gnn_in['W_l'], 'L0_gnn_b_l': _L0_gnn_in['b_l'], 'L0_gnn_W_r': _L0_gnn_in['W_r'], 'L0_gnn_gamma': _L0_gnn_in['gamma'], 'L0_gnn_beta': _L0_gnn_in['beta'], 'L0_ffn_Wg1': _L0_ffn_in['Wg1'], 'L0_ffn_bg1': _L0_ffn_in['bg1'], 'L0_ffn_Wg2': _L0_ffn_in['Wg2'], 'L0_ffn_bg2': _L0_ffn_in['bg2'], 'L0_ffn_W1': _L0_ffn_in['W1'], 'L0_ffn_b1': _L0_ffn_in['b1'], 'L0_ffn_g1': _L0_ffn_in['g1'], 'L0_ffn_be1': _L0_ffn_in['be1'], 'L0_ffn_W2': _L0_ffn_in['W2'], 'L0_ffn_b2': _L0_ffn_in['b2'], 'L0_ffn_g2': _L0_ffn_in['g2'], 'L0_ffn_be2': _L0_ffn_in['be2'], 'L0_ffn_W3': _L0_ffn_in['W3'], 'L0_ffn_b3': _L0_ffn_in['b3']}

def reference(x, src, dst, L0_gnn_W_l, L0_gnn_b_l, L0_gnn_W_r, L0_gnn_gamma, L0_gnn_beta, L0_ffn_Wg1, L0_ffn_bg1, L0_ffn_Wg2, L0_ffn_bg2, L0_ffn_W1, L0_ffn_b1, L0_ffn_g1, L0_ffn_be1, L0_ffn_W2, L0_ffn_b2, L0_ffn_g2, L0_ffn_be2, L0_ffn_W3, L0_ffn_b3):
    import jax
    import jax.numpy as jnp

    def _L0_gnn_ref(x, edge_index, W_l, b_l, W_r, gamma, beta):
        import jax, jax.numpy as jnp
        import numpy as np
        N, E, D = (6250, 50000, 512)
        EPS = 1e-05
        n = x.shape[0]
        src, dst = (edge_index[0], edge_index[1])
        agg = jax.ops.segment_sum(x[src], dst, num_segments=n)
        cnt = jax.ops.segment_sum(jnp.ones((src.shape[0],), x.dtype), dst, num_segments=n)
        mean_agg = agg / jnp.maximum(cnt, 1.0)[:, None]
        h = mean_agg @ W_l.T + b_l + x @ W_r.T
        mu = jnp.mean(h, axis=0)
        var = jnp.var(h, axis=0)
        h = (h - mu) * jax.lax.rsqrt(var + EPS) * gamma + beta
        return jax.nn.relu(h) + x

    def _L0_ffn_ref(x, Wg1, bg1, Wg2, bg2, W1, b1, g1, be1, W2, b2, g2, be2, W3, b3):
        import jax, jax.numpy as jnp
        import numpy as np
        D, H, E, K = (512, 256, 8, 2)
        EPS = 1e-05

        def _ln(x, g, b):
            m = jnp.mean(x, axis=-1, keepdims=True)
            v = jnp.var(x, axis=-1, keepdims=True)
            return (x - m) * jax.lax.rsqrt(v + EPS) * g + b
        B, S, d = x.shape
        t = x.reshape(-1, d)
        logits = jax.nn.gelu(t @ Wg1 + bg1, approximate=False) @ Wg2 + bg2
        gates_full = jax.nn.softmax(logits, axis=-1)
        topv, topi = jax.lax.top_k(gates_full, K)
        topv = topv / jnp.sum(topv, axis=-1, keepdims=True)
        cw = jnp.sum(jax.nn.one_hot(topi, E, dtype=t.dtype) * topv[..., None], axis=1)
        h = jnp.einsum('td,edh->eth', t, W1) + b1[:, None, :]
        h = jax.nn.gelu(_ln(h, g1[:, None, :], be1[:, None, :]), approximate=False)
        h = jnp.einsum('eth,ehg->etg', h, W2) + b2[:, None, :]
        h = jax.nn.gelu(_ln(h, g2[:, None, :], be2[:, None, :]), approximate=False)
        o = jnp.einsum('eth,eho->eto', h, W3) + b3[:, None, :]
        out = jnp.einsum('te,eto->to', cw, o)
        return out.reshape(B, S, -1)
    edge_index = jnp.stack([src, dst])
    x = x + _L0_gnn_ref(_layernorm(x, axis=-1), edge_index, L0_gnn_W_l, L0_gnn_b_l, L0_gnn_W_r, L0_gnn_gamma, L0_gnn_beta)
    x = x + _L0_ffn_ref(_layernorm(x, axis=-1)[None], L0_ffn_Wg1, L0_ffn_bg1, L0_ffn_Wg2, L0_ffn_bg2, L0_ffn_W1, L0_ffn_b1, L0_ffn_g1, L0_ffn_be1, L0_ffn_W2, L0_ffn_b2, L0_ffn_g2, L0_ffn_be2, L0_ffn_W3, L0_ffn_b3)[0]
    return x

_drawn_inputs = setup_inputs


def setup_inputs(seed=0):
    import zlib

    import numpy as np

    out = dict(_drawn_inputs(seed))
    spreads = {'L0_gnn_b_l': (0.0, 0.8),
     'L0_gnn_gamma': (1.0, 0.2),
     'L0_gnn_beta': (0.0, 0.1),
     'L0_ffn_bg1': (0.0, 0.28),
     'L0_ffn_bg2': (0.0, 0.1),
     'L0_ffn_b1': (0.0, 0.545),
     'L0_ffn_g1': (1.0, 0.6),
     'L0_ffn_be1': (0.0, 0.8),
     'L0_ffn_b2': (0.0, 0.1),
     'L0_ffn_g2': (1.0, 0.6),
     'L0_ffn_be2': (0.0, 0.8),
     'L0_ffn_b3': (0.0, 0.1)}
    factors = {}
    for name, (base, spread) in spreads.items():
        noise = np.random.default_rng([zlib.crc32(name.encode()), seed]).standard_normal(out[name].shape)
        drawn = base * np.exp(spread * noise) if base else spread * noise
        out[name] = jnp.asarray(drawn.astype(out[name].dtype))
    for name, factor in factors.items():
        out[name] = (out[name] * factor).astype(out[name].dtype)
    return out
```

```python
from contextlib import ExitStack

import concourse.bass as bass
from concourse import mybir

P = 128
N, D, H, E = 6250, 512, 256, 8
EDGES = 106250
G = 2 * E
TILES = -(-N // P)
LAST = N - (TILES - 1) * P
NPAD = TILES * P
KD, KH = D // P, H // P
ETILES = -(-EDGES // P)
ECHUNKS = -(-(ETILES + 8) // P)
ECOLS = ECHUNKS * P
RING = 8
NO_NODE = 8000
FAR = 9999.0
EPS = 1e-5
TABLE = 1024.0
WALL = E * KD * H + E * KH * H + E * KH * D
W2_AT, W3_AT = E * KD * H, E * KD * H + E * KH * H


def places(nc, stage):
    def sb(name, shape, dt):
        return stage.enter_context(nc.sbuf_tensor(name, shape, dt))

    def pb(name, shape, dt):
        return stage.enter_context(nc.psum_tensor(name, shape, dt))

    def sem(name):
        return stage.enter_context(nc.semaphore(name))

    return sb, pb, sem


def wait_apart(eng, met, k, signal, value):
    if not isinstance(value, int):
        value = eng.snap(value)
    eng.wait_ge(met, k)
    eng.wait_ge(signal, value)


def build(nc, x, src_t, dst_t, dst_r, wl_t, wr_t, bl_b, gamma_t, beta_t, wall, wg1, bg1_b,
          bias_rows, row_mask, sel_in, wg2b, g1_t, be1_t, g2_t, be2_t, out):
    f32, f32r, f16, i32 = mybir.dt.float32, mybir.dt.float32r, mybir.dt.float16, mybir.dt.int32
    u32, bf16 = mybir.dt.uint32, mybir.dt.bfloat16
    ALU, ACT, AX = mybir.AluOpType, mybir.ActivationFunctionType, mybir.AxisListType

    with ExitStack() as whole:
        sb, pb, sem = places(nc, whole)

        table = nc.dram_tensor("table", (NPAD, 2 * D), f16).ap()
        h_rows = nc.dram_tensor("h_rows", (NPAD, D), f32).ap()

        ident = sb("ident", [P, P], f32)
        ident16 = sb("ident16", [P, P], f16)
        ones32 = sb("ones32", [P, P], f32)
        s_const = sem("s_const")
        s_ident = sem("s_ident")
        bnmv = sb("bnmv", [P, KD, 2], f32)

        with ExitStack() as stage:
            sb, pb, sem = places(nc, stage)

            NX = 4
            stats = sb("stats", [P, KD, TILES, 6], f32)
            one16 = sb("one16", [P, 2], f16)
            zero16 = sb("zero16", [P, D], f16)
            iota_j = sb("iota_j", [P, P], f32)
            xin = sb("xin", [P, NX, D], f32)
            lst = sb("lst", [P, NX, 6], f32)
            mv = sb("mv", [P, NX, 2], f32)
            var_s = sb("var_s", [P, NX], f32)
            mhalf = sb("mhalf", [P, 1], f32)
            rstd = sb("rstd", [P, NX], f32)
            xs = sb("xs", [P, NX, D], f32)
            pair = sb("pair", [P, NX, 2 * D], f16)
            s_x = [sem(f"s_x{u}") for u in range(NX)]
            s_store = [sem(f"s_store{u}") for u in range(NX)]
            s_lst, s_mv, s_var, s_r, s_xs, s_hi, s_lo = (
                sem(f"s_t_{n}") for n in ("lst", "mv", "var", "r", "xs", "hi", "lo"))

            srcc = sb("srcc", [P, ECOLS], i32)
            dsti = sb("dsti", [P, ECOLS], i32)
            dstc = sb("dstc", [P, ECOLS], f32)
            dri = sb("dri", [P, ECHUNKS, P], i32)
            drf = sb("drf", [P, ECHUNKS, P], f32)
            dmin = sb("dmin", [P, ECHUNKS], f32)
            dmax = sb("dmax", [P, ECHUNKS], f32)
            etp1 = sb("etp1", [P, ECHUNKS], f32)
            etneg = sb("etneg", [P, ECHUNKS], f32)
            base = sb("base", [P, TILES], f32)
            topn = sb("topn", [P, TILES], f32)
            negb = sb("negb", [P, TILES], f32)
            rel0 = sb("rel0", [P, TILES], f32)
            rel = sb("rel", [P, TILES], f32)
            ends = sb("ends", [P, 2, TILES], f32)
            endr = sb("endr", [P, 2, TILES], f32)
            first_t = sb("first_t", [1, TILES], i32)
            end_t = sb("end_t", [1, TILES], i32)
            first_f = sb("first_f", [1, TILES], f32)
            s_edge = sem("s_edge")
            s_iota = sem("s_iota")
            s_bd = sem("s_bd")
            s_all = sem("s_all")
            s_bounds = sem("s_bounds")

            wst = sb("wst", [P, 2, KD, D], f32)
            w_hi = sb("w_hi", [P, 2, KD, D], f32r)
            w_lo = sb("w_lo", [P, 2, KD, D], f32r)
            bl = sb("bl", [P, D], f32)
            s_wst = sem("s_wst")
            s_whi = sem("s_whi")
            s_wlo = sem("s_wlo")

            idx = sb("idx", [P, RING], i32)
            rows = sb("rows", [P, RING, 2 * D], f16)
            hot = sb("hot", [P, RING, P], f16)
            cden = sb("cden", [P, 2], f32)
            rcnt = sb("rcnt", [P, 2], f32)
            mean = sb("mean", [P, 2, D], f32)
            xt = sb("xt", [P, 2, 2 * D], f16)
            m_hi = sb("m_hi", [P, KD, P], f32r)
            m_lo = sb("m_lo", [P, KD, P], f32r)
            x_hl = sb("x_hl", [P, 2 * KD, P], f32r)
            hs = sb("hs", [P, 2, D], f32)
            agg = [pb(f"agg{v}", [P, D], f32) for v in range(2)]
            cnt = [pb(f"cnt{v}", [P, D], f32) for v in range(2)]
            ps_m = pb("ps_m", [P, KD, P], f32)
            ps_x = pb("ps_x", [P, 2 * KD, P], f16)
            ps_h = pb("ps_h", [P, D], f32)
            ps_ht = pb("ps_ht", [P, KD, P], f32)
            s_rows0 = sem("s_rows0")
            s_idx = sem("s_idx")
            s_hot = sem("s_hot")
            s_got = [sem(f"s_got{k}") for k in range(RING)]
            s_used = sem("s_used")
            s_agg, s_cden, s_rcnt, s_mean, s_trm, s_trx, s_mhi, s_mlo, s_xhl, s_h, s_hs, s_tht, s_bs = (
                sem(f"s_a_{n}") for n in ("agg", "cden", "rcnt", "mean", "trm", "trx", "mhi", "mlo",
                                          "xhl", "h", "hs", "tht", "bs"))
            s_xt = [sem(f"s_xt{v}") for v in range(2)]
            s_hst = [sem(f"s_hst{v}") for v in range(2)]

            def tiles4(eng, body):
                for u in range(NX):
                    body(u, 0, u)
                with eng.Fori(1, TILES // NX) as i:
                    for u in range(NX):
                        body(i * NX + u, i, u)
                body(TILES - 1, TILES // NX, 0)

            def is_first(t):
                return isinstance(t, int) and t < NX

            def is_last(t):
                return isinstance(t, int) and t == TILES - 1

            def gather_then_linear(eng, gather, linear):
                gather(0, 0)
                gather(1, 1)
                linear(0, 0, 0)
                gather(2, 0)
                linear(1, 0, 1)
                with eng.Fori(1, TILES // 2) as i:
                    gather(i * 2 + 1, 1)
                    linear(i * 2, i, 0)
                    gather(i * 2 + 2, 0)
                    linear(i * 2 + 1, i, 1)
                linear(TILES - 1, TILES // 2, 0)

            block = stage.enter_context(nc.Block())

            @block.sync
            def _(sp):
                for t in range(NX):
                    sp.dma_start(xin[:, t, :], x[t * P:(t + 1) * P, :]).then_inc(s_x[t], 16)
                sp.dma_start(srcc[:, :], src_t).then_inc(s_edge, 16)
                sp.dma_start(dsti[:, :], dst_t).then_inc(s_edge, 16)
                sp.dma_start(dri[:, :, :], dst_r).then_inc(s_edge, 16)
                sp.dma_start(wst[:, 0, :, :], wl_t).then_inc(s_wst, 16)
                sp.dma_start(wst[:, 1, :, :], wr_t).then_inc(s_wst, 16)
                sp.dma_start(bl[:, :], bl_b).then_inc(s_wst, 16)

                def store(t, i, u):
                    sp.wait_ge(s_hi, t + 1)
                    sp.wait_ge(s_lo, t + 1)
                    sp.dma_start(table[bass.ds(t * P, P), :], pair[:, u, :]).then_inc(s_store[u], 16)

                def load(t, u, n=P):
                    sp.wait_ge(s_xs, t - NX + 1)
                    sp.dma_start(xin[0:n, u, :], x[bass.ds(t * P, n), :]).then_inc(s_x[u], 16)

                for u in range(NX):
                    load(NX + u, u)
                    store(u, 0, u)
                with sp.Fori(1, TILES // NX - 1) as i:
                    for u in range(NX):
                        load(i * NX + u + NX, u)
                        store(i * NX + u, i, u)
                load(TILES - 1, 0, LAST)
                for u in range(NX):
                    store(TILES - 1 - NX + u, TILES // NX - 1, u)
                store(TILES - 1, TILES // NX, 0)
                for u in range(NX):
                    sp.wait_ge(s_store[u], 16 * (TILES // NX + (u == 0)))

                def fetch(t, i, v):
                    if not (isinstance(t, int) and t < 2):
                        sp.wait_ge(s_trx, t - 1)
                    sp.dma_start(xt[:, v, :], table[bass.ds(t * P, P), :]).then_inc(s_xt[v], 16)

                def keep(t, i, v):
                    sp.wait_ge(s_hs, t + 1)
                    sp.dma_start(h_rows[bass.ds(t * P, P), :], hs[:, v, :]).then_inc(s_hst[v], 16)

                fetch(0, 0, 0)
                fetch(1, 0, 1)
                with sp.Fori(0, TILES // 2 - 1) as i:
                    keep(i * 2, i, 0)
                    fetch(i * 2 + 2, i + 1, 0)
                    keep(i * 2 + 1, i, 1)
                    fetch(i * 2 + 3, i + 1, 1)
                keep(TILES - 3, 0, 0)
                fetch(TILES - 1, 0, 0)
                keep(TILES - 2, 0, 1)
                keep(TILES - 1, 0, 0)
                sp.wait_ge(s_hst[0], 16 * (TILES // 2 + 1))
                sp.wait_ge(s_hst[1], 16 * (TILES // 2))

            @block.gpsimd
            def _(pool):
                nc.gpsimd.memset(ident[:, :], 0.0).then_inc(s_ident, 1)
                nc.gpsimd.memset(ones32[:, :], 1.0).then_inc(s_ident, 1)
                pool.wait_ge(s_ident, 2)
                nc.gpsimd.affine_select(out=ident[:, :], in_=ident[:, :], compare_op=ALU.not_equal,
                                        fill=1.0, base=0, pattern=[[-1, P]],
                                        channel_multiplier=1).then_inc(s_ident, 1)
                pool.wait_ge(s_ident, 3)
                nc.gpsimd.tensor_copy(ident16[:, :], ident[:, :]).then_inc(s_const, 1)
                for tile, first, step, n, per_row in (
                        (iota_j, 0, 1, P, 0), (base, 0, P, TILES, 0), (topn, P - 1, P, TILES, 0),
                        (negb, 0, -P, TILES, 0), (etp1, 1, P, ECHUNKS, 1),
                        (etneg, int(FAR), -P, ECHUNKS, -1)):
                    nc.gpsimd.iota(tile[:, :], pattern=[[step, n]], base=first, channel_multiplier=per_row,
                                   allow_small_or_imprecise_dtypes=True).then_inc(s_iota, 1)

                def power(t, u):
                    pool.wait_ge(s_var, t + 1)
                    nc.gpsimd.tensor_tensor(rstd[:, u:u + 1], var_s[:, u:u + 1], mhalf[:, :],
                                            ALU.pow).then_inc(s_r, 1)

                power(0, 0)

                def low(t, i, u):
                    if not is_last(t):
                        power(t + 1, (u + 1) % NX)
                    pool.wait_ge(s_hi, t + 1)
                    nc.gpsimd.tensor_tensor(pair[:, u, D:], xs[:, u, :], pair[:, u, 0:D],
                                            ALU.subtract).then_inc(s_lo, 1)
                tiles4(pool, low)

                pool.wait_ge(s_bd, 4 + 4 * ECHUNKS)
                nc.gpsimd.partition_all_reduce(endr[:, :, :], ends[:, :, :], P, bass.bass_isa.ReduceOp.max
                                               ).then_inc(s_all, 1)
                for u in range(NX):
                    pool.wait_ge(s_store[u], 16 * (TILES // NX + (u == 0)))
                pool.wait_ge(s_bounds, 3)
                pool.wait_ge(s_rows0, 1)
                groups = pool.alloc_register("groups")
                pool.reg_mov(groups, 0)

                def gather(t, v):
                    first = pool.value_load(first_t[0:1, bass.ds(t, 1)], min_val=0, max_val=ETILES - 1)
                    end = pool.value_load(end_t[0:1, bass.ds(t, 1)], min_val=0, max_val=ETILES)
                    with pool.Fori(first, end, RING) as e:
                        g = pool.snap(groups, min_val=0, max_val=TILES * ETILES)
                        for k in range(RING):
                            pool.wait_ge(s_used, g * RING + (k + 1))
                            nc.gpsimd.tensor_copy(idx[:, k:k + 1], srcc[:, bass.ds(e + k, 1)]
                                                  ).then_inc(s_idx, 1)
                            wait_apart(pool, s_rows0, 1, s_idx, g * RING + (k + 1))
                            with pool.If(e + k < end):
                                pool.indirect_dma_start(
                                    rows[:, k, :], None, table,
                                    bass.IndirectOffsetOnAxis(idx[:, k:k + 1], axis=0),
                                    bounds_check=N - 1, oob_is_err=False).then_inc(s_got[k], 16)
                        pool.reg_add(groups, groups, 1)

                gather_then_linear(pool, gather, lambda t, i, v: None)

            @block.vector
            def _(dve):
                nc.vector.memset(mhalf[:, :], -0.5)
                nc.vector.memset(zero16[:, :], 0.0)
                nc.vector.memset(one16[:, :], 1.0).then_inc(s_const, 1)
                nc.vector.memset(rows[:, :, :], 0.0).then_inc(s_rows0, 1)

                def moments(t, u, i):
                    dve.wait_ge(s_x[u], (i + 1) * 16)
                    nc.vector.bn_stats(lst[:, u, :], xin[:, u, :]).then_inc(s_lst, 1)

                def variance(t, u):
                    nc.vector.bn_aggr(mv[:, u, :], lst[:, u, :]).then_inc(s_mv, 1)
                    dve.wait_ge(s_mv, t + 1)
                    nc.vector.tensor_scalar(var_s[:, u:u + 1], mv[:, u, 1:2], EPS, TABLE ** -2,
                                            ALU.add, ALU.mult).then_inc(s_var, 1)

                moments(0, 0, 0)
                dve.wait_ge(s_lst, 1)
                variance(0, 0)

                def normal(t, i, u):
                    v, j = (u + 1) % NX, i if u + 1 < NX else i + 1
                    if not is_last(t):
                        moments(t + 1, v, j)
                    dve.wait_ge(s_r, t + 1)
                    if not is_first(t):
                        dve.wait_ge(s_lo, t - NX + 1)
                    if not is_last(t):
                        dve.wait_ge(s_lst, t + 2)
                    nc.vector.tensor_scalar(xs[:, u, :], xin[:, u, :], mv[:, u, 0:1], rstd[:, u:u + 1],
                                            ALU.subtract, ALU.mult).then_inc(s_xs, 1)
                    if not is_last(t):
                        variance(t + 1, v)
                tiles4(dve, normal)

                dve.wait_ge(s_edge, 48)
                dve.wait_ge(s_iota, 6)
                nc.vector.tensor_copy(dstc[:, :], dsti[:, :])
                nc.vector.memset(ends[:, :, :], 0.0).then_inc(s_bd, 1)
                nc.vector.tensor_copy(drf[:, :, :], dri[:, :, :]).then_inc(s_bd, 1)
                dve.wait_ge(s_bd, 2)
                nc.vector.tensor_reduce(dmin[:, :], drf[:, :, :], AX.X, ALU.min).then_inc(s_bd, 1)
                nc.vector.tensor_reduce(dmax[:, :], drf[:, :, :], AX.X, ALU.max).then_inc(s_bd, 1)
                dve.wait_ge(s_bd, 4)
                for c in range(ECHUNKS):
                    n = 4 + 4 * c
                    nc.vector.tensor_scalar(rel0[:, :], base[:, :], dmax[:, c:c + 1], None,
                                            ALU.is_le).then_inc(s_bd, 1)
                    dve.wait_ge(s_bd, n + 1)
                    nc.vector.scalar_tensor_tensor(out=rel[:, :], in0=topn[:, :], scalar=dmin[:, c:c + 1],
                                                   in1=rel0[:, :], op0=ALU.is_ge, op1=ALU.mult
                                                   ).then_inc(s_bd, 1)
                    dve.wait_ge(s_bd, n + 2)
                    for j, score in enumerate((etp1, etneg)):
                        nc.vector.scalar_tensor_tensor(out=ends[:, j, :], in0=rel[:, :],
                                                       scalar=score[:, c:c + 1], in1=ends[:, j, :],
                                                       op0=ALU.mult, op1=ALU.max).then_inc(s_bd, 1)
                    dve.wait_ge(s_bd, n + 4)
                dve.wait_ge(s_all, 1)
                nc.vector.tensor_copy(end_t[:, :], endr[0:1, 0, :]).then_inc(s_bounds, 1)
                nc.vector.tensor_scalar(first_f[:, :], endr[0:1, 1, :], -1.0, FAR, ALU.mult, ALU.add
                                        ).then_inc(s_bounds, 1)
                dve.wait_ge(s_bounds, 2)
                nc.vector.tensor_scalar(first_t[:, :], first_f[:, :], float(ETILES - 1), None, ALU.min
                                        ).then_inc(s_bounds, 1)

                dve.wait_ge(s_whi, 1)
                nc.vector.tensor_tensor(w_lo[:, :, :, :], wst[:, :, :, :],
                                        w_hi[:, :, :, :].bitcast(f32), ALU.subtract).then_inc(s_wlo, 1)
                dve.wait_ge(s_bounds, 3)

                groups = dve.alloc_register("groups")
                dve.reg_mov(groups, 0)

                def gather(t, v):
                    first = dve.value_load(first_t[0:1, bass.ds(t, 1)], min_val=0, max_val=ETILES - 1)
                    end = dve.value_load(end_t[0:1, bass.ds(t, 1)], min_val=0, max_val=ETILES)
                    with dve.Fori(first, end, RING) as e:
                        g = dve.snap(groups, min_val=0, max_val=TILES * ETILES)
                        for k in range(RING):
                            dve.wait_ge(s_used, g * RING + (k + 1))
                            nc.vector.tensor_scalar(hot[:, k, :], iota_j[:, :],
                                                    dstc[:, bass.ds(e + k, 1)], negb[:, bass.ds(t, 1)],
                                                    ALU.subtract, ALU.is_equal).then_inc(s_hot, 1)
                        dve.reg_add(groups, groups, 1)
                    dve.wait_ge(s_agg, t + 1)
                    nc.vector.tensor_scalar(cden[:, v:v + 1], cnt[v][:, 0:1], 1.0, TABLE,
                                            ALU.max, ALU.mult).then_inc(s_cden, 1)
                    dve.wait_ge(s_cden, t + 1)
                    nc.vector.reciprocal(rcnt[:, v:v + 1], cden[:, v:v + 1]).then_inc(s_rcnt, 1)

                def linear(t, i, v):
                    dve.wait_ge(s_mhi, t + 1)
                    nc.vector.tensor_tensor(m_lo[:, :, :], ps_m[:, :, :], m_hi[:, :, :].bitcast(f32),
                                            ALU.subtract).then_inc(s_mlo, 1)
                    dve.wait_ge(s_h, t + 1)
                    if not (isinstance(t, int) and t < 2):
                        dve.wait_ge(s_hst[v], 16 * i)
                    nc.vector.tensor_tensor(hs[:, v, :], ps_h[:, :], bl[:, :], ALU.add
                                            ).then_inc(s_hs, 1)
                    dve.wait_ge(s_tht, t + 1)
                    n = LAST if is_last(t) else P
                    for b in range(KD):
                        nc.vector.bn_stats(stats[:, b, bass.ds(t, 1), :], ps_ht[:, b, 0:n]
                                           ).then_inc(s_bs, 1)

                gather_then_linear(dve, gather, linear)
                dve.wait_ge(s_bs, KD * TILES)
                for b in range(KD):
                    nc.vector.bn_aggr(bnmv[:, b, :], stats[:, b, :, :])

            @block.scalar
            def _(act):
                def high(t, i, u):
                    act.wait_ge(s_xs, t + 1)
                    if not is_first(t):
                        act.wait_ge(s_store[u], 16 * i)
                    nc.scalar.activation(pair[:, u, 0:D], xs[:, u, :], ACT.Copy).then_inc(s_hi, 1)
                tiles4(act, high)
                act.wait_ge(s_wst, 48)
                nc.scalar.activation(w_hi[:, :, :, :], wst[:, :, :, :], ACT.Copy).then_inc(s_whi, 1)

                def gather(t, v):
                    act.wait_ge(s_rcnt, t + 1)
                    nc.scalar.activation(mean[:, v, :], agg[v][:, :], ACT.Copy,
                                         scale=rcnt[:, v:v + 1]).then_inc(s_mean, 1)

                def linear(t, i, v):
                    act.wait_ge(s_trm, t + 1)
                    if not (isinstance(t, int) and t == 0):
                        act.wait_ge(s_h, t)
                    nc.scalar.activation(m_hi[:, :, :], ps_m[:, :, :], ACT.Copy).then_inc(s_mhi, 1)
                    act.wait_ge(s_trx, t + 1)
                    nc.scalar.activation(x_hl[:, :, :], ps_x[:, :, :], ACT.Copy, scale=1.0 / TABLE
                                         ).then_inc(s_xhl, 1)
                gather_then_linear(act, gather, linear)

            @block.tensor
            def _(pe):
                pe.sem_inc(s_used, RING)
                pe.wait_ge(s_const, 2)
                pe.wait_ge(s_wlo, 1)
                pe.wait_ge(s_bounds, 3)
                groups = pe.alloc_register("groups")
                got = [pe.alloc_register(f"got{k}") for k in range(RING)]
                for k in range(RING):
                    pe.reg_mov(got[k], 0)
                pe.reg_mov(groups, 0)

                def gather(t, v):
                    first = pe.value_load(first_t[0:1, bass.ds(t, 1)], min_val=0, max_val=ETILES - 1)
                    end = pe.value_load(end_t[0:1, bass.ds(t, 1)], min_val=0, max_val=ETILES)
                    nc.tensor.matmul(agg[v][:, :], zero16[:, 0:P], zero16[:, :], start=True, stop=False)
                    nc.tensor.matmul(cnt[v][:, 0:2], zero16[:, 0:P], zero16[:, 0:2], start=True, stop=False)
                    with pe.Fori(first, end, RING) as e:
                        g = pe.snap(groups, min_val=0, max_val=TILES * ETILES)
                        for k in range(RING):
                            with pe.If(e + k < end):
                                pe.reg_add(got[k], got[k], 16)
                                arrived = pe.snap(got[k], min_val=16)
                                pe.wait_ge(s_hot, g * RING + (k + 1))
                                pe.wait_ge(s_got[k], arrived)
                                nc.tensor.matmul(agg[v][:, :], hot[:, k, :], rows[:, k, 0:D],
                                                 start=False, stop=False)
                                nc.tensor.matmul(agg[v][:, :], hot[:, k, :], rows[:, k, D:],
                                                 start=False, stop=False)
                                nc.tensor.matmul(cnt[v][:, 0:2], hot[:, k, :], one16[:, :],
                                                 start=False, stop=False).then_inc(s_used, 1)
                            with pe.Else():
                                nc.tensor.matmul(cnt[v][:, 0:2], zero16[:, 0:P], zero16[:, 0:2],
                                                 start=False, stop=False).then_inc(s_used, 1)
                        pe.reg_add(groups, groups, 1)
                    nc.tensor.matmul(agg[v][:, :], zero16[:, 0:P], zero16[:, :], start=False, stop=True)
                    nc.tensor.matmul(cnt[v][:, 0:2], zero16[:, 0:P], zero16[:, 0:2], start=False, stop=True
                                     ).then_inc(s_agg, 1)

                def linear(t, i, v):
                    pe.wait_ge(s_mean, t + 1)
                    for b in range(KD):
                        last = nc.tensor.transpose(ps_m[:, b, :], mean[:, v, b * P:(b + 1) * P], ident[:, :])
                    last.then_inc(s_trm, 1)
                    pe.wait_ge(s_xt[v], 16 * (i + 1))
                    for b in range(2 * KD):
                        last = nc.tensor.transpose(ps_x[:, b, :], xt[:, v, b * P:(b + 1) * P], ident16[:, :])
                    last.then_inc(s_trx, 1)
                    pe.wait_ge(s_xhl, t + 1)
                    for b in range(KD):
                        for a, w in ((b, w_hi), (b, w_lo), (KD + b, w_hi)):
                            nc.tensor.matmul(ps_h[:, :], x_hl[:, a, :], w[:, 1, b, :],
                                             start=(b == 0 and w is w_hi and a == b), stop=False)
                    pe.wait_ge(s_mhi, t + 1)
                    pe.wait_ge(s_mlo, t + 1)
                    for b in range(KD):
                        for a, w in ((m_hi, w_hi), (m_hi, w_lo), (m_lo, w_hi)):
                            last = nc.tensor.matmul(ps_h[:, :], a[:, b, :], w[:, 0, b, :],
                                                    start=False, stop=(b == KD - 1 and a is m_lo))
                    last.then_inc(s_h, 1)
                    pe.wait_ge(s_hs, t + 1)
                    if not (isinstance(t, int) and t == 0):
                        pe.wait_ge(s_bs, t * KD)
                    for b in range(KD):
                        last = nc.tensor.transpose(ps_ht[:, b, :], hs[:, v, b * P:(b + 1) * P], ident[:, :])
                    last.then_inc(s_tht, 1)

                gather_then_linear(pe, gather, linear)

        sb, pb, sem = places(nc, whole)
        w_hi = sb("we_hi", [P, WALL], f32r)
        w_lo = sb("we_lo", [P, WALL], f32r)
        scale_r = sb("scale_r", [P, D], f32)
        shift_r = sb("shift_r", [P, D], f32)
        bias_hl = sb("bias_hl", [32, D], f32r)
        sel = sb("sel", [32, 16], f32r)
        wg1_hi = sb("wg1_hi", [P, KD, G], f32r)
        wg1_lo = sb("wg1_lo", [P, KD, G], f32r)
        bg1 = sb("bg1", [P, G], f32)
        wg2 = sb("wg2", [P, E], f32)
        g1, be1, g2, be2 = (sb(n, [P, E * KH], f32) for n in ("g1", "be1", "g2", "be2"))

        with ExitStack() as stage:
            sb, pb, sem = places(nc, stage)

            CH = 2048
            wst = sb("wst2", [P, 2, CH], f32)
            gb = sb("gb", [P, 2, KD], f32)
            small = sb("small", [P, 8], f32)
            mh = sb("mh2", [P, KD], f32)
            bsc = sb("bsc", [P, 2, KD], f32)
            diag = sb("diag", [P, 2, KD, P], f32)
            bstage = sb("bstage", [32, D], f32)
            bh = sb("bh", [32, D], f32r)
            bd = sb("bd", [32, D], f32)
            bh2 = sb("bh2", [32, D], f32)
            rmask = sb("rmask", [32, 2], f32)
            self32 = sb("self32", [32, 16], f32)
            wgst = sb("wgst", [P, KD, G], f32)
            ps_row = [pb(f"ps_row{j}", [P, D], f32) for j in range(2)]
            s_ws = [sem(f"s_ws{j}") for j in range(2)]
            s_wh, s_wl, s_cin, s_zero = sem("s_wh"), sem("s_wl"), sem("s_cin"), sem("s_zero")
            s_bn, s_bp, s_diag, s_row, s_k = sem("s_bn"), sem("s_bp"), sem("s_diag"), sem("s_row"), sem("s_k")
            s_kh = sem("s_kh")
            NCH = WALL // CH

            block = stage.enter_context(nc.Block())

            @block.sync
            def _(sp):
                sp.dma_start(gb[:, 0, :], gamma_t).then_inc(s_cin, 16)
                sp.dma_start(gb[:, 1, :], beta_t).then_inc(s_cin, 16)
                sp.dma_start(bstage[:, :], bias_rows).then_inc(s_cin, 16)
                sp.dma_start(rmask[:, :], row_mask).then_inc(s_cin, 16)
                sp.dma_start(self32[:, :], sel_in).then_inc(s_cin, 16)
                sp.dma_start(wgst[:, :, :], wg1).then_inc(s_cin, 16)
                sp.dma_start(bg1[:, :], bg1_b).then_inc(s_cin, 16)
                for tile, a in ((g1, g1_t), (be1, be1_t), (g2, g2_t), (be2, be2_t)):
                    sp.dma_start(tile[:, :], a).then_inc(s_cin, 16)
                sp.wait_ge(s_zero, 1)
                sp.dma_start(wg2[0:G + 1, :], wg2b).then_inc(s_cin, 16)
                for c in range(NCH):
                    if c >= 2:
                        sp.wait_ge(s_wl, c - 1)
                    sp.dma_start(wst[:, c % 2, :], wall[:, c * CH:(c + 1) * CH]).then_inc(s_ws[c % 2], 16)

            @block.scalar
            def _(act):
                for c in range(NCH):
                    act.wait_ge(s_ws[c % 2], 16 * (c // 2 + 1))
                    nc.scalar.activation(w_hi[:, c * CH:(c + 1) * CH], wst[:, c % 2, :], ACT.Copy
                                         ).then_inc(s_wh, 1)

            @block.gpsimd
            def _(pool):
                nc.gpsimd.memset(mh[:, :], -0.5).then_inc(s_bp, 1)
                nc.gpsimd.memset(wg2[:, :], 0.0).then_inc(s_zero, 1)
                pool.wait_ge(s_bn, KD + 1)
                pool.wait_ge(s_bp, 1)
                nc.gpsimd.tensor_tensor(small[:, 0:KD], small[:, KD:2 * KD], mh[:, :], ALU.pow
                                        ).then_inc(s_bp, 1)

            @block.vector
            def _(dve):
                nc.vector.tensor_scalar(small[:, KD:2 * KD], bnmv[:, :, 1], EPS, None, ALU.add
                                        ).then_inc(s_bn, KD + 1)
                dve.wait_ge(s_bp, 2)
                dve.wait_ge(s_cin, 16 * 12)
                nc.vector.tensor_tensor(bsc[:, 0, :], small[:, 0:KD], gb[:, 0, :], ALU.mult).then_inc(s_k, 1)
                dve.wait_ge(s_k, 1)
                nc.vector.tensor_tensor(mh[:, :], bsc[:, 0, :], bnmv[:, :, 0], ALU.mult).then_inc(s_k, 1)
                dve.wait_ge(s_k, 2)
                nc.vector.tensor_tensor(bsc[:, 1, :], gb[:, 1, :], mh[:, :], ALU.subtract).then_inc(s_k, 1)
                dve.wait_ge(s_k, 3)
                for j in range(2):
                    for b in range(KD):
                        nc.vector.tensor_scalar(diag[:, j, b, :], ident[:, :], bsc[:, j, b:b + 1], None,
                                                ALU.mult).then_inc(s_diag, 1)
                nc.vector.tensor_copy(bh[:, :], bstage[:, :])
                nc.vector.tensor_copy(sel[:, :], self32[:, :])
                nc.vector.tensor_copy(wg1_hi[:, :, :], wgst[:, :, :]).then_inc(s_k, 1)
                dve.wait_ge(s_k, 4)
                nc.vector.tensor_tensor(wg1_lo[:, :, :], wgst[:, :, :], wg1_hi[:, :, :].bitcast(f32),
                                        ALU.subtract)
                nc.vector.tensor_tensor(bd[:, :], bstage[:, :], bh[:, :].bitcast(f32), ALU.subtract)
                nc.vector.tensor_scalar(bh2[:, :], bh[:, :].bitcast(f32), rmask[:, 0:1], None, ALU.mult
                                        ).then_inc(s_k, 1)
                dve.wait_ge(s_k, 5)
                nc.vector.scalar_tensor_tensor(out=bias_hl[:, :], in0=bd[:, :], scalar=rmask[:, 1:2],
                                               in1=bh2[:, :], op0=ALU.mult, op1=ALU.add).then_inc(s_k, 1)
                for c in range(NCH):
                    dve.wait_ge(s_wh, c + 1)
                    nc.vector.tensor_tensor(w_lo[:, c * CH:(c + 1) * CH], wst[:, c % 2, :],
                                            w_hi[:, c * CH:(c + 1) * CH].bitcast(f32), ALU.subtract
                                            ).then_inc(s_wl, 1)
                dve.wait_ge(s_row, 2)
                nc.vector.tensor_copy(scale_r[:, :], ps_row[0][:, :])
                nc.vector.tensor_copy(shift_r[:, :], ps_row[1][:, :])

            @block.tensor
            def _(pe):
                pe.wait_ge(s_diag, 2 * KD)
                for j in range(2):
                    for b in range(KD):
                        last = nc.tensor.matmul(ps_row[j][:, b * P:(b + 1) * P], ones32[:, :],
                                                diag[:, j, b, :], start=True, stop=True)
                    last.then_inc(s_row, 1)

        with ExitStack() as stage:
            sb, pb, sem = places(nc, stage)

            PAIRS = E // 2
            W = 2 * H
            xa = sb("xa", [P, 2, D], f32)
            ht = sb("ht", [P, D], f32)
            pr = sb("pr", [P, 2 * D], f16)
            acc = sb("acc", [P, 2, D], f32)
            t_hi = sb("t_hi", [P, 2, KD, P], f32r)
            t_lo = sb("t_lo", [P, 2, KD, P], f32r)
            z = [sb(f"z{y}", [P, W], f32) for y in range(2)]
            gel = [sb(f"gel{y}", [P, 4, P], f32) for y in range(2)]
            a_hi = [sb(f"a_hi{y}", [P, 4, P], f32r) for y in range(2)]
            a_lo = [sb(f"a_lo{y}", [P, 4, P], f32r) for y in range(2)]
            st = [sb(f"st{y}", [P, 2, 6], f32) for y in range(3)]
            mv = [sb(f"mvy{y}", [P, 2, 2], f32) for y in range(3)]
            ve = [sb(f"ve{y}", [P, 2], f32) for y in range(3)]
            rs = [sb(f"rs{y}", [P, 2], f32) for y in range(3)]
            mhalf = sb("mhalf2", [P, 2], f32)
            euler = sb("euler", [P, E], f32)
            iota8 = sb("iota8", [P, E], f32)
            gpre = sb("gpre", [P, G], f32)
            gbuf = sb("gbuf", [P, P], f32)
            gt = sb("gt", [P, P], f32)
            top = sb("top", [P, 2, 8], f32)
            topi = sb("topi", [P, 8], u32)
            topf = sb("topf", [P, 8], f32)
            lm, ex, gates, ca, cb = (sb(n, [P, E], f32) for n in ("lm", "ex", "gates", "ca", "cb"))
            sums = sb("sums", [P, 4], f32)
            wtop = sb("wtop", [P, 2], f32)
            cw = sb("cw", [P, 2, E], f32)
            ps_1 = [pb(f"ps_1{v}", [P, W], f32) for v in range(2)]
            ps_2 = pb("ps_2", [P, W], f32)
            ps_t = [pb(f"ps_t{y}", [P, 4, P], f32) for y in range(2)]
            ps_3 = [pb(f"ps_3{e}", [P, D], f32) for e in range(2)]
            ps_p = pb("ps_p", [P, 4, P], f32)

            s_c0, s_load, s_loadx = sem("s_c0"), sem("s_load"), [sem("s_lx0"), sem("s_lx1")]
            s_bn1, s_bn2, s_u1, s_u2, s_x1, s_pst, s_pmv, s_pve, s_ppow, s_tn, s_ttr, s_thi, s_tlo = (
                sem(f"s_p_{n}") for n in ("bn1", "bn2", "u1", "u2", "x1", "st", "mv", "ve", "pow",
                                          "tn", "ttr", "thi", "tlo"))
            s_g1, s_gpre, s_gel, s_gtr, s_gt, s_g2, s_lm, s_ex, s_cw = (
                sem(f"s_g_{n}") for n in ("g1", "gpre", "gel", "gtr", "gt", "g2", "lm", "ex", "cw"))
            s_sm = [sem(f"s_sm{k}") for k in range(10)]
            s_l = [sem(f"s_l{y}") for y in range(3)]
            s_st, s_mv, s_ve, s_pow, s_z, s_tr, s_gl, s_ah, s_al = (
                [sem(f"s_{n}{y}") for y in range(2)]
                for n in ("st", "mv", "ve", "pow", "z", "tr", "gl", "ah", "al"))
            s_cmb = sem("s_cmb")
            s_out = [sem("s_out0"), sem("s_out1")]

            def units(eng, body):
                body(0, 0, 0)
                with eng.Fori(0, (TILES - 5) // 2) as j:
                    body(j * 2 + 1, 1, j)
                    body(j * 2 + 2, 0, j + 1)
                for t in range(TILES - 4, TILES + 1):
                    body(t, t % 2, t // 2)

            def lives(t, p, lag):
                return not isinstance(t, int) or 0 <= t * PAIRS + p - lag < TILES * PAIRS

            def before(t, first):
                return not (isinstance(t, int) and t < first)

            block = stage.enter_context(nc.Block())

            @block.sync
            def _(sp):
                def load(t, v, j):
                    n = LAST if isinstance(t, int) and t == TILES - 1 else P
                    if before(t, 1):
                        sp.wait_ge(s_ttr, t)
                        sp.wait_ge(s_u2, t)
                    sp.dma_start(ht[:, :], h_rows[bass.ds(t * P, P), :]).then_inc(s_load, 16)
                    sp.dma_start(pr[:, :], table[bass.ds(t * P, P), :]).then_inc(s_load, 16)
                    if before(t, 2):
                        sp.wait_ge(s_cmb, t * E - 15)
                    sp.dma_start(xa[0:n, v, :], x[bass.ds(t * P, n), :]).then_inc(s_loadx[v], 16)

                def store(t, v, j, n=P):
                    sp.wait_ge(s_cmb, t * E + E)
                    sp.dma_start(out[bass.ds(t * P, n), :], acc[0:n, v, :]).then_inc(s_out[v], 16)

                load(0, 0, 0)
                load(1, 1, 0)

                def step(t, v, j):
                    if not isinstance(t, int) or t <= TILES - 3:
                        load(t + 2, v, j + 1)
                    if before(t, 1):
                        store(t - 1, 1 - v, j, LAST if isinstance(t, int) and t == TILES else P)
                units(sp, step)
                sp.wait_ge(s_out[0], 16 * (TILES // 2 + 1))
                sp.wait_ge(s_out[1], 16 * (TILES // 2))

            @block.gpsimd
            def _(pool):
                nc.gpsimd.memset(mhalf[:, :], -0.5)
                nc.gpsimd.memset(euler[:, :], 2.718281828459045)
                nc.gpsimd.memset(gbuf[:, :], 0.0).then_inc(s_c0, 1)
                pool.wait_ge(s_c0, 1)
                nc.gpsimd.memset(gbuf[:, G:G + 1], 1.0)
                nc.gpsimd.iota(iota8[:, :], pattern=[[1, E]], base=0, channel_multiplier=0,
                               allow_small_or_imprecise_dtypes=True).then_inc(s_c0, 1)
                pool.wait_ge(s_c0, 2)

                def power(y, n, k=2):
                    nc.gpsimd.tensor_tensor(rs[y][:, 0:k], ve[y][:, 0:k], mhalf[:, 0:k], ALU.pow
                                            ).then_inc(s_pow[y] if y < 2 else s_ppow, 1)

                def split(t, p, y, lag):
                    if not lives(t, p, lag):
                        return
                    n = t * PAIRS + (p - lag)
                    pool.wait_ge(s_ah[y], n + 1)
                    nc.gpsimd.tensor_tensor(a_lo[y][:, :, :], gel[y][:, :, :],
                                            a_hi[y][:, :, :].bitcast(f32), ALU.subtract
                                            ).then_inc(s_al[y], 1)

                def normal(t, y, p, lag):
                    if lives(t, p, lag):
                        pool.wait_ge(s_ve[y], t * PAIRS + (p - lag) + 1)
                        power(y, 0)

                def prepare(t):
                    pool.wait_ge(s_pve, t + 1)
                    power(2, t, 1)

                prepare(0)

                def step(t, v, j):
                    for p in range(PAIRS):
                        if p == 2 and not (isinstance(t, int) and t >= TILES - 1):
                            prepare(t + 1)
                        normal(t, 0, p, 0)
                        split(t, p, 0, 1)
                        normal(t, 1, p, 2)
                        if p == 3 and not (isinstance(t, int) and t == TILES):
                            pool.wait_ge(s_lm, t + 1)
                            nc.gpsimd.tensor_tensor(ex[:, :], euler[:, :], lm[:, :], ALU.pow
                                                    ).then_inc(s_ex, 1)
                        split(t, p, 1, 3)
                units(pool, step)

            @block.vector
            def _(dve):
                dve.wait_ge(s_c0, 2)

                def moments(t, p, y, lag):
                    if not lives(t, p, lag):
                        return
                    n = t * PAIRS + (p - lag)
                    src = ps_1[p % 2] if y == 0 else ps_2
                    dve.wait_ge(s_l[y], n + 1)
                    for e in range(2):
                        last = nc.vector.bn_stats(st[y][:, e, :], src[:, e * H:(e + 1) * H])
                    last.then_inc(s_st[y], 1)
                    wait_apart(dve, s_c0, 2, s_st[y], n + 1)
                    for e in range(2):
                        last = nc.vector.bn_aggr(mv[y][:, e, :], st[y][:, e, :])
                    last.then_inc(s_mv[y], 1)
                    dve.wait_ge(s_mv[y], n + 1)
                    nc.vector.tensor_scalar(ve[y][:, :], mv[y][:, :, 1], EPS, None, ALU.add
                                            ).then_inc(s_ve[y], 1)

                def normal(t, p, y, lag):
                    if not lives(t, p, lag):
                        return
                    n = t * PAIRS + (p - lag)
                    src = ps_1[p % 2] if y == 0 else ps_2
                    dve.wait_ge(s_pow[y], n + 1)
                    if before(t, 2) or n >= 1:
                        dve.wait_ge(s_tr[y], n)
                    for e in range(2):
                        last = nc.vector.tensor_scalar(z[y][:, e * H:(e + 1) * H],
                                                       src[:, e * H:(e + 1) * H],
                                                       mv[y][:, e, 0:1], rs[y][:, e:e + 1],
                                                       ALU.subtract, ALU.mult)
                    last.then_inc(s_z[y], 1)

                def combine(t, v, j, p):
                    if not lives(t, p, 4):
                        return
                    n = t * E + (2 * p - E)
                    dve.wait_ge(s_l[2], t * PAIRS + (p - 4) + 1)
                    dve.wait_ge(s_cw, t)
                    if p == 0 and before(t, 3):
                        dve.wait_ge(s_out[1 - v], 16 * (j - 1 if v == 0 else j))
                    for e in range(2):
                        first = p == 0 and e == 0
                        if not first:
                            dve.wait_ge(s_cmb, n + e)
                        nc.vector.scalar_tensor_tensor(
                            out=acc[:, 1 - v, :], in0=ps_3[e][:, :], scalar=cw[:, 1 - v, 2 * p + e:2 * p + e + 1],
                            in1=(xa if first else acc)[:, 1 - v, :], op0=ALU.mult, op1=ALU.add
                        ).then_inc(s_cmb, 1)

                def batch_norm(t, v, j):
                    dve.wait_ge(s_load, t * 32 + 32)
                    dve.wait_ge(s_loadx[v], 16 * (j + 1))
                    nc.vector.tensor_tensor(ht[:, :], ht[:, :], scale_r[:, :], ALU.mult).then_inc(s_bn1, 1)
                    nc.vector.scalar_tensor_tensor(out=xa[:, v, :], in0=pr[:, 0:D], scalar=1.0 / TABLE,
                                                   in1=xa[:, v, :], op0=ALU.mult, op1=ALU.add
                                                   ).then_inc(s_u1, 1)
                    dve.wait_ge(s_bn1, t + 1)
                    nc.vector.tensor_tensor(ht[:, :], ht[:, :], shift_r[:, :], ALU.add).then_inc(s_bn2, 1)
                    dve.wait_ge(s_u1, t + 1)
                    nc.vector.scalar_tensor_tensor(out=xa[:, v, :], in0=pr[:, D:], scalar=1.0 / TABLE,
                                                   in1=xa[:, v, :], op0=ALU.mult, op1=ALU.add
                                                   ).then_inc(s_u2, 1)
                    dve.wait_ge(s_bn2, t + 1)
                    dve.wait_ge(s_u2, t + 1)
                    nc.vector.scalar_tensor_tensor(out=xa[:, v, :], in0=ht[:, :], scalar=0.0,
                                                   in1=xa[:, v, :], op0=ALU.max, op1=ALU.add
                                                   ).then_inc(s_x1, 1)
                    dve.wait_ge(s_x1, t + 1)
                    nc.vector.bn_stats(st[2][:, 0, :], xa[:, v, :]).then_inc(s_pst, 1)
                    wait_apart(dve, s_c0, 2, s_pst, t + 1)
                    nc.vector.bn_aggr(mv[2][:, 0, :], st[2][:, 0, :]).then_inc(s_pmv, 1)
                    dve.wait_ge(s_pmv, t + 1)
                    nc.vector.tensor_scalar(ve[2][:, 0:1], mv[2][:, 0, 1:2], EPS, None, ALU.add
                                            ).then_inc(s_pve, 1)

                def layer_norm(t, v):
                    dve.wait_ge(s_ppow, t + 1)
                    nc.vector.tensor_scalar(ht[:, :], xa[:, v, :], mv[2][:, 0, 0:1], rs[2][:, 0:1],
                                            ALU.subtract, ALU.mult).then_inc(s_tn, 1)

                def low(t, v):
                    dve.wait_ge(s_thi, t + 1)
                    nc.vector.tensor_tensor(t_lo[:, v, :, :], ps_p[:, :, :], t_hi[:, v, :, :].bitcast(f32),
                                            ALU.subtract).then_inc(s_tlo, 1)

                def gate_bias(t):
                    dve.wait_ge(s_g1, t + 1)
                    nc.vector.tensor_tensor(gpre[:, :], ps_p[:, 0, 0:G], bg1[:, :], ALU.add
                                            ).then_inc(s_gpre, 1)

                def logits(t):
                    wait_apart(dve, s_c0, 2, s_g2, t + 1)
                    nc.vector.max(top[:, 0, :], ps_p[:, 0, 0:E]).then_inc(s_sm[0], 1)
                    dve.wait_ge(s_sm[0], t + 1)
                    nc.vector.tensor_scalar(lm[:, :], ps_p[:, 0, 0:E], top[:, 0, 0:1], None, ALU.subtract
                                            ).then_inc(s_lm, 1)

                def weights(t, v):
                    def link(k, ins):
                        ins.then_inc(s_sm[k], 1)
                        wait_apart(dve, s_c0, 2, s_sm[k], t + 1)
                    dve.wait_ge(s_ex, t + 1)
                    link(1, nc.vector.reduce_sum(sums[:, 0:1], ex[:, :], axis=AX.X))
                    link(2, nc.vector.reciprocal(sums[:, 1:2], sums[:, 0:1]))
                    link(3, nc.vector.tensor_scalar(gates[:, :], ex[:, :], sums[:, 1:2], None, ALU.mult))
                    link(4, nc.vector.max(top[:, 1, :], gates[:, :]))
                    link(5, nc.vector.max_index(topi[:, :], top[:, 1, :], gates[:, :]))
                    nc.vector.tensor_copy(topf[:, 0:2], topi[:, 0:2])
                    link(6, nc.vector.tensor_tensor(sums[:, 2:3], top[:, 1, 0:1], top[:, 1, 1:2], ALU.add))
                    link(7, nc.vector.reciprocal(sums[:, 3:4], sums[:, 2:3]))
                    link(8, nc.vector.tensor_scalar(wtop[:, :], top[:, 1, 0:2], sums[:, 3:4], None, ALU.mult))
                    nc.vector.tensor_scalar(ca[:, :], iota8[:, :], topf[:, 0:1], wtop[:, 0:1],
                                            ALU.is_equal, ALU.mult)
                    link(9, nc.vector.tensor_scalar(cb[:, :], iota8[:, :], topf[:, 1:2], wtop[:, 1:2],
                                                    ALU.is_equal, ALU.mult))
                    nc.vector.tensor_tensor(cw[:, v, :], ca[:, :], cb[:, :], ALU.add).then_inc(s_cw, 1)

                batch_norm(0, 0, 0)
                layer_norm(0, 0)
                low(0, 0)

                def step(t, v, j):
                    more = not (isinstance(t, int) and t >= TILES - 1)
                    here = not (isinstance(t, int) and t == TILES)
                    for p in range(PAIRS):
                        moments(t, p, 0, 0)
                        if p == 1 and more:
                            batch_norm(t + 1, 1 - v, j if v == 0 else j + 1)
                        if p == 2 and more:
                            layer_norm(t + 1, 1 - v)
                        if p == 0 and here:
                            gate_bias(t)
                        normal(t, p, 0, 0)
                        moments(t, p, 1, 2)
                        combine(t, v, j, p)
                        if p == 3 and more:
                            low(t + 1, 1 - v)
                        if p == 2 and here:
                            logits(t)
                        if p == 3 and here:
                            weights(t, v)
                        normal(t, p, 1, 2)
                units(dve, step)

            @block.scalar
            def _(act):
                def gelu(t, p, y, lag):
                    if not lives(t, p, lag):
                        return
                    n = t * PAIRS + (p - lag)
                    pair = (p - lag) % PAIRS
                    act.wait_ge(s_tr[y], n + 1)
                    if before(t, 2) or n >= 1:
                        act.wait_ge(s_al[y], n)
                    for c in range(4):
                        col = pair * 4 + c
                        last = nc.scalar.activation(gel[y][:, c, :], ps_t[y][:, c, :], ACT.Gelu,
                                                    scale=(g1, g2)[y][:, col:col + 1],
                                                    bias=(be1, be2)[y][:, col:col + 1])
                    last.then_inc(s_gl[y], 1)
                    act.wait_ge(s_gl[y], n + 1)
                    if before(t, 2) or n >= 1:
                        act.wait_ge(s_l[y + 1], n)
                    nc.scalar.activation(a_hi[y][:, :, :], gel[y][:, :, :], ACT.Copy).then_inc(s_ah[y], 1)

                def high(t, v):
                    act.wait_ge(s_ttr, t + 1)
                    nc.scalar.activation(t_hi[:, v, :, :], ps_p[:, :, :], ACT.Copy).then_inc(s_thi, 1)

                high(0, 0)

                def step(t, v, j):
                    more = not (isinstance(t, int) and t >= TILES - 1)
                    here = not (isinstance(t, int) and t == TILES)
                    for p in range(PAIRS):
                        if p == 3 and more:
                            high(t + 1, 1 - v)
                        gelu(t, p, 0, 1)
                        gelu(t, p, 1, 3)
                        if p == 0 and here:
                            act.wait_ge(s_gpre, t + 1)
                            nc.scalar.activation(gbuf[:, 0:G], gpre[:, :], ACT.Gelu).then_inc(s_gel, 1)
                        if p == 1 and here:
                            act.wait_ge(s_gtr, t + 1)
                            nc.scalar.activation(gt[:, :], ps_p[:, 0, :], ACT.Copy).then_inc(s_gt, 1)
                units(act, step)

            @block.tensor
            def _(pe):
                pe.wait_ge(s_c0, 2)

                def three(out, pairs, start, stop):
                    passes = [(a, w) for ah, al, wh, wl in pairs for a, w in ((ah, wh), (ah, wl), (al, wh))]
                    for k, (a, w) in enumerate(passes):
                        last = nc.tensor.matmul(out, a, w, start=start and k == 0,
                                                stop=stop and k == len(passes) - 1)
                    return last

                def bias(out, row, cols):
                    nc.tensor.matmul(out, sel[:, row:row + 1].to_broadcast([32, P]), bias_hl[:, cols],
                                     start=True, stop=False)

                def transpose(t, v):
                    pe.wait_ge(s_tn, t + 1)
                    if before(t, 1):
                        pe.wait_ge(s_lm, t)
                    for b in range(KD):
                        last = nc.tensor.transpose(ps_p[:, b, :], ht[:, b * P:(b + 1) * P], ident[:, :])
                    last.then_inc(s_ttr, 1)

                def layer1(t, p, v):
                    if not lives(t, p, 0):
                        return
                    n = t * PAIRS + p
                    if p == 0:
                        pe.wait_ge(s_tlo, t + 1)
                    if before(t, 1) or n >= 2:
                        pe.wait_ge(s_z[0], n - 1)
                    o = ps_1[p % 2][:, :]
                    bias(o, p, slice(0, D))
                    three(o, [(t_hi[:, v, b, :], t_lo[:, v, b, :],
                               w_hi[:, (p * KD + b) * W:(p * KD + b + 1) * W],
                               w_lo[:, (p * KD + b) * W:(p * KD + b + 1) * W]) for b in range(KD)],
                          False, True).then_inc(s_l[0], 1)

                def turn(t, p, y, lag):
                    if not lives(t, p, lag):
                        return
                    n = t * PAIRS + (p - lag)
                    pe.wait_ge(s_z[y], n + 1)
                    if before(t, 2) or n >= 1:
                        pe.wait_ge(s_gl[y], n)
                    for c in range(4):
                        last = nc.tensor.transpose(ps_t[y][:, c, :], z[y][:, c * P:(c + 1) * P], ident[:, :])
                    last.then_inc(s_tr[y], 1)

                def layer2(t, p):
                    if not lives(t, p, 2):
                        return
                    n = t * PAIRS + (p - 2)
                    pair = (p - 2) % PAIRS
                    pe.wait_ge(s_al[0], n + 1)
                    if before(t, 2) or n >= 1:
                        pe.wait_ge(s_z[1], n)
                    nc.tensor.matmul(ps_2[:, :], sel[:, 4 + pair:5 + pair].to_broadcast([32, P]),
                                     bias_hl[:, :], start=True, stop=False)
                    for e in range(2):
                        at = [W2_AT + ((2 * pair + e) * KH + b) * H for b in range(KH)]
                        last = three(ps_2[:, e * H:(e + 1) * H],
                                     [(a_hi[0][:, 2 * e + b, :], a_lo[0][:, 2 * e + b, :],
                                       w_hi[:, at[b]:at[b] + H], w_lo[:, at[b]:at[b] + H])
                                      for b in range(KH)], False, e == 1)
                    last.then_inc(s_l[1], 1)

                def layer3(t, p):
                    if not lives(t, p, 4):
                        return
                    n = t * PAIRS + (p - 4)
                    pe.wait_ge(s_al[1], n + 1)
                    if before(t, 2) or n >= 1:
                        pe.wait_ge(s_cmb, n * 2)
                    for e in range(2):
                        at = [W3_AT + ((2 * p + e) * KH + b) * D for b in range(KH)]
                        bias(ps_3[e][:, :], 8 + 2 * p + e, slice(0, D))
                        last = three(ps_3[e][:, :],
                                     [(a_hi[1][:, 2 * e + b, :], a_lo[1][:, 2 * e + b, :],
                                       w_hi[:, at[b]:at[b] + D], w_lo[:, at[b]:at[b] + D])
                                      for b in range(KH)], False, True)
                    last.then_inc(s_l[2], 1)

                transpose(0, 0)

                def step(t, v, j):
                    more = not (isinstance(t, int) and t >= TILES - 1)
                    here = not (isinstance(t, int) and t == TILES)
                    for p in range(PAIRS):
                        layer1(t, p, v)
                        if p == 3 and more:
                            transpose(t + 1, 1 - v)
                        layer2(t, p)
                        turn(t, p, 0, 1)
                        turn(t, p, 1, 3)
                        if p == 0 and here:
                            three(ps_p[:, 0, 0:G], [(t_hi[:, v, b, :], t_lo[:, v, b, :], wg1_hi[:, b, :],
                                                     wg1_lo[:, b, :]) for b in range(KD)], True, True
                                  ).then_inc(s_g1, 1)
                        if p == 1 and here:
                            pe.wait_ge(s_gel, t + 1)
                            nc.tensor.transpose(ps_p[:, 0, :], gbuf[:, :], ident[:, :]).then_inc(s_gtr, 1)
                        if p == 2 and here:
                            pe.wait_ge(s_gt, t + 1)
                            nc.tensor.matmul(ps_p[:, 0, 0:E], gt[:, :], wg2[:, :], start=True, stop=True
                                             ).then_inc(s_g2, 1)
                        layer3(t, p)
                units(pe, step)


def kernel(x, src, dst, L0_gnn_W_l, L0_gnn_b_l, L0_gnn_W_r, L0_gnn_gamma, L0_gnn_beta, L0_ffn_Wg1,
           L0_ffn_bg1, L0_ffn_Wg2, L0_ffn_bg2, L0_ffn_W1, L0_ffn_b1, L0_ffn_g1, L0_ffn_be1, L0_ffn_W2,
           L0_ffn_b2, L0_ffn_g2, L0_ffn_be2, L0_ffn_W3, L0_ffn_b3):
    import numpy as np
    import concourse.bacc as bacc
    from concourse.bass_utils import run_bass_kernel_spmd

    def arr(a):
        return np.ascontiguousarray(a)

    def edges(a, fill):
        return np.concatenate([np.asarray(a), np.full(ECOLS * P - EDGES, fill, np.int32)])

    def by_block(w):
        w = np.asarray(w)
        return w.reshape(-1, P, w.shape[-1]).transpose(1, 0, 2)

    def column(a):
        return arr(np.asarray(a).reshape(-1, P).T)

    def experts(w):
        w = np.asarray(w)
        return w.reshape(E, -1, P, w.shape[-1]).transpose(2, 0, 1, 3).reshape(P, -1)

    src_p, dst_p = edges(src, 0), edges(dst, NO_NODE)
    w1 = np.asarray(L0_ffn_W1).reshape(E // 2, 2, KD, P, H).transpose(3, 0, 2, 1, 4).reshape(P, -1)
    b1, b2 = (np.asarray(b).reshape(E // 2, 2 * H) for b in (L0_ffn_b1, L0_ffn_b2))
    b3 = np.asarray(L0_ffn_b3)
    sel = np.zeros((32, 16), np.float32)
    row_mask = np.zeros((32, 2), np.float32)
    for at, n, col in ((0, 4, 0), (8, 4, 4), (16, 8, 8)):
        for j in range(n):
            sel[at + j, col + j] = sel[at + n + j, col + j] = 1.0
            row_mask[at + j, 0] = row_mask[at + n + j, 1] = 1.0
    given = {
        "x": arr(x),
        "src_t": arr(src_p.reshape(ECOLS, P).T),
        "dst_t": arr(dst_p.reshape(ECOLS, P).T),
        "dst_r": arr(dst_p.reshape(ECHUNKS, P, P).transpose(1, 0, 2)),
        "wl_t": arr(by_block(np.asarray(L0_gnn_W_l).T)),
        "wr_t": arr(by_block(np.asarray(L0_gnn_W_r).T)),
        "bl_b": arr(np.broadcast_to(np.asarray(L0_gnn_b_l), (P, D))),
        "gamma_t": column(L0_gnn_gamma),
        "beta_t": column(L0_gnn_beta),
        "wall": arr(np.concatenate([w1, experts(L0_ffn_W2), experts(L0_ffn_W3)], axis=1)),
        "wg1": arr(by_block(L0_ffn_Wg1)),
        "bg1_b": arr(np.broadcast_to(np.asarray(L0_ffn_bg1), (P, G))),
        "bias_rows": arr(np.concatenate([b1, b1, b2, b2, b3, b3])),
        "row_mask": row_mask,
        "sel_in": sel,
        "wg2b": arr(np.concatenate([np.asarray(L0_ffn_Wg2), np.asarray(L0_ffn_bg2)[None, :]])),
        "g1_t": column(L0_ffn_g1), "be1_t": column(L0_ffn_be1),
        "g2_t": column(L0_ffn_g2), "be2_t": column(L0_ffn_be2),
    }
    nc = bacc.Bacc("TRN2", target_bir_lowering=False, num_devices=1)
    args = [nc.dram_tensor(n, a.shape, mybir.dt.from_np(a.dtype), kind="ExternalInput").ap()
            for n, a in given.items()]
    out = nc.dram_tensor("out", (N, D), mybir.dt.float32, kind="ExternalOutput").ap()
    build(nc, *args, out)
    r = run_bass_kernel_spmd(nc, [given], core_ids=[0])
    return r.results[0]["out"]
```

```python
from contextlib import ExitStack

import concourse.bass as bass
from concourse import mybir

P = 128
N, D, H, E = 6250, 512, 256, 8
EDGES = 106250
G = 2 * E
TILES = -(-N // P)
LAST = N - (TILES - 1) * P
NPAD = TILES * P
KD, KH = D // P, H // P
ETILES = -(-EDGES // P)
ECHUNKS = -(-(ETILES + 8) // P)
ECOLS = ECHUNKS * P
SET = 8
AHEAD = 3
LEAD = 3
NO_NODE = 8000
FAR = 9999.0
EPS = 1e-5
TABLE = 1024.0
WALL = E * KD * H + E * KH * H + E * KH * D
W2_AT, W3_AT = E * KD * H, E * KD * H + E * KH * H


def places(nc, stage):
    def sb(name, shape, dt):
        return stage.enter_context(nc.sbuf_tensor(name, shape, dt))

    def pb(name, shape, dt):
        return stage.enter_context(nc.psum_tensor(name, shape, dt))

    def sem(name):
        return stage.enter_context(nc.semaphore(name))

    return sb, pb, sem


def wait_apart(eng, met, k, signal, value):
    if not isinstance(value, int):
        value = eng.snap(value)
    eng.wait_ge(met, k)
    eng.wait_ge(signal, value)


def build(nc, x, src_t, dst_t, dst_r, wl_t, wr_t, bl_b, gamma_t, beta_t, wall, wg1, bg1_b,
          bias_rows, row_mask, sel_in, wg2b, g1_t, be1_t, g2_t, be2_t, out):
    f32, f32r, f16, i32 = mybir.dt.float32, mybir.dt.float32r, mybir.dt.float16, mybir.dt.int32
    u32, bf16 = mybir.dt.uint32, mybir.dt.bfloat16
    ALU, ACT, AX = mybir.AluOpType, mybir.ActivationFunctionType, mybir.AxisListType

    with ExitStack() as whole:
        sb, pb, sem = places(nc, whole)

        table = nc.dram_tensor("table", (NPAD, 2 * D), f16).ap()
        h_rows = nc.dram_tensor("h_rows", (NPAD, D), f32).ap()

        ident = sb("ident", [P, P], f32)
        ident16 = sb("ident16", [P, P], f16)
        ones32 = sb("ones32", [P, P], f32)
        s_const = sem("s_const")
        s_ident = sem("s_ident")
        bnmv = sb("bnmv", [P, KD, 2], f32)

        with ExitStack() as graph:
            sb, pb, sem = places(nc, graph)

            stats = sb("stats", [P, KD, TILES, 6], f32)
            one16 = sb("one16", [P, 2], f16)
            zero16 = sb("zero16", [P, D], f16)
            iota_j = sb("iota_j", [P, P], f32)
            negb = sb("negb", [P, TILES], f32)
            dstc = sb("dstc", [P, ECOLS], f32)
            first_t = sb("first_t", [1, TILES], i32)
            end_t = sb("end_t", [1, TILES], i32)
            w_hi = sb("w_hi", [P, 2, KD, D], f32r)
            w_lo = sb("w_lo", [P, 2, KD, D], f32r)
            bl = sb("bl", [P, D], f32)

            with ExitStack() as stage:
                sb, pb, sem = places(nc, stage)

                NX = 4
                GROUPS = TILES // NX
                assert GROUPS % 2 == 0 and TILES == GROUPS * NX + 1
                xin = sb("xin", [P, 2 * NX, D], f32)
                lst = sb("lst", [P, 2 * NX, 6], f32)
                mv = sb("mv", [P, 2 * NX, 2], f32)
                var_s = sb("var_s", [P, 2 * NX], f32)
                mhalf = sb("mhalf", [P, NX], f32)
                rstd = sb("rstd", [P, 2 * NX], f32)
                xs = sb("xs", [P, NX, D], f32)
                pair = sb("pair", [P, NX, 2 * D], f16)
                s_x = [sem(f"s_x{u}") for u in range(2 * NX)]
                s_store = [sem(f"s_store{u}") for u in range(NX)]
                s_lst, s_mv, s_var, s_r, s_xs, s_hi, s_lo = (
                    sem(f"s_t_{n}") for n in ("lst", "mv", "var", "r", "xs", "hi", "lo"))

                dsti = sb("dsti", [P, ECOLS], i32)
                dri = sb("dri", [P, ECHUNKS, P], i32)
                drf = sb("drf", [P, ECHUNKS, P], f32)
                dmin = sb("dmin", [P, ECHUNKS], f32)
                dmax = sb("dmax", [P, ECHUNKS], f32)
                etp1 = sb("etp1", [P, ECHUNKS], f32)
                etneg = sb("etneg", [P, ECHUNKS], f32)
                base = sb("base", [P, TILES], f32)
                topn = sb("topn", [P, TILES], f32)
                rel0 = sb("rel0", [P, TILES], f32)
                rel = sb("rel", [P, TILES], f32)
                ends = sb("ends", [P, 2, TILES], f32)
                endr = sb("endr", [P, 2, TILES], f32)
                first_f = sb("first_f", [1, TILES], f32)
                s_edge = sem("s_edge")
                s_iota = sem("s_iota")
                s_bd = sem("s_bd")
                s_all = sem("s_all")
                s_bounds = sem("s_bounds")

                wst = sb("wst", [P, 2, KD, D], f32)
                s_wst = sem("s_wst")
                s_whi = sem("s_whi")
                s_wlo = sem("s_wlo")

                def over_groups(eng, body):
                    body(0, 0, 0)
                    body(1, 1, 0)
                    with eng.Fori(1, GROUPS // 2 - 1) as i:
                        body(i * 2, 0, i)
                        body(i * 2 + 1, 1, i)
                    body(GROUPS - 2, 0, GROUPS // 2 - 1)
                    body(GROUPS - 1, 1, GROUPS // 2 - 1)
                    body(GROUPS, 0, GROUPS // 2)

                def fixed(g):
                    return isinstance(g, int)

                def size(g):
                    return 1 if fixed(g) and g == GROUPS else NX

                block = stage.enter_context(nc.Block())

                @block.sync
                def _(sp):
                    for t in range(2 * NX):
                        sp.dma_start(xin[:, t, :], x[t * P:(t + 1) * P, :]).then_inc(s_x[t], 16)
                    sp.dma_start(dsti[:, :], dst_t).then_inc(s_edge, 16)
                    sp.dma_start(dri[:, :, :], dst_r).then_inc(s_edge, 16)
                    sp.dma_start(wst[:, 0, :, :], wl_t).then_inc(s_wst, 16)
                    sp.dma_start(wst[:, 1, :, :], wr_t).then_inc(s_wst, 16)
                    sp.dma_start(bl[:, :], bl_b).then_inc(s_wst, 16)

                    def step(g, w, i):
                        for u in range(size(g)):
                            t, s = g * NX + u, w * NX + u
                            ahead = t + 2 * NX
                            if not fixed(g) or ahead < TILES:
                                n = LAST if fixed(g) and ahead == TILES - 1 else P
                                sp.wait_ge(s_xs, t + 1)
                                sp.dma_start(xin[0:n, s, :], x[bass.ds(ahead * P, n), :]).then_inc(s_x[s], 16)
                            sp.wait_ge(s_hi, t + 1)
                            sp.wait_ge(s_lo, t + 1)
                            sp.dma_start(table[bass.ds(t * P, P), :], pair[:, u, :]).then_inc(s_store[u], 16)
                    over_groups(sp, step)
                    for u in range(NX):
                        sp.wait_ge(s_store[u], 16 * (GROUPS + (u == 0)))

                @block.gpsimd
                def _(pool):
                    nc.gpsimd.memset(mhalf[:, :], -0.5).then_inc(s_ident, 1)
                    nc.gpsimd.memset(ident[:, :], 0.0).then_inc(s_ident, 1)
                    nc.gpsimd.memset(ones32[:, :], 1.0).then_inc(s_ident, 1)
                    pool.wait_ge(s_ident, 3)
                    nc.gpsimd.affine_select(out=ident[:, :], in_=ident[:, :], compare_op=ALU.not_equal,
                                            fill=1.0, base=0, pattern=[[-1, P]],
                                            channel_multiplier=1).then_inc(s_ident, 1)
                    pool.wait_ge(s_ident, 4)
                    nc.gpsimd.tensor_copy(ident16[:, :], ident[:, :])
                    for tile, first, step, n, per_row in (
                            (iota_j, 0, 1, P, 0), (base, 0, P, TILES, 0), (topn, P - 1, P, TILES, 0),
                            (negb, 0, -P, TILES, 0), (etp1, 1, P, ECHUNKS, 1),
                            (etneg, int(FAR), -P, ECHUNKS, -1)):
                        nc.gpsimd.iota(tile[:, :], pattern=[[step, n]], base=first,
                                       channel_multiplier=per_row,
                                       allow_small_or_imprecise_dtypes=True).then_inc(s_iota, 1)

                    def power(g, w):
                        n = size(g)
                        pool.wait_ge(s_var, g + 1)
                        nc.gpsimd.tensor_tensor(rstd[:, w * NX:w * NX + n], var_s[:, w * NX:w * NX + n],
                                                mhalf[:, 0:n], ALU.pow).then_inc(s_r, 1)

                    power(0, 0)

                    def step(g, w, i):
                        for u in range(size(g)):
                            if u == 2:
                                power(g + 1, 1 - w)
                            pool.wait_ge(s_hi, g * NX + u + 1)
                            nc.gpsimd.tensor_tensor(pair[:, u, D:], xs[:, u, :], pair[:, u, 0:D],
                                                    ALU.subtract).then_inc(s_lo, 1)
                    over_groups(pool, step)

                    pool.wait_ge(s_bd, 4 + 4 * ECHUNKS)
                    nc.gpsimd.partition_all_reduce(endr[:, :, :], ends[:, :, :], P,
                                                   bass.bass_isa.ReduceOp.max).then_inc(s_all, 1)

                @block.vector
                def _(dve):
                    nc.vector.memset(zero16[:, :], 0.0)
                    nc.vector.memset(one16[:, :], 1.0).then_inc(s_const, 1)

                    def sums(g, w, i):
                        for u in range(size(g)):
                            dve.wait_ge(s_x[w * NX + u], (i + 1) * 16)
                            last = nc.vector.bn_stats(lst[:, w * NX + u, :], xin[:, w * NX + u, :])
                        last.then_inc(s_lst, 1)

                    def variance(g, w):
                        n = size(g)
                        for u in range(n):
                            last = nc.vector.bn_aggr(mv[:, w * NX + u, :], lst[:, w * NX + u, :])
                        last.then_inc(s_mv, 1)
                        dve.wait_ge(s_mv, g + 1)
                        nc.vector.tensor_scalar(var_s[:, w * NX:w * NX + n], mv[:, w * NX:w * NX + n, 1],
                                                EPS, TABLE ** -2, ALU.add, ALU.mult).then_inc(s_var, 1)

                    sums(0, 0, 0)
                    dve.wait_ge(s_lst, 1)
                    variance(0, 0)

                    def step(g, w, i):
                        more = not fixed(g) or g < GROUPS
                        if more:
                            sums(g + 1, 1 - w, i + w)
                        dve.wait_ge(s_r, g + 1)
                        if more:
                            dve.wait_ge(s_lst, g + 2)
                        for u in range(size(g)):
                            if not fixed(g) or g > 0:
                                dve.wait_ge(s_lo, g * NX + u - NX + 1)
                            nc.vector.tensor_scalar(xs[:, u, :], xin[:, w * NX + u, :],
                                                    mv[:, w * NX + u, 0:1], rstd[:, w * NX + u:w * NX + u + 1],
                                                    ALU.subtract, ALU.mult).then_inc(s_xs, 1)
                        if more:
                            variance(g + 1, 1 - w)
                    over_groups(dve, step)

                    dve.wait_ge(s_edge, 32)
                    dve.wait_ge(s_iota, 6)
                    nc.vector.tensor_copy(dstc[:, :], dsti[:, :])
                    nc.vector.memset(ends[:, :, :], 0.0).then_inc(s_bd, 1)
                    nc.vector.tensor_copy(drf[:, :, :], dri[:, :, :]).then_inc(s_bd, 1)
                    dve.wait_ge(s_bd, 2)
                    nc.vector.tensor_reduce(dmin[:, :], drf[:, :, :], AX.X, ALU.min).then_inc(s_bd, 1)
                    nc.vector.tensor_reduce(dmax[:, :], drf[:, :, :], AX.X, ALU.max).then_inc(s_bd, 1)
                    dve.wait_ge(s_bd, 4)
                    for c in range(ECHUNKS):
                        n = 4 + 4 * c
                        nc.vector.tensor_scalar(rel0[:, :], base[:, :], dmax[:, c:c + 1], None,
                                                ALU.is_le).then_inc(s_bd, 1)
                        dve.wait_ge(s_bd, n + 1)
                        nc.vector.scalar_tensor_tensor(out=rel[:, :], in0=topn[:, :],
                                                       scalar=dmin[:, c:c + 1], in1=rel0[:, :],
                                                       op0=ALU.is_ge, op1=ALU.mult).then_inc(s_bd, 1)
                        dve.wait_ge(s_bd, n + 2)
                        for j, score in enumerate((etp1, etneg)):
                            nc.vector.scalar_tensor_tensor(out=ends[:, j, :], in0=rel[:, :],
                                                           scalar=score[:, c:c + 1], in1=ends[:, j, :],
                                                           op0=ALU.mult, op1=ALU.max).then_inc(s_bd, 1)
                        dve.wait_ge(s_bd, n + 4)
                    dve.wait_ge(s_whi, 1)
                    nc.vector.tensor_tensor(w_lo[:, :, :, :], wst[:, :, :, :],
                                            w_hi[:, :, :, :].bitcast(f32), ALU.subtract)
                    dve.wait_ge(s_all, 1)
                    nc.vector.tensor_scalar(first_f[:, :], endr[0:1, 1, :], -1.0, FAR, ALU.mult, ALU.add
                                            ).then_inc(s_bounds, 1)
                    dve.wait_ge(s_bounds, 1)
                    nc.vector.tensor_scalar(first_f[:, :], first_f[:, :], float(ETILES - 1), None, ALU.min
                                            ).then_inc(s_bounds, 1)
                    dve.wait_ge(s_bounds, 2)
                    nc.vector.tensor_copy(first_t[:, :], first_f[:, :])
                    nc.vector.scalar_tensor_tensor(out=end_t[:, :], in0=first_f[:, :], scalar=1.0,
                                                   in1=endr[0:1, 0, :], op0=ALU.add, op1=ALU.max)

                @block.scalar
                def _(act):
                    def step(g, w, i):
                        for u in range(size(g)):
                            act.wait_ge(s_xs, g * NX + u + 1)
                            if not fixed(g) or g > 0:
                                act.wait_ge(s_store[u], g * 16)
                            nc.scalar.activation(pair[:, u, 0:D], xs[:, u, :], ACT.Copy).then_inc(s_hi, 1)
                    over_groups(act, step)
                    act.wait_ge(s_wst, 48)
                    nc.scalar.activation(w_hi[:, :, :, :], wst[:, :, :, :], ACT.Copy).then_inc(s_whi, 1)

            with ExitStack() as stage:
                sb, pb, sem = places(nc, stage)

                idx = sb("idx", [P, 2 * AHEAD, SET], i32)
                rows = sb("rows", [P, 2 * AHEAD, SET, 2 * D], f16)
                hot = sb("hot", [P, 2 * AHEAD, SET, P], f16)
                cden = sb("cden", [P, 2], f32)
                rcnt = sb("rcnt", [P, 2], f32)
                mean = sb("mean", [P, 2, D], f32)
                xt = sb("xt", [P, 2, 2 * D], f16)
                m_hi = sb("m_hi", [P, KD, P], f32r)
                m_lo = sb("m_lo", [P, KD, P], f32r)
                x_hl = sb("x_hl", [P, 2 * KD, P], f32r)
                hs = sb("hs", [P, 2, D], f32)
                agg = [pb(f"agg{v}", [P, D], f32) for v in range(2)]
                cnt = [pb(f"cnt{v}", [P, D], f32) for v in range(2)]
                ps_m = pb("ps_m", [P, KD, P], f32)
                ps_x = pb("ps_x", [P, 2 * KD, P], f16)
                ps_h = pb("ps_h", [P, D], f32)
                ps_ht = pb("ps_ht", [P, KD, P], f32)
                s_idx = [sem(f"s_idx{q}") for q in range(2 * AHEAD)]
                s_hot = sem("s_hot")
                s_got = [sem(f"s_got{q}") for q in range(2 * AHEAD)]
                s_used = sem("s_used")
                (s_agg, s_cden, s_rcnt, s_mean, s_trm, s_trx, s_mhi, s_mlo, s_xhl, s_h, s_hs, s_tht,
                 s_bs) = (sem(f"s_a_{n}") for n in ("agg", "cden", "rcnt", "mean", "trm", "trx", "mhi",
                                                    "mlo", "xhl", "h", "hs", "tht", "bs"))
                s_xt = [sem(f"s_xt{v}") for v in range(2)]
                s_hst = [sem(f"s_hst{v}") for v in range(2)]

                def over_tiles(eng, body):
                    for t in range(3):
                        body(t, t // 2, t % 2)
                    with eng.Fori(1, TILES // 2 - 1) as i:
                        body(i * 2 + 1, i, 1)
                        body(i * 2 + 2, i + 1, 0)
                    for t in range(TILES - 2, TILES + 2):
                        body(t, t // 2, t % 2)

                def there(t):
                    return not isinstance(t, int) or 0 <= t < TILES

                class Sets:

                    def __init__(self, eng, name, arrivals=False):
                        self.eng = eng
                        self.groups = eng.alloc_register(name + "_groups")
                        self.last = [eng.alloc_register(f"{name}_last{q}") for q in range(2 * AHEAD)]
                        self.arrived = [eng.alloc_register(f"{name}_arrived{q}")
                                        for q in range(2 * AHEAD * arrivals)]
                        for r in (self.groups, *self.last):
                            eng.reg_mov(r, 1)
                        for r in self.arrived:
                            eng.reg_mov(r, 0)

                    def over_groups(self, t, v, group):
                        eng = self.eng
                        first = eng.value_load(first_t[0:1, bass.ds(t, 1)], min_val=0, max_val=ETILES - 1)
                        end = eng.value_load(end_t[0:1, bass.ds(t, 1)], min_val=1, max_val=ETILES)

                        def some(e, k):
                            q = AHEAD * v + k
                            free = eng.snap(self.last[q], min_val=1, max_val=TILES * ETILES)
                            g = eng.snap(self.groups, min_val=1, max_val=TILES * ETILES)
                            group(e, end, q, free, g - 1)
                            eng.reg_add(self.groups, self.groups, 1)
                            eng.reg_mov(self.last[q], self.groups)
                            if k + 1 < AHEAD:
                                with eng.If(e + SET < end):
                                    some(e + SET, k + 1)

                        with eng.Fori(first, end, AHEAD * SET) as e:
                            some(e, 0)

                block = stage.enter_context(nc.Block())

                @block.sync
                def _(sp):
                    sets = Sets(sp, "sp")

                    def sources(e, end, q, free, g):
                        sp.wait_ge(s_used, free)
                        sp.dma_start(idx[:, q, :], src_t[:, bass.ds(e + LEAD, SET)]).then_inc(s_idx[q], 16)

                    def step(t, i, v):
                        if there(t):
                            sets.over_groups(t, v, sources)
                    over_tiles(sp, step)
                    sp.wait_ge(s_hst[0], 16 * (TILES // 2 + 1))
                    sp.wait_ge(s_hst[1], 16 * (TILES // 2))

                @block.gpsimd
                def _(pool):
                    sets = Sets(pool, "pool", True)

                    def gather(e, end, q, free, g):
                        def rows_of(k):
                            pool.indirect_dma_start(
                                rows[:, q, k, :], None, table,
                                bass.IndirectOffsetOnAxis(idx[:, q, k:k + 1], axis=0),
                                bounds_check=N - 1, oob_is_err=False).then_inc(s_got[q], 16)

                        pool.reg_add(sets.arrived[q], sets.arrived[q], 16)
                        arrived = pool.snap(sets.arrived[q], min_val=16, max_val=1 << 24)
                        left = pool.snap(end - e)
                        pool.wait_ge(s_const, 1)
                        pool.wait_ge(s_used, free)
                        pool.wait_ge(s_idx[q], arrived)
                        with pool.If(left >= SET):
                            for k in range(SET):
                                rows_of(k)
                        with pool.Else():
                            rows_of(0)
                            for k in range(1, SET):
                                with pool.If(left > k):
                                    rows_of(k)

                    def step(t, i, v):
                        if there(t):
                            sets.over_groups(t, v, gather)
                    over_tiles(pool, step)

                @block.vector
                def _(dve):
                    sets = Sets(dve, "dve")

                    def hots(t, v):
                        def one_hot(e, end, q, free, g):
                            dve.wait_ge(s_used, free)
                            for k in range(SET):
                                last = nc.vector.tensor_scalar(hot[:, q, k, :], iota_j[:, :],
                                                               dstc[:, bass.ds(e + k, 1)],
                                                               negb[:, bass.ds(t, 1)],
                                                               ALU.subtract, ALU.is_equal)
                            last.then_inc(s_hot, 1)
                        sets.over_groups(t, v, one_hot)

                    hots(0, 0)

                    def step(t, i, v):
                        w = 1 - v
                        if there(t):
                            dve.wait_ge(s_agg, t + 1)
                            nc.vector.tensor_scalar(cden[:, v:v + 1], cnt[v][:, 0:1], 1.0, TABLE,
                                                    ALU.max, ALU.mult).then_inc(s_cden, 1)
                            dve.wait_ge(s_cden, t + 1)
                            nc.vector.reciprocal(rcnt[:, v:v + 1], cden[:, v:v + 1]).then_inc(s_rcnt, 1)
                        if there(t + 1):
                            hots(t + 1, w)
                        if there(t - 1):
                            dve.wait_ge(s_h, t)
                            if not (isinstance(t, int) and t < 3):
                                dve.wait_ge(s_hst[w], 16 * (i if v == 1 else i - 1))
                                dve.wait_ge(s_tht, t - 2)
                            nc.vector.tensor_tensor(hs[:, w, :], ps_h[:, :], bl[:, :], ALU.add
                                                    ).then_inc(s_hs, 1)
                        if there(t):
                            dve.wait_ge(s_mhi, t + 1)
                            nc.vector.tensor_tensor(m_lo[:, :, :], ps_m[:, :, :],
                                                    m_hi[:, :, :].bitcast(f32), ALU.subtract
                                                    ).then_inc(s_mlo, 1)
                        if there(t - 2):
                            dve.wait_ge(s_tht, t - 1)
                            n = LAST if isinstance(t, int) and t == TILES + 1 else P
                            for b in range(KD):
                                nc.vector.bn_stats(stats[:, b, bass.ds(t - 2, 1), :], ps_ht[:, b, 0:n]
                                                   ).then_inc(s_bs, 1)
                    over_tiles(dve, step)
                    dve.wait_ge(s_bs, KD * TILES)
                    for b in range(KD):
                        nc.vector.bn_aggr(bnmv[:, b, :], stats[:, b, :, :])

                @block.scalar
                def _(act):
                    def fetch(t, i, v):
                        if not (isinstance(t, int) and t < 2):
                            act.wait_ge(s_trx, t - 1)
                        act.dma_start(xt[:, v, :], table[bass.ds(t * P, P), :]).then_inc(s_xt[v], 16)

                    def step(t, i, v):
                        if there(t):
                            fetch(t, i, v)
                            act.wait_ge(s_rcnt, t + 1)
                            nc.scalar.activation(mean[:, v, :], agg[v][:, :], ACT.Copy,
                                                 scale=rcnt[:, v:v + 1]).then_inc(s_mean, 1)
                            act.wait_ge(s_trx, t + 1)
                            nc.scalar.activation(x_hl[:, :, :], ps_x[:, :, :], ACT.Copy, scale=1.0 / TABLE
                                                 ).then_inc(s_xhl, 1)
                            act.wait_ge(s_trm, t + 1)
                            nc.scalar.activation(m_hi[:, :, :], ps_m[:, :, :], ACT.Copy).then_inc(s_mhi, 1)
                        if there(t - 1):
                            act.wait_ge(s_hs, t)
                            act.dma_start(h_rows[bass.ds((t - 1) * P, P), :], hs[:, 1 - v, :]
                                          ).then_inc(s_hst[1 - v], 16)
                    over_tiles(act, step)

                @block.tensor
                def _(pe):
                    pe.sem_inc(s_used, 1)
                    sets = Sets(pe, "pe", True)

                    def gather(t, v):
                        def add(q, k):
                            for cols in (slice(0, D), slice(D, 2 * D)):
                                nc.tensor.matmul(agg[v][:, :], hot[:, q, k, :], rows[:, q, k, cols],
                                                 start=False, stop=False)
                            nc.tensor.matmul(cnt[v][:, 0:2], hot[:, q, k, :], one16[:, :],
                                             start=False, stop=False)

                        def group(e, end, q, free, g):
                            hots = pe.snap(g + 1)
                            left = pe.snap(end - e)
                            with pe.If(left >= SET):
                                pe.reg_add(sets.arrived[q], sets.arrived[q], 16 * SET)
                            with pe.Else():
                                pe.reg_add(sets.arrived[q], sets.arrived[q], 16)
                                for k in range(1, SET):
                                    with pe.If(left > k):
                                        pe.reg_add(sets.arrived[q], sets.arrived[q], 16)
                            arrived = pe.snap(sets.arrived[q], min_val=16, max_val=1 << 24)
                            pe.wait_ge(s_hot, hots)
                            pe.wait_ge(s_got[q], arrived)
                            add(q, 0)
                            with pe.If(left >= SET):
                                for k in range(1, SET):
                                    add(q, k)
                            with pe.Else():
                                for k in range(1, SET):
                                    with pe.If(left > k):
                                        add(q, k)
                            nc.tensor.matmul(cnt[v][:, 0:2], zero16[:, 0:P], zero16[:, 0:2],
                                             start=False, stop=False).then_inc(s_used, 1)

                        nc.tensor.matmul(agg[v][:, :], zero16[:, 0:P], zero16[:, :], start=True, stop=False)
                        nc.tensor.matmul(cnt[v][:, 0:2], zero16[:, 0:P], zero16[:, 0:2],
                                         start=True, stop=False)
                        sets.over_groups(t, v, group)
                        nc.tensor.matmul(agg[v][:, :], zero16[:, 0:P], zero16[:, :], start=False, stop=True)
                        nc.tensor.matmul(cnt[v][:, 0:2], zero16[:, 0:P], zero16[:, 0:2],
                                         start=False, stop=True).then_inc(s_agg, 1)

                    def linear(t):
                        pe.wait_ge(s_xhl, t + 1)
                        if there(t - 1):
                            pe.wait_ge(s_hs, t)
                        for b in range(KD):
                            for a, w in ((b, w_hi), (b, w_lo), (KD + b, w_hi)):
                                nc.tensor.matmul(ps_h[:, :], x_hl[:, a, :], w[:, 1, b, :],
                                                 start=(b == 0 and w is w_hi and a == b), stop=False)
                        pe.wait_ge(s_mlo, t + 1)
                        for b in range(KD):
                            for a, w in ((m_hi, w_hi), (m_hi, w_lo), (m_lo, w_hi)):
                                last = nc.tensor.matmul(ps_h[:, :], a[:, b, :], w[:, 0, b, :],
                                                        start=False, stop=(b == KD - 1 and a is m_lo))
                        last.then_inc(s_h, 1)

                    def turn(t, i, v):
                        pe.wait_ge(s_xt[v], 16 * (i + 1))
                        for b in range(2 * KD):
                            last = nc.tensor.transpose(ps_x[:, b, :], xt[:, v, b * P:(b + 1) * P],
                                                       ident16[:, :])
                        last.then_inc(s_trx, 1)
                        pe.wait_ge(s_mean, t + 1)
                        for b in range(KD):
                            last = nc.tensor.transpose(ps_m[:, b, :], mean[:, v, b * P:(b + 1) * P],
                                                       ident[:, :])
                        last.then_inc(s_trm, 1)

                    def turn_h(t, v):
                        pe.wait_ge(s_hs, t + 1)
                        if there(t - 1):
                            pe.wait_ge(s_bs, t * KD)
                        for b in range(KD):
                            last = nc.tensor.transpose(ps_ht[:, b, :], hs[:, v, b * P:(b + 1) * P],
                                                       ident[:, :])
                        last.then_inc(s_tht, 1)

                    def step(t, i, v):
                        if there(t):
                            gather(t, v)
                        if there(t - 1):
                            linear(t - 1)
                        if there(t):
                            turn(t, i, v)
                        if there(t - 2):
                            turn_h(t - 2, v)
                    over_tiles(pe, step)

        sb, pb, sem = places(nc, whole)
        w_hi = sb("we_hi", [P, WALL], f32r)
        w_lo = sb("we_lo", [P, WALL], f32r)
        scale_r = sb("scale_r", [P, D], f32)
        shift_r = sb("shift_r", [P, D], f32)
        bias_hl = sb("bias_hl", [32, D], f32r)
        sel = sb("sel", [32, 16], f32r)
        wg1_hi = sb("wg1_hi", [P, KD, G], f32r)
        wg1_lo = sb("wg1_lo", [P, KD, G], f32r)
        bg1 = sb("bg1", [P, G], f32)
        wg2 = sb("wg2", [P, E], f32)
        g1, be1, g2, be2 = (sb(n, [P, E * KH], f32) for n in ("g1", "be1", "g2", "be2"))

        with ExitStack() as stage:
            sb, pb, sem = places(nc, stage)

            CH = 2048
            wst = sb("wst2", [P, 2, CH], f32)
            gb = sb("gb", [P, 2, KD], f32)
            small = sb("small", [P, 8], f32)
            mh = sb("mh2", [P, KD], f32)
            bsc = sb("bsc", [P, 2, KD], f32)
            diag = sb("diag", [P, 2, KD, P], f32)
            bstage = sb("bstage", [32, D], f32)
            bh = sb("bh", [32, D], f32r)
            bd = sb("bd", [32, D], f32)
            bh2 = sb("bh2", [32, D], f32)
            rmask = sb("rmask", [32, 2], f32)
            self32 = sb("self32", [32, 16], f32)
            wgst = sb("wgst", [P, KD, G], f32)
            ps_row = [pb(f"ps_row{j}", [P, D], f32) for j in range(2)]
            s_ws = [sem(f"s_ws{j}") for j in range(2)]
            s_wh, s_wl, s_cin, s_zero = sem("s_wh"), sem("s_wl"), sem("s_cin"), sem("s_zero")
            s_bn, s_bp, s_diag, s_row, s_k = sem("s_bn"), sem("s_bp"), sem("s_diag"), sem("s_row"), sem("s_k")
            s_kh = sem("s_kh")
            NCH = WALL // CH

            block = stage.enter_context(nc.Block())

            @block.sync
            def _(sp):
                sp.dma_start(gb[:, 0, :], gamma_t).then_inc(s_cin, 16)
                sp.dma_start(gb[:, 1, :], beta_t).then_inc(s_cin, 16)
                sp.dma_start(bstage[:, :], bias_rows).then_inc(s_cin, 16)
                sp.dma_start(rmask[:, :], row_mask).then_inc(s_cin, 16)
                sp.dma_start(self32[:, :], sel_in).then_inc(s_cin, 16)
                sp.dma_start(wgst[:, :, :], wg1).then_inc(s_cin, 16)
                sp.dma_start(bg1[:, :], bg1_b).then_inc(s_cin, 16)
                for tile, a in ((g1, g1_t), (be1, be1_t), (g2, g2_t), (be2, be2_t)):
                    sp.dma_start(tile[:, :], a).then_inc(s_cin, 16)
                sp.wait_ge(s_zero, 1)
                sp.dma_start(wg2[0:G + 1, :], wg2b).then_inc(s_cin, 16)
                for c in range(NCH):
                    if c >= 2:
                        sp.wait_ge(s_wl, c - 1)
                    sp.dma_start(wst[:, c % 2, :], wall[:, c * CH:(c + 1) * CH]).then_inc(s_ws[c % 2], 16)

            @block.scalar
            def _(act):
                for c in range(NCH):
                    act.wait_ge(s_ws[c % 2], 16 * (c // 2 + 1))
                    nc.scalar.activation(w_hi[:, c * CH:(c + 1) * CH], wst[:, c % 2, :], ACT.Copy
                                         ).then_inc(s_wh, 1)

            @block.gpsimd
            def _(pool):
                nc.gpsimd.memset(mh[:, :], -0.5).then_inc(s_bp, 1)
                nc.gpsimd.memset(wg2[:, :], 0.0).then_inc(s_zero, 1)
                pool.wait_ge(s_bn, KD + 1)
                pool.wait_ge(s_bp, 1)
                nc.gpsimd.tensor_tensor(small[:, 0:KD], small[:, KD:2 * KD], mh[:, :], ALU.pow
                                        ).then_inc(s_bp, 1)

            @block.vector
            def _(dve):
                nc.vector.tensor_scalar(small[:, KD:2 * KD], bnmv[:, :, 1], EPS, None, ALU.add
                                        ).then_inc(s_bn, KD + 1)
                dve.wait_ge(s_bp, 2)
                dve.wait_ge(s_cin, 16 * 12)
                nc.vector.tensor_tensor(bsc[:, 0, :], small[:, 0:KD], gb[:, 0, :], ALU.mult).then_inc(s_k, 1)
                dve.wait_ge(s_k, 1)
                nc.vector.tensor_tensor(mh[:, :], bsc[:, 0, :], bnmv[:, :, 0], ALU.mult).then_inc(s_k, 1)
                dve.wait_ge(s_k, 2)
                nc.vector.tensor_tensor(bsc[:, 1, :], gb[:, 1, :], mh[:, :], ALU.subtract).then_inc(s_k, 1)
                dve.wait_ge(s_k, 3)
                for j in range(2):
                    for b in range(KD):
                        nc.vector.tensor_scalar(diag[:, j, b, :], ident[:, :], bsc[:, j, b:b + 1], None,
                                                ALU.mult).then_inc(s_diag, 1)
                nc.vector.tensor_copy(bh[:, :], bstage[:, :])
                nc.vector.tensor_copy(sel[:, :], self32[:, :])
                nc.vector.tensor_copy(wg1_hi[:, :, :], wgst[:, :, :]).then_inc(s_k, 1)
                dve.wait_ge(s_k, 4)
                nc.vector.tensor_tensor(wg1_lo[:, :, :], wgst[:, :, :], wg1_hi[:, :, :].bitcast(f32),
                                        ALU.subtract)
                nc.vector.tensor_tensor(bd[:, :], bstage[:, :], bh[:, :].bitcast(f32), ALU.subtract)
                nc.vector.tensor_scalar(bh2[:, :], bh[:, :].bitcast(f32), rmask[:, 0:1], None, ALU.mult
                                        ).then_inc(s_k, 1)
                dve.wait_ge(s_k, 5)
                nc.vector.scalar_tensor_tensor(out=bias_hl[:, :], in0=bd[:, :], scalar=rmask[:, 1:2],
                                               in1=bh2[:, :], op0=ALU.mult, op1=ALU.add).then_inc(s_k, 1)
                for c in range(NCH):
                    dve.wait_ge(s_wh, c + 1)
                    nc.vector.tensor_tensor(w_lo[:, c * CH:(c + 1) * CH], wst[:, c % 2, :],
                                            w_hi[:, c * CH:(c + 1) * CH].bitcast(f32), ALU.subtract
                                            ).then_inc(s_wl, 1)
                dve.wait_ge(s_row, 2)
                nc.vector.tensor_copy(scale_r[:, :], ps_row[0][:, :])
                nc.vector.tensor_copy(shift_r[:, :], ps_row[1][:, :])

            @block.tensor
            def _(pe):
                pe.wait_ge(s_diag, 2 * KD)
                for j in range(2):
                    for b in range(KD):
                        last = nc.tensor.matmul(ps_row[j][:, b * P:(b + 1) * P], ones32[:, :],
                                                diag[:, j, b, :], start=True, stop=True)
                    last.then_inc(s_row, 1)

        with ExitStack() as stage:
            sb, pb, sem = places(nc, stage)

            PAIRS = E // 2
            W = 2 * H
            xa = sb("xa", [P, 2, D], f32)
            ht = sb("ht", [P, D], f32)
            pr = sb("pr", [P, 2 * D], f16)
            acc = sb("acc", [P, 2, D], f32)
            t_hi = sb("t_hi", [P, 2, KD, P], f32r)
            t_lo = sb("t_lo", [P, 2, KD, P], f32r)
            z = [sb(f"z{y}", [P, W], f32) for y in range(2)]
            gel = [sb(f"gel{y}", [P, 4, P], f32) for y in range(2)]
            a_hi = [sb(f"a_hi{y}", [P, 4, P], f32r) for y in range(2)]
            a_lo = [sb(f"a_lo{y}", [P, 4, P], f32r) for y in range(2)]
            st = [sb(f"st{y}", [P, 2, 6], f32) for y in range(3)]
            mv = [sb(f"mvy{y}", [P, 2, 2], f32) for y in range(3)]
            ve = [sb(f"ve{y}", [P, 2], f32) for y in range(3)]
            rs = [sb(f"rs{y}", [P, 2], f32) for y in range(3)]
            mhalf = sb("mhalf2", [P, 2], f32)
            euler = sb("euler", [P, E], f32)
            iota8 = sb("iota8", [P, E], f32)
            gpre = sb("gpre", [P, G], f32)
            gbuf = sb("gbuf", [P, P], f32)
            gt = sb("gt", [P, P], f32)
            top = sb("top", [P, 2, 8], f32)
            topi = sb("topi", [P, 8], u32)
            topf = sb("topf", [P, 8], f32)
            lm, ex, gates, ca, cb = (sb(n, [P, E], f32) for n in ("lm", "ex", "gates", "ca", "cb"))
            sums = sb("sums", [P, 4], f32)
            wtop = sb("wtop", [P, 2], f32)
            cw = sb("cw", [P, 2, E], f32)
            ps_1 = [pb(f"ps_1{v}", [P, W], f32) for v in range(2)]
            ps_2 = pb("ps_2", [P, W], f32)
            ps_t = [pb(f"ps_t{y}", [P, 4, P], f32) for y in range(2)]
            ps_3 = [pb(f"ps_3{e}", [P, D], f32) for e in range(2)]
            ps_p = pb("ps_p", [P, 4, P], f32)

            s_c0, s_load, s_loadx = sem("s_c0"), sem("s_load"), [sem("s_lx0"), sem("s_lx1")]
            s_bn1, s_bn2, s_u1, s_u2, s_x1, s_pst, s_pmv, s_pve, s_ppow, s_tn, s_ttr, s_thi, s_tlo = (
                sem(f"s_p_{n}") for n in ("bn1", "bn2", "u1", "u2", "x1", "st", "mv", "ve", "pow",
                                          "tn", "ttr", "thi", "tlo"))
            s_g1, s_gpre, s_gel, s_gtr, s_gt, s_g2, s_lm, s_ex, s_cw = (
                sem(f"s_g_{n}") for n in ("g1", "gpre", "gel", "gtr", "gt", "g2", "lm", "ex", "cw"))
            s_sm = [sem(f"s_sm{k}") for k in range(10)]
            s_l = [sem(f"s_l{y}") for y in range(3)]
            s_st, s_mv, s_ve, s_pow, s_z, s_tr, s_gl, s_ah, s_al = (
                [sem(f"s_{n}{y}") for y in range(2)]
                for n in ("st", "mv", "ve", "pow", "z", "tr", "gl", "ah", "al"))
            s_cmb = sem("s_cmb")
            s_out = [sem("s_out0"), sem("s_out1")]

            def units(eng, body):
                body(0, 0, 0)
                with eng.Fori(0, (TILES - 5) // 2) as j:
                    body(j * 2 + 1, 1, j)
                    body(j * 2 + 2, 0, j + 1)
                for t in range(TILES - 4, TILES + 1):
                    body(t, t % 2, t // 2)

            def lives(t, p, lag):
                return not isinstance(t, int) or 0 <= t * PAIRS + p - lag < TILES * PAIRS

            def before(t, first):
                return not (isinstance(t, int) and t < first)

            block = stage.enter_context(nc.Block())

            @block.sync
            def _(sp):
                def load(t, v, j):
                    n = LAST if isinstance(t, int) and t == TILES - 1 else P
                    if before(t, 1):
                        sp.wait_ge(s_ttr, t)
                        sp.wait_ge(s_u2, t)
                    sp.dma_start(ht[:, :], h_rows[bass.ds(t * P, P), :]).then_inc(s_load, 16)
                    sp.dma_start(pr[:, :], table[bass.ds(t * P, P), :]).then_inc(s_load, 16)
                    if before(t, 2):
                        sp.wait_ge(s_cmb, t * E - 15)
                    sp.dma_start(xa[0:n, v, :], x[bass.ds(t * P, n), :]).then_inc(s_loadx[v], 16)

                def store(t, v, j, n=P):
                    sp.wait_ge(s_cmb, t * E + E)
                    sp.dma_start(out[bass.ds(t * P, n), :], acc[0:n, v, :]).then_inc(s_out[v], 16)

                load(0, 0, 0)
                load(1, 1, 0)

                def step(t, v, j):
                    if not isinstance(t, int) or t <= TILES - 3:
                        load(t + 2, v, j + 1)
                    if before(t, 1):
                        store(t - 1, 1 - v, j, LAST if isinstance(t, int) and t == TILES else P)
                units(sp, step)
                sp.wait_ge(s_out[0], 16 * (TILES // 2 + 1))
                sp.wait_ge(s_out[1], 16 * (TILES // 2))

            @block.gpsimd
            def _(pool):
                nc.gpsimd.memset(mhalf[:, :], -0.5)
                nc.gpsimd.memset(euler[:, :], 2.718281828459045)
                nc.gpsimd.memset(gbuf[:, :], 0.0).then_inc(s_c0, 1)
                pool.wait_ge(s_c0, 1)
                nc.gpsimd.memset(gbuf[:, G:G + 1], 1.0)
                nc.gpsimd.iota(iota8[:, :], pattern=[[1, E]], base=0, channel_multiplier=0,
                               allow_small_or_imprecise_dtypes=True).then_inc(s_c0, 1)
                pool.wait_ge(s_c0, 2)

                def power(y, n, k=2):
                    nc.gpsimd.tensor_tensor(rs[y][:, 0:k], ve[y][:, 0:k], mhalf[:, 0:k], ALU.pow
                                            ).then_inc(s_pow[y] if y < 2 else s_ppow, 1)

                def split(t, p, y, lag):
                    if not lives(t, p, lag):
                        return
                    n = t * PAIRS + (p - lag)
                    pool.wait_ge(s_ah[y], n + 1)
                    nc.gpsimd.tensor_tensor(a_lo[y][:, :, :], gel[y][:, :, :],
                                            a_hi[y][:, :, :].bitcast(f32), ALU.subtract
                                            ).then_inc(s_al[y], 1)

                def normal(t, y, p, lag):
                    if lives(t, p, lag):
                        pool.wait_ge(s_ve[y], t * PAIRS + (p - lag) + 1)
                        power(y, 0)

                def prepare(t):
                    pool.wait_ge(s_pve, t + 1)
                    power(2, t, 1)

                prepare(0)

                def step(t, v, j):
                    for p in range(PAIRS):
                        if p == 2 and not (isinstance(t, int) and t >= TILES - 1):
                            prepare(t + 1)
                        normal(t, 0, p, 0)
                        split(t, p, 0, 1)
                        normal(t, 1, p, 2)
                        if p == 3 and not (isinstance(t, int) and t == TILES):
                            pool.wait_ge(s_lm, t + 1)
                            nc.gpsimd.tensor_tensor(ex[:, :], euler[:, :], lm[:, :], ALU.pow
                                                    ).then_inc(s_ex, 1)
                        split(t, p, 1, 3)
                units(pool, step)

            @block.vector
            def _(dve):
                dve.wait_ge(s_c0, 2)

                def moments(t, p, y, lag):
                    if not lives(t, p, lag):
                        return
                    n = t * PAIRS + (p - lag)
                    src = ps_1[p % 2] if y == 0 else ps_2
                    dve.wait_ge(s_l[y], n + 1)
                    for e in range(2):
                        last = nc.vector.bn_stats(st[y][:, e, :], src[:, e * H:(e + 1) * H])
                    last.then_inc(s_st[y], 1)
                    wait_apart(dve, s_c0, 2, s_st[y], n + 1)
                    for e in range(2):
                        last = nc.vector.bn_aggr(mv[y][:, e, :], st[y][:, e, :])
                    last.then_inc(s_mv[y], 1)
                    dve.wait_ge(s_mv[y], n + 1)
                    nc.vector.tensor_scalar(ve[y][:, :], mv[y][:, :, 1], EPS, None, ALU.add
                                            ).then_inc(s_ve[y], 1)

                def normal(t, p, y, lag):
                    if not lives(t, p, lag):
                        return
                    n = t * PAIRS + (p - lag)
                    src = ps_1[p % 2] if y == 0 else ps_2
                    dve.wait_ge(s_pow[y], n + 1)
                    if before(t, 2) or n >= 1:
                        dve.wait_ge(s_tr[y], n)
                    for e in range(2):
                        last = nc.vector.tensor_scalar(z[y][:, e * H:(e + 1) * H],
                                                       src[:, e * H:(e + 1) * H],
                                                       mv[y][:, e, 0:1], rs[y][:, e:e + 1],
                                                       ALU.subtract, ALU.mult)
                    last.then_inc(s_z[y], 1)

                def combine(t, v, j, p):
                    if not lives(t, p, 4):
                        return
                    n = t * E + (2 * p - E)
                    dve.wait_ge(s_l[2], t * PAIRS + (p - 4) + 1)
                    dve.wait_ge(s_cw, t)
                    if p == 0 and before(t, 3):
                        dve.wait_ge(s_out[1 - v], 16 * (j - 1 if v == 0 else j))
                    for e in range(2):
                        first = p == 0 and e == 0
                        if not first:
                            dve.wait_ge(s_cmb, n + e)
                        nc.vector.scalar_tensor_tensor(
                            out=acc[:, 1 - v, :], in0=ps_3[e][:, :], scalar=cw[:, 1 - v, 2 * p + e:2 * p + e + 1],
                            in1=(xa if first else acc)[:, 1 - v, :], op0=ALU.mult, op1=ALU.add
                        ).then_inc(s_cmb, 1)

                def batch_norm(t, v, j):
                    dve.wait_ge(s_load, t * 32 + 32)
                    dve.wait_ge(s_loadx[v], 16 * (j + 1))
                    nc.vector.tensor_tensor(ht[:, :], ht[:, :], scale_r[:, :], ALU.mult).then_inc(s_bn1, 1)
                    nc.vector.scalar_tensor_tensor(out=xa[:, v, :], in0=pr[:, 0:D], scalar=1.0 / TABLE,
                                                   in1=xa[:, v, :], op0=ALU.mult, op1=ALU.add
                                                   ).then_inc(s_u1, 1)
                    dve.wait_ge(s_bn1, t + 1)
                    nc.vector.tensor_tensor(ht[:, :], ht[:, :], shift_r[:, :], ALU.add).then_inc(s_bn2, 1)
                    dve.wait_ge(s_u1, t + 1)
                    nc.vector.scalar_tensor_tensor(out=xa[:, v, :], in0=pr[:, D:], scalar=1.0 / TABLE,
                                                   in1=xa[:, v, :], op0=ALU.mult, op1=ALU.add
                                                   ).then_inc(s_u2, 1)
                    dve.wait_ge(s_bn2, t + 1)
                    dve.wait_ge(s_u2, t + 1)
                    nc.vector.scalar_tensor_tensor(out=xa[:, v, :], in0=ht[:, :], scalar=0.0,
                                                   in1=xa[:, v, :], op0=ALU.max, op1=ALU.add
                                                   ).then_inc(s_x1, 1)
                    dve.wait_ge(s_x1, t + 1)
                    nc.vector.bn_stats(st[2][:, 0, :], xa[:, v, :]).then_inc(s_pst, 1)
                    wait_apart(dve, s_c0, 2, s_pst, t + 1)
                    nc.vector.bn_aggr(mv[2][:, 0, :], st[2][:, 0, :]).then_inc(s_pmv, 1)
                    dve.wait_ge(s_pmv, t + 1)
                    nc.vector.tensor_scalar(ve[2][:, 0:1], mv[2][:, 0, 1:2], EPS, None, ALU.add
                                            ).then_inc(s_pve, 1)

                def layer_norm(t, v):
                    dve.wait_ge(s_ppow, t + 1)
                    nc.vector.tensor_scalar(ht[:, :], xa[:, v, :], mv[2][:, 0, 0:1], rs[2][:, 0:1],
                                            ALU.subtract, ALU.mult).then_inc(s_tn, 1)

                def low(t, v):
                    dve.wait_ge(s_thi, t + 1)
                    nc.vector.tensor_tensor(t_lo[:, v, :, :], ps_p[:, :, :], t_hi[:, v, :, :].bitcast(f32),
                                            ALU.subtract).then_inc(s_tlo, 1)

                def gate_bias(t):
                    dve.wait_ge(s_g1, t + 1)
                    nc.vector.tensor_tensor(gpre[:, :], ps_p[:, 0, 0:G], bg1[:, :], ALU.add
                                            ).then_inc(s_gpre, 1)

                def logits(t):
                    wait_apart(dve, s_c0, 2, s_g2, t + 1)
                    nc.vector.max(top[:, 0, :], ps_p[:, 0, 0:E]).then_inc(s_sm[0], 1)
                    dve.wait_ge(s_sm[0], t + 1)
                    nc.vector.tensor_scalar(lm[:, :], ps_p[:, 0, 0:E], top[:, 0, 0:1], None, ALU.subtract
                                            ).then_inc(s_lm, 1)

                def weights(t, v):
                    def link(k, ins):
                        ins.then_inc(s_sm[k], 1)
                        wait_apart(dve, s_c0, 2, s_sm[k], t + 1)
                    dve.wait_ge(s_ex, t + 1)
                    link(1, nc.vector.reduce_sum(sums[:, 0:1], ex[:, :], axis=AX.X))
                    link(2, nc.vector.reciprocal(sums[:, 1:2], sums[:, 0:1]))
                    link(3, nc.vector.tensor_scalar(gates[:, :], ex[:, :], sums[:, 1:2], None, ALU.mult))
                    link(4, nc.vector.max(top[:, 1, :], gates[:, :]))
                    link(5, nc.vector.max_index(topi[:, :], top[:, 1, :], gates[:, :]))
                    nc.vector.tensor_copy(topf[:, 0:2], topi[:, 0:2])
                    link(6, nc.vector.tensor_tensor(sums[:, 2:3], top[:, 1, 0:1], top[:, 1, 1:2], ALU.add))
                    link(7, nc.vector.reciprocal(sums[:, 3:4], sums[:, 2:3]))
                    link(8, nc.vector.tensor_scalar(wtop[:, :], top[:, 1, 0:2], sums[:, 3:4], None, ALU.mult))
                    nc.vector.tensor_scalar(ca[:, :], iota8[:, :], topf[:, 0:1], wtop[:, 0:1],
                                            ALU.is_equal, ALU.mult)
                    link(9, nc.vector.tensor_scalar(cb[:, :], iota8[:, :], topf[:, 1:2], wtop[:, 1:2],
                                                    ALU.is_equal, ALU.mult))
                    nc.vector.tensor_tensor(cw[:, v, :], ca[:, :], cb[:, :], ALU.add).then_inc(s_cw, 1)

                batch_norm(0, 0, 0)
                layer_norm(0, 0)
                low(0, 0)

                def step(t, v, j):
                    more = not (isinstance(t, int) and t >= TILES - 1)
                    here = not (isinstance(t, int) and t == TILES)
                    for p in range(PAIRS):
                        moments(t, p, 0, 0)
                        if p == 1 and more:
                            batch_norm(t + 1, 1 - v, j if v == 0 else j + 1)
                        if p == 2 and more:
                            layer_norm(t + 1, 1 - v)
                        if p == 0 and here:
                            gate_bias(t)
                        normal(t, p, 0, 0)
                        moments(t, p, 1, 2)
                        combine(t, v, j, p)
                        if p == 3 and more:
                            low(t + 1, 1 - v)
                        if p == 2 and here:
                            logits(t)
                        if p == 3 and here:
                            weights(t, v)
                        normal(t, p, 1, 2)
                units(dve, step)

            @block.scalar
            def _(act):
                def gelu(t, p, y, lag):
                    if not lives(t, p, lag):
                        return
                    n = t * PAIRS + (p - lag)
                    pair = (p - lag) % PAIRS
                    act.wait_ge(s_tr[y], n + 1)
                    if before(t, 2) or n >= 1:
                        act.wait_ge(s_al[y], n)
                    for c in range(4):
                        col = pair * 4 + c
                        last = nc.scalar.activation(gel[y][:, c, :], ps_t[y][:, c, :], ACT.Gelu,
                                                    scale=(g1, g2)[y][:, col:col + 1],
                                                    bias=(be1, be2)[y][:, col:col + 1])
                    last.then_inc(s_gl[y], 1)
                    act.wait_ge(s_gl[y], n + 1)
                    if before(t, 2) or n >= 1:
                        act.wait_ge(s_l[y + 1], n)
                    nc.scalar.activation(a_hi[y][:, :, :], gel[y][:, :, :], ACT.Copy).then_inc(s_ah[y], 1)

                def high(t, v):
                    act.wait_ge(s_ttr, t + 1)
                    nc.scalar.activation(t_hi[:, v, :, :], ps_p[:, :, :], ACT.Copy).then_inc(s_thi, 1)

                high(0, 0)

                def step(t, v, j):
                    more = not (isinstance(t, int) and t >= TILES - 1)
                    here = not (isinstance(t, int) and t == TILES)
                    for p in range(PAIRS):
                        if p == 3 and more:
                            high(t + 1, 1 - v)
                        gelu(t, p, 0, 1)
                        gelu(t, p, 1, 3)
                        if p == 0 and here:
                            act.wait_ge(s_gpre, t + 1)
                            nc.scalar.activation(gbuf[:, 0:G], gpre[:, :], ACT.Gelu).then_inc(s_gel, 1)
                        if p == 1 and here:
                            act.wait_ge(s_gtr, t + 1)
                            nc.scalar.activation(gt[:, :], ps_p[:, 0, :], ACT.Copy).then_inc(s_gt, 1)
                units(act, step)

            @block.tensor
            def _(pe):
                pe.wait_ge(s_c0, 2)

                def three(out, pairs, start, stop):
                    passes = [(a, w) for ah, al, wh, wl in pairs for a, w in ((ah, wh), (ah, wl), (al, wh))]
                    for k, (a, w) in enumerate(passes):
                        last = nc.tensor.matmul(out, a, w, start=start and k == 0,
                                                stop=stop and k == len(passes) - 1)
                    return last

                def bias(out, row, cols):
                    nc.tensor.matmul(out, sel[:, row:row + 1].to_broadcast([32, P]), bias_hl[:, cols],
                                     start=True, stop=False)

                def transpose(t, v):
                    pe.wait_ge(s_tn, t + 1)
                    if before(t, 1):
                        pe.wait_ge(s_lm, t)
                    for b in range(KD):
                        last = nc.tensor.transpose(ps_p[:, b, :], ht[:, b * P:(b + 1) * P], ident[:, :])
                    last.then_inc(s_ttr, 1)

                def layer1(t, p, v):
                    if not lives(t, p, 0):
                        return
                    n = t * PAIRS + p
                    if p == 0:
                        pe.wait_ge(s_tlo, t + 1)
                    if before(t, 1) or n >= 2:
                        pe.wait_ge(s_z[0], n - 1)
                    o = ps_1[p % 2][:, :]
                    bias(o, p, slice(0, D))
                    three(o, [(t_hi[:, v, b, :], t_lo[:, v, b, :],
                               w_hi[:, (p * KD + b) * W:(p * KD + b + 1) * W],
                               w_lo[:, (p * KD + b) * W:(p * KD + b + 1) * W]) for b in range(KD)],
                          False, True).then_inc(s_l[0], 1)

                def turn(t, p, y, lag):
                    if not lives(t, p, lag):
                        return
                    n = t * PAIRS + (p - lag)
                    pe.wait_ge(s_z[y], n + 1)
                    if before(t, 2) or n >= 1:
                        pe.wait_ge(s_gl[y], n)
                    for c in range(4):
                        last = nc.tensor.transpose(ps_t[y][:, c, :], z[y][:, c * P:(c + 1) * P], ident[:, :])
                    last.then_inc(s_tr[y], 1)

                def layer2(t, p):
                    if not lives(t, p, 2):
                        return
                    n = t * PAIRS + (p - 2)
                    pair = (p - 2) % PAIRS
                    pe.wait_ge(s_al[0], n + 1)
                    if before(t, 2) or n >= 1:
                        pe.wait_ge(s_z[1], n)
                    nc.tensor.matmul(ps_2[:, :], sel[:, 4 + pair:5 + pair].to_broadcast([32, P]),
                                     bias_hl[:, :], start=True, stop=False)
                    for e in range(2):
                        at = [W2_AT + ((2 * pair + e) * KH + b) * H for b in range(KH)]
                        last = three(ps_2[:, e * H:(e + 1) * H],
                                     [(a_hi[0][:, 2 * e + b, :], a_lo[0][:, 2 * e + b, :],
                                       w_hi[:, at[b]:at[b] + H], w_lo[:, at[b]:at[b] + H])
                                      for b in range(KH)], False, e == 1)
                    last.then_inc(s_l[1], 1)

                def layer3(t, p):
                    if not lives(t, p, 4):
                        return
                    n = t * PAIRS + (p - 4)
                    pe.wait_ge(s_al[1], n + 1)
                    if before(t, 2) or n >= 1:
                        pe.wait_ge(s_cmb, n * 2)
                    for e in range(2):
                        at = [W3_AT + ((2 * p + e) * KH + b) * D for b in range(KH)]
                        bias(ps_3[e][:, :], 8 + 2 * p + e, slice(0, D))
                        last = three(ps_3[e][:, :],
                                     [(a_hi[1][:, 2 * e + b, :], a_lo[1][:, 2 * e + b, :],
                                       w_hi[:, at[b]:at[b] + D], w_lo[:, at[b]:at[b] + D])
                                      for b in range(KH)], False, True)
                    last.then_inc(s_l[2], 1)

                transpose(0, 0)

                def step(t, v, j):
                    more = not (isinstance(t, int) and t >= TILES - 1)
                    here = not (isinstance(t, int) and t == TILES)
                    for p in range(PAIRS):
                        layer1(t, p, v)
                        if p == 3 and more:
                            transpose(t + 1, 1 - v)
                        layer2(t, p)
                        turn(t, p, 0, 1)
                        turn(t, p, 1, 3)
                        if p == 0 and here:
                            three(ps_p[:, 0, 0:G], [(t_hi[:, v, b, :], t_lo[:, v, b, :], wg1_hi[:, b, :],
                                                     wg1_lo[:, b, :]) for b in range(KD)], True, True
                                  ).then_inc(s_g1, 1)
                        if p == 1 and here:
                            pe.wait_ge(s_gel, t + 1)
                            nc.tensor.transpose(ps_p[:, 0, :], gbuf[:, :], ident[:, :]).then_inc(s_gtr, 1)
                        if p == 2 and here:
                            pe.wait_ge(s_gt, t + 1)
                            nc.tensor.matmul(ps_p[:, 0, 0:E], gt[:, :], wg2[:, :], start=True, stop=True
                                             ).then_inc(s_g2, 1)
                        layer3(t, p)
                units(pe, step)


def kernel(x, src, dst, L0_gnn_W_l, L0_gnn_b_l, L0_gnn_W_r, L0_gnn_gamma, L0_gnn_beta, L0_ffn_Wg1,
           L0_ffn_bg1, L0_ffn_Wg2, L0_ffn_bg2, L0_ffn_W1, L0_ffn_b1, L0_ffn_g1, L0_ffn_be1, L0_ffn_W2,
           L0_ffn_b2, L0_ffn_g2, L0_ffn_be2, L0_ffn_W3, L0_ffn_b3):
    import numpy as np
    import concourse.bacc as bacc
    from concourse.bass_utils import run_bass_kernel_spmd

    def arr(a):
        return np.ascontiguousarray(a)

    def edges(a, fill):
        return np.concatenate([np.asarray(a), np.full(ECOLS * P - EDGES, fill, np.int32)])

    def by_block(w):
        w = np.asarray(w)
        return w.reshape(-1, P, w.shape[-1]).transpose(1, 0, 2)

    def column(a):
        return arr(np.asarray(a).reshape(-1, P).T)

    def experts(w):
        w = np.asarray(w)
        return w.reshape(E, -1, P, w.shape[-1]).transpose(2, 0, 1, 3).reshape(P, -1)

    src_p, dst_p = edges(src, 0), edges(dst, NO_NODE)
    w1 = np.asarray(L0_ffn_W1).reshape(E // 2, 2, KD, P, H).transpose(3, 0, 2, 1, 4).reshape(P, -1)
    b1, b2 = (np.asarray(b).reshape(E // 2, 2 * H) for b in (L0_ffn_b1, L0_ffn_b2))
    b3 = np.asarray(L0_ffn_b3)
    sel = np.zeros((32, 16), np.float32)
    row_mask = np.zeros((32, 2), np.float32)
    for at, n, col in ((0, 4, 0), (8, 4, 4), (16, 8, 8)):
        for j in range(n):
            sel[at + j, col + j] = sel[at + n + j, col + j] = 1.0
            row_mask[at + j, 0] = row_mask[at + n + j, 1] = 1.0
    given = {
        "x": arr(x),
        "src_t": arr(np.concatenate([np.zeros((P, LEAD), np.int32), src_p.reshape(ECOLS, P).T], axis=1)),
        "dst_t": arr(dst_p.reshape(ECOLS, P).T),
        "dst_r": arr(dst_p.reshape(ECHUNKS, P, P).transpose(1, 0, 2)),
        "wl_t": arr(by_block(np.asarray(L0_gnn_W_l).T)),
        "wr_t": arr(by_block(np.asarray(L0_gnn_W_r).T)),
        "bl_b": arr(np.broadcast_to(np.asarray(L0_gnn_b_l), (P, D))),
        "gamma_t": column(L0_gnn_gamma),
        "beta_t": column(L0_gnn_beta),
        "wall": arr(np.concatenate([w1, experts(L0_ffn_W2), experts(L0_ffn_W3)], axis=1)),
        "wg1": arr(by_block(L0_ffn_Wg1)),
        "bg1_b": arr(np.broadcast_to(np.asarray(L0_ffn_bg1), (P, G))),
        "bias_rows": arr(np.concatenate([b1, b1, b2, b2, b3, b3])),
        "row_mask": row_mask,
        "sel_in": sel,
        "wg2b": arr(np.concatenate([np.asarray(L0_ffn_Wg2), np.asarray(L0_ffn_bg2)[None, :]])),
        "g1_t": column(L0_ffn_g1), "be1_t": column(L0_ffn_be1),
        "g2_t": column(L0_ffn_g2), "be2_t": column(L0_ffn_be2),
    }
    nc = bacc.Bacc("TRN2", target_bir_lowering=False, num_devices=1)
    args = [nc.dram_tensor(n, a.shape, mybir.dt.from_np(a.dtype), kind="ExternalInput").ap()
            for n, a in given.items()]
    out = nc.dram_tensor("out", (N, D), mybir.dt.float32, kind="ExternalOutput").ap()
    build(nc, *args, out)
    r = run_bass_kernel_spmd(nc, [given], core_ids=[0])
    return r.results[0]["out"]
```

```python
from contextlib import ExitStack

import concourse.bass as bass
from concourse import mybir

P = 128
N, D, H, E = 6250, 512, 256, 8
EDGES = 106250
G = 2 * E
TILES = -(-N // P)
LAST = N - (TILES - 1) * P
NPAD = TILES * P
KD, KH = D // P, H // P
ETILES = -(-EDGES // P)
ECHUNKS = -(-(ETILES + 8) // P)
ECOLS = ECHUNKS * P
SET = 8
AHEAD = 3
LEAD = 3
BR = 2 * E
NO_NODE = 8000
FAR = 9999.0
EPS = 1e-5
TABLE = 1024.0
WALL = E * KD * H + E * KH * H + E * KH * D
W2_AT, W3_AT = E * KD * H, E * KD * H + E * KH * H


def places(nc, stage):
    def sb(name, shape, dt):
        return stage.enter_context(nc.sbuf_tensor(name, shape, dt))

    def pb(name, shape, dt):
        return stage.enter_context(nc.psum_tensor(name, shape, dt))

    def sem(name):
        return stage.enter_context(nc.semaphore(name))

    return sb, pb, sem


def wait_apart(eng, met, k, signal, value):
    if not isinstance(value, int):
        value = eng.snap(value)
    eng.wait_ge(met, k)
    eng.wait_ge(signal, value)


def build(nc, x, src_t, dst_t, dst_r, wl_t, wr_t, bl_b, gamma_t, beta_t, wall, wg1, bg1_c,
          bias_rows, row_mask, b3_rows, b3_mask, sel_in, wg2b, g1_t, be1_t, g2_t, be2_t, out):
    f32, f32r, f16, i32 = mybir.dt.float32, mybir.dt.float32r, mybir.dt.float16, mybir.dt.int32
    u32, bf16 = mybir.dt.uint32, mybir.dt.bfloat16
    ALU, ACT, AX = mybir.AluOpType, mybir.ActivationFunctionType, mybir.AxisListType

    with ExitStack() as whole:
        sb, pb, sem = places(nc, whole)

        table = nc.dram_tensor("table", (NPAD, 2 * D), f16).ap()
        h_rows = nc.dram_tensor("h_rows", (NPAD, D), f32).ap()
        u_rows = nc.dram_tensor("u_rows", (NPAD, D), f32).ap()

        ident = sb("ident", [P, P], f32)
        ident16 = sb("ident16", [P, P], f16)
        ones32 = sb("ones32", [P, P], f32)
        s_const = sem("s_const")
        s_ident = sem("s_ident")
        bnmv = sb("bnmv", [P, KD, 2], f32)

        with ExitStack() as graph:
            sb, pb, sem = places(nc, graph)

            stats = sb("stats", [P, KD, TILES, 6], f32)
            one16 = sb("one16", [P, 2], f16)
            zero16 = sb("zero16", [P, D], f16)
            iota_j = sb("iota_j", [P, P], f32)
            negb = sb("negb", [P, TILES], f32)
            dstc = sb("dstc", [P, ECOLS], f32)
            first_t = sb("first_t", [1, TILES], i32)
            end_t = sb("end_t", [1, TILES], i32)
            w_hi = sb("w_hi", [P, 2, KD, D], f32r)
            w_lo = sb("w_lo", [P, 2, KD, D], f32r)
            bl = sb("bl", [P, D], f32)

            with ExitStack() as stage:
                sb, pb, sem = places(nc, stage)

                NX = 4
                GROUPS = TILES // NX
                assert GROUPS % 2 == 0 and TILES == GROUPS * NX + 1
                xin = sb("xin", [P, 2 * NX, D], f32)
                lst = sb("lst", [P, 2 * NX, 6], f32)
                mv = sb("mv", [P, 2 * NX, 2], f32)
                var_s = sb("var_s", [P, 2 * NX], f32)
                mhalf = sb("mhalf", [P, NX], f32)
                rstd = sb("rstd", [P, 2 * NX], f32)
                xs = sb("xs", [P, 2 * NX, D], f32)
                pair = sb("pair", [P, 2 * NX, 2 * D], f16)
                s_x = [sem(f"s_x{u}") for u in range(2 * NX)]
                s_store = [sem(f"s_store{u}") for u in range(2 * NX)]
                s_lst, s_mv, s_var, s_r, s_xs, s_hi, s_lo = (
                    sem(f"s_t_{n}") for n in ("lst", "mv", "var", "r", "xs", "hi", "lo"))

                dsti = sb("dsti", [P, ECOLS], i32)
                dri = sb("dri", [P, ECHUNKS, P], i32)
                drf = sb("drf", [P, ECHUNKS, P], f32)
                dmin = sb("dmin", [P, ECHUNKS], f32)
                dmax = sb("dmax", [P, ECHUNKS], f32)
                etp1 = sb("etp1", [P, ECHUNKS], f32)
                etneg = sb("etneg", [P, ECHUNKS], f32)
                base = sb("base", [P, TILES], f32)
                topn = sb("topn", [P, TILES], f32)
                rel0 = sb("rel0", [P, TILES], f32)
                rel = sb("rel", [P, TILES], f32)
                ends = sb("ends", [P, 2, TILES], f32)
                endr = sb("endr", [P, 2, TILES], f32)
                first_f = sb("first_f", [1, TILES], f32)
                s_edge = sem("s_edge")
                s_iota = sem("s_iota")
                s_bd = sem("s_bd")
                s_all = sem("s_all")
                s_bounds = sem("s_bounds")

                wst = sb("wst", [P, 2, KD, D], f32)
                s_wst = sem("s_wst")
                s_whi = sem("s_whi")
                s_wlo = sem("s_wlo")

                def over_groups(eng, body):
                    body(0, 0, 0)
                    body(1, 1, 0)
                    with eng.Fori(1, GROUPS // 2 - 1) as i:
                        body(i * 2, 0, i)
                        body(i * 2 + 1, 1, i)
                    body(GROUPS - 2, 0, GROUPS // 2 - 1)
                    body(GROUPS - 1, 1, GROUPS // 2 - 1)
                    body(GROUPS, 0, GROUPS // 2)

                def fixed(g):
                    return isinstance(g, int)

                def size(g):
                    return 1 if fixed(g) and g == GROUPS else NX

                block = stage.enter_context(nc.Block())

                @block.sync
                def _(sp):
                    for t in range(2 * NX):
                        sp.dma_start(xin[:, t, :], x[t * P:(t + 1) * P, :]).then_inc(s_x[t], 16)
                    sp.dma_start(dsti[:, :], dst_t).then_inc(s_edge, 16)
                    sp.dma_start(dri[:, :, :], dst_r).then_inc(s_edge, 16)
                    sp.dma_start(wst[:, 0, :, :], wl_t).then_inc(s_wst, 16)
                    sp.dma_start(wst[:, 1, :, :], wr_t).then_inc(s_wst, 16)
                    sp.dma_start(bl[:, :], bl_b).then_inc(s_wst, 16)

                    def step(g, w, i):
                        for u in range(size(g)):
                            t, s = g * NX + u, w * NX + u
                            ahead = t + 2 * NX
                            if not fixed(g) or ahead < TILES:
                                n = LAST if fixed(g) and ahead == TILES - 1 else P
                                sp.wait_ge(s_xs, t + 1)
                                sp.dma_start(xin[0:n, s, :], x[bass.ds(ahead * P, n), :]).then_inc(s_x[s], 16)
                        for u in range(size(g)):
                            t, s = g * NX + u, w * NX + u
                            sp.wait_ge(s_hi, t + 1)
                            sp.wait_ge(s_lo, t + 1)
                            sp.dma_start(table[bass.ds(t * P, P), :], pair[:, s, :]).then_inc(s_store[s], 16)
                    over_groups(sp, step)
                    for s in range(2 * NX):
                        sp.wait_ge(s_store[s], 16 * (GROUPS // 2 + (s == 0)))

                @block.gpsimd
                def _(pool):
                    nc.gpsimd.memset(mhalf[:, :], -0.5).then_inc(s_ident, 1)
                    nc.gpsimd.memset(ident[:, :], 0.0).then_inc(s_ident, 1)
                    nc.gpsimd.memset(ones32[:, :], 1.0).then_inc(s_ident, 1)
                    pool.wait_ge(s_ident, 3)
                    nc.gpsimd.affine_select(out=ident[:, :], in_=ident[:, :], compare_op=ALU.not_equal,
                                            fill=1.0, base=0, pattern=[[-1, P]],
                                            channel_multiplier=1).then_inc(s_ident, 1)
                    pool.wait_ge(s_ident, 4)
                    nc.gpsimd.tensor_copy(ident16[:, :], ident[:, :])
                    for tile, first, step, n, per_row in (
                            (iota_j, 0, 1, P, 0), (base, 0, P, TILES, 0), (topn, P - 1, P, TILES, 0),
                            (negb, 0, -P, TILES, 0), (etp1, 1, P, ECHUNKS, 1),
                            (etneg, int(FAR), -P, ECHUNKS, -1)):
                        nc.gpsimd.iota(tile[:, :], pattern=[[step, n]], base=first,
                                       channel_multiplier=per_row,
                                       allow_small_or_imprecise_dtypes=True).then_inc(s_iota, 1)

                    def power(g, w):
                        n = size(g)
                        pool.wait_ge(s_var, g + 1)
                        nc.gpsimd.tensor_tensor(rstd[:, w * NX:w * NX + n], var_s[:, w * NX:w * NX + n],
                                                mhalf[:, 0:n], ALU.pow).then_inc(s_r, 1)

                    power(0, 0)

                    def step(g, w, i):
                        for u in range(size(g)):
                            if u == 2:
                                power(g + 1, 1 - w)
                            pool.wait_ge(s_hi, g * NX + u + 1)
                            s = w * NX + u
                            nc.gpsimd.tensor_tensor(pair[:, s, D:], xs[:, s, :], pair[:, s, 0:D],
                                                    ALU.subtract).then_inc(s_lo, 1)
                    over_groups(pool, step)

                    pool.wait_ge(s_bd, 4 + 4 * ECHUNKS)
                    nc.gpsimd.partition_all_reduce(endr[:, :, :], ends[:, :, :], P,
                                                   bass.bass_isa.ReduceOp.max).then_inc(s_all, 1)

                @block.vector
                def _(dve):
                    nc.vector.memset(zero16[:, :], 0.0)
                    nc.vector.memset(one16[:, :], 1.0).then_inc(s_const, 1)

                    def sums(g, w, i):
                        for u in range(size(g)):
                            dve.wait_ge(s_x[w * NX + u], (i + 1) * 16)
                            last = nc.vector.bn_stats(lst[:, w * NX + u, :], xin[:, w * NX + u, :])
                        last.then_inc(s_lst, 1)

                    def variance(g, w):
                        n = size(g)
                        for u in range(n):
                            last = nc.vector.bn_aggr(mv[:, w * NX + u, :], lst[:, w * NX + u, :])
                        last.then_inc(s_mv, 1)
                        dve.wait_ge(s_mv, g + 1)
                        nc.vector.tensor_scalar(var_s[:, w * NX:w * NX + n], mv[:, w * NX:w * NX + n, 1],
                                                EPS, TABLE ** -2, ALU.add, ALU.mult).then_inc(s_var, 1)

                    sums(0, 0, 0)
                    dve.wait_ge(s_lst, 1)
                    variance(0, 0)

                    def step(g, w, i):
                        more = not fixed(g) or g < GROUPS
                        if more:
                            sums(g + 1, 1 - w, i + w)
                        dve.wait_ge(s_r, g + 1)
                        if more:
                            dve.wait_ge(s_lst, g + 2)
                        for u in range(size(g)):
                            if not fixed(g) or g > 1:
                                dve.wait_ge(s_lo, (g - 2) * NX + u + 1)
                            nc.vector.tensor_scalar(xs[:, w * NX + u, :], xin[:, w * NX + u, :],
                                                    mv[:, w * NX + u, 0:1], rstd[:, w * NX + u:w * NX + u + 1],
                                                    ALU.subtract, ALU.mult).then_inc(s_xs, 1)
                        if more:
                            variance(g + 1, 1 - w)
                    over_groups(dve, step)

                    dve.wait_ge(s_edge, 32)
                    dve.wait_ge(s_iota, 6)
                    nc.vector.tensor_copy(dstc[:, :], dsti[:, :])
                    nc.vector.memset(ends[:, :, :], 0.0).then_inc(s_bd, 1)
                    nc.vector.tensor_copy(drf[:, :, :], dri[:, :, :]).then_inc(s_bd, 1)
                    dve.wait_ge(s_bd, 2)
                    nc.vector.tensor_reduce(dmin[:, :], drf[:, :, :], AX.X, ALU.min).then_inc(s_bd, 1)
                    nc.vector.tensor_reduce(dmax[:, :], drf[:, :, :], AX.X, ALU.max).then_inc(s_bd, 1)
                    dve.wait_ge(s_bd, 4)
                    for c in range(ECHUNKS):
                        n = 4 + 4 * c
                        nc.vector.tensor_scalar(rel0[:, :], base[:, :], dmax[:, c:c + 1], None,
                                                ALU.is_le).then_inc(s_bd, 1)
                        dve.wait_ge(s_bd, n + 1)
                        nc.vector.scalar_tensor_tensor(out=rel[:, :], in0=topn[:, :],
                                                       scalar=dmin[:, c:c + 1], in1=rel0[:, :],
                                                       op0=ALU.is_ge, op1=ALU.mult).then_inc(s_bd, 1)
                        dve.wait_ge(s_bd, n + 2)
                        for j, score in enumerate((etp1, etneg)):
                            nc.vector.scalar_tensor_tensor(out=ends[:, j, :], in0=rel[:, :],
                                                           scalar=score[:, c:c + 1], in1=ends[:, j, :],
                                                           op0=ALU.mult, op1=ALU.max).then_inc(s_bd, 1)
                        dve.wait_ge(s_bd, n + 4)
                    dve.wait_ge(s_whi, 1)
                    nc.vector.tensor_tensor(w_lo[:, :, :, :], wst[:, :, :, :],
                                            w_hi[:, :, :, :].bitcast(f32), ALU.subtract)
                    dve.wait_ge(s_all, 1)
                    nc.vector.tensor_scalar(first_f[:, :], endr[0:1, 1, :], -1.0, FAR, ALU.mult, ALU.add
                                            ).then_inc(s_bounds, 1)
                    dve.wait_ge(s_bounds, 1)
                    nc.vector.tensor_scalar(first_f[:, :], first_f[:, :], float(ETILES - 1), None, ALU.min
                                            ).then_inc(s_bounds, 1)
                    dve.wait_ge(s_bounds, 2)
                    nc.vector.tensor_copy(first_t[:, :], first_f[:, :])
                    nc.vector.scalar_tensor_tensor(out=end_t[:, :], in0=first_f[:, :], scalar=1.0,
                                                   in1=endr[0:1, 0, :], op0=ALU.add, op1=ALU.max)

                @block.scalar
                def _(act):
                    def step(g, w, i):
                        for u in range(size(g)):
                            s = w * NX + u
                            act.wait_ge(s_xs, g * NX + u + 1)
                            if not fixed(g) or g > 1:
                                act.wait_ge(s_store[s], i * 16)
                            nc.scalar.activation(pair[:, s, 0:D], xs[:, s, :], ACT.Copy).then_inc(s_hi, 1)
                    over_groups(act, step)
                    act.wait_ge(s_wst, 48)
                    nc.scalar.activation(w_hi[:, :, :, :], wst[:, :, :, :], ACT.Copy).then_inc(s_whi, 1)

            with ExitStack() as stage:
                sb, pb, sem = places(nc, stage)

                idx = sb("idx", [P, 2 * AHEAD, SET], i32)
                rows = sb("rows", [P, 2 * AHEAD, SET, 2 * D], f16)
                hot = sb("hot", [P, 2 * AHEAD, SET, P], f16)
                cden = sb("cden", [P, 2], f32)
                rcnt = sb("rcnt", [P, 2], f32)
                mean = sb("mean", [P, 2, D], f32)
                xt = sb("xt", [P, 2, 2 * D], f16)
                xu = sb("xu", [P, 2, D], f32)
                m_hi = sb("m_hi", [P, KD, P], f32r)
                m_lo = sb("m_lo", [P, KD, P], f32r)
                x_hl = sb("x_hl", [P, 2 * KD, P], f32r)
                hs = sb("hs", [P, 2, D], f32)
                agg = [pb(f"agg{v}", [P, D], f32) for v in range(2)]
                cnt = [pb(f"cnt{v}", [P, D], f32) for v in range(2)]
                ps_m = pb("ps_m", [P, KD, P], f32)
                ps_x = pb("ps_x", [P, 2 * KD, P], f16)
                ps_h = pb("ps_h", [P, D], f32)
                ps_ht = pb("ps_ht", [P, KD, P], f32)
                s_idx = [sem(f"s_idx{q}") for q in range(2 * AHEAD)]
                s_hot = sem("s_hot")
                s_got = [sem(f"s_got{q}") for q in range(2 * AHEAD)]
                s_used = sem("s_used")
                (s_agg, s_cden, s_rcnt, s_mean, s_trm, s_trx, s_mhi, s_mlo, s_xhl, s_h, s_hs, s_tht,
                 s_bs) = (sem(f"s_a_{n}") for n in ("agg", "cden", "rcnt", "mean", "trm", "trx", "mhi",
                                                    "mlo", "xhl", "h", "hs", "tht", "bs"))
                s_u1, s_u2 = sem("s_u1"), sem("s_u2")
                s_xt = [sem(f"s_xt{v}") for v in range(2)]
                s_xu = [sem(f"s_xu{v}") for v in range(2)]
                s_hst = [sem(f"s_hst{v}") for v in range(2)]
                s_ust = [sem(f"s_ust{v}") for v in range(2)]

                def over_tiles(eng, body):
                    for t in range(3):
                        body(t, t // 2, t % 2)
                    with eng.Fori(1, TILES // 2 - 1) as i:
                        body(i * 2 + 1, i, 1)
                        body(i * 2 + 2, i + 1, 0)
                    for t in range(TILES - 2, TILES + 2):
                        body(t, t // 2, t % 2)

                def there(t):
                    return not isinstance(t, int) or 0 <= t < TILES

                def size(t):
                    return LAST if isinstance(t, int) and t == TILES - 1 else P

                class Sets:

                    def __init__(self, eng, name, arrivals=False):
                        self.eng = eng
                        self.groups = eng.alloc_register(name + "_groups")
                        self.last = [eng.alloc_register(f"{name}_last{q}") for q in range(2 * AHEAD)]
                        self.arrived = [eng.alloc_register(f"{name}_arrived{q}")
                                        for q in range(2 * AHEAD * arrivals)]
                        for r in (self.groups, *self.last):
                            eng.reg_mov(r, 1)
                        for r in self.arrived:
                            eng.reg_mov(r, 0)

                    def over_groups(self, t, v, group):
                        eng = self.eng
                        first = eng.value_load(first_t[0:1, bass.ds(t, 1)], min_val=0, max_val=ETILES - 1)
                        end = eng.value_load(end_t[0:1, bass.ds(t, 1)], min_val=1, max_val=ETILES)

                        def some(e, k):
                            q = AHEAD * v + k
                            free = eng.snap(self.last[q], min_val=1, max_val=TILES * ETILES)
                            g = eng.snap(self.groups, min_val=1, max_val=TILES * ETILES)
                            group(e, end, q, free, g - 1)
                            eng.reg_add(self.groups, self.groups, 1)
                            eng.reg_mov(self.last[q], self.groups)
                            if k + 1 < AHEAD:
                                with eng.If(e + SET < end):
                                    some(e + SET, k + 1)

                        with eng.Fori(first, end, AHEAD * SET) as e:
                            some(e, 0)

                block = stage.enter_context(nc.Block())

                @block.sync
                def _(sp):
                    sets = Sets(sp, "sp")

                    def sources(e, end, q, free, g):
                        sp.wait_ge(s_used, free)
                        sp.dma_start(idx[:, q, :], src_t[:, bass.ds(e + LEAD, SET)]).then_inc(s_idx[q], 16)

                    def step(t, i, v):
                        if there(t):
                            sets.over_groups(t, v, sources)
                    over_tiles(sp, step)
                    for stored in (s_hst, s_ust):
                        sp.wait_ge(stored[0], 16 * (TILES // 2 + 1))
                        sp.wait_ge(stored[1], 16 * (TILES // 2))

                @block.gpsimd
                def _(pool):
                    sets = Sets(pool, "pool", True)

                    def gather(e, end, q, free, g):
                        def rows_of(k):
                            pool.indirect_dma_start(
                                rows[:, q, k, :], None, table,
                                bass.IndirectOffsetOnAxis(idx[:, q, k:k + 1], axis=0),
                                bounds_check=N - 1, oob_is_err=False).then_inc(s_got[q], 16)

                        pool.reg_add(sets.arrived[q], sets.arrived[q], 16)
                        arrived = pool.snap(sets.arrived[q], min_val=16, max_val=1 << 24)
                        left = pool.snap(end - e)
                        pool.wait_ge(s_const, 1)
                        pool.wait_ge(s_used, free)
                        pool.wait_ge(s_idx[q], arrived)
                        with pool.If(left >= SET):
                            for k in range(SET):
                                rows_of(k)
                        with pool.Else():
                            rows_of(0)
                            for k in range(1, SET):
                                with pool.If(left > k):
                                    rows_of(k)

                    def step(t, i, v):
                        if there(t):
                            sets.over_groups(t, v, gather)
                    over_tiles(pool, step)

                @block.vector
                def _(dve):
                    sets = Sets(dve, "dve")

                    def hots(t, v):
                        def one_hot(e, end, q, free, g):
                            dve.wait_ge(s_used, free)
                            for k in range(SET):
                                last = nc.vector.tensor_scalar(hot[:, q, k, :], iota_j[:, :],
                                                               dstc[:, bass.ds(e + k, 1)],
                                                               negb[:, bass.ds(t, 1)],
                                                               ALU.subtract, ALU.is_equal)
                            last.then_inc(s_hot, 1)
                        sets.over_groups(t, v, one_hot)

                    hots(0, 0)

                    def step(t, i, v):
                        w = 1 - v
                        if there(t):
                            dve.wait_ge(s_agg, t + 1)
                            nc.vector.tensor_scalar(cden[:, v:v + 1], cnt[v][:, 0:1], 1.0, TABLE,
                                                    ALU.max, ALU.mult).then_inc(s_cden, 1)
                            dve.wait_ge(s_cden, t + 1)
                            nc.vector.reciprocal(rcnt[:, v:v + 1], cden[:, v:v + 1]).then_inc(s_rcnt, 1)
                        if there(t + 1):
                            hots(t + 1, w)
                        if there(t):
                            n = size(t)
                            dve.wait_ge(s_xt[v], 16 * (i + 1))
                            dve.wait_ge(s_xu[v], 16 * (i + 1))
                            nc.vector.scalar_tensor_tensor(out=xu[0:n, v, :], in0=xt[0:n, v, 0:D],
                                                           scalar=1.0 / TABLE, in1=xu[0:n, v, :],
                                                           op0=ALU.mult, op1=ALU.add).then_inc(s_u1, 1)
                        if there(t - 1):
                            dve.wait_ge(s_h, t)
                            if not (isinstance(t, int) and t < 3):
                                dve.wait_ge(s_hst[w], 16 * (i if v == 1 else i - 1))
                                dve.wait_ge(s_tht, t - 2)
                            nc.vector.tensor_tensor(hs[:, w, :], ps_h[:, :], bl[:, :], ALU.add
                                                    ).then_inc(s_hs, 1)
                        if there(t):
                            dve.wait_ge(s_u1, t + 1)
                            nc.vector.scalar_tensor_tensor(out=xu[0:n, v, :], in0=xt[0:n, v, D:],
                                                           scalar=1.0 / TABLE, in1=xu[0:n, v, :],
                                                           op0=ALU.mult, op1=ALU.add).then_inc(s_u2, 1)
                            dve.wait_ge(s_mhi, t + 1)
                            nc.vector.tensor_tensor(m_lo[:, :, :], ps_m[:, :, :],
                                                    m_hi[:, :, :].bitcast(f32), ALU.subtract
                                                    ).then_inc(s_mlo, 1)
                        if there(t - 2):
                            dve.wait_ge(s_tht, t - 1)
                            n = LAST if isinstance(t, int) and t == TILES + 1 else P
                            for b in range(KD):
                                nc.vector.bn_stats(stats[:, b, bass.ds(t - 2, 1), :], ps_ht[:, b, 0:n]
                                                   ).then_inc(s_bs, 1)
                    over_tiles(dve, step)
                    dve.wait_ge(s_bs, KD * TILES)
                    for b in range(KD):
                        nc.vector.bn_aggr(bnmv[:, b, :], stats[:, b, :, :])

                @block.scalar
                def _(act):
                    def fetch(t, i, v):
                        n = size(t)
                        if not (isinstance(t, int) and t < 2):
                            act.wait_ge(s_trx, t - 1)
                            act.wait_ge(s_u2, t - 1)
                            act.wait_ge(s_ust[v], 16 * i)
                        act.dma_start(xt[:, v, :], table[bass.ds(t * P, P), :]).then_inc(s_xt[v], 16)
                        act.dma_start(xu[0:n, v, :], x[bass.ds(t * P, n), :]).then_inc(s_xu[v], 16)

                    def step(t, i, v):
                        if there(t):
                            fetch(t, i, v)
                            act.wait_ge(s_rcnt, t + 1)
                            nc.scalar.activation(mean[:, v, :], agg[v][:, :], ACT.Copy,
                                                 scale=rcnt[:, v:v + 1]).then_inc(s_mean, 1)
                            act.wait_ge(s_trx, t + 1)
                            nc.scalar.activation(x_hl[:, :, :], ps_x[:, :, :], ACT.Copy, scale=1.0 / TABLE
                                                 ).then_inc(s_xhl, 1)
                            act.wait_ge(s_trm, t + 1)
                            nc.scalar.activation(m_hi[:, :, :], ps_m[:, :, :], ACT.Copy).then_inc(s_mhi, 1)
                        if there(t - 1):
                            act.wait_ge(s_hs, t)
                            act.dma_start(h_rows[bass.ds((t - 1) * P, P), :], hs[:, 1 - v, :]
                                          ).then_inc(s_hst[1 - v], 16)
                        if there(t):
                            n = size(t)
                            act.wait_ge(s_u2, t + 1)
                            act.dma_start(u_rows[bass.ds(t * P, n), :], xu[0:n, v, :]
                                          ).then_inc(s_ust[v], 16)
                    over_tiles(act, step)

                @block.tensor
                def _(pe):
                    pe.sem_inc(s_used, 1)
                    sets = Sets(pe, "pe", True)

                    def gather(t, v):
                        def add(q, k):
                            for cols in (slice(0, D), slice(D, 2 * D)):
                                nc.tensor.matmul(agg[v][:, :], hot[:, q, k, :], rows[:, q, k, cols],
                                                 start=False, stop=False)
                            nc.tensor.matmul(cnt[v][:, 0:2], hot[:, q, k, :], one16[:, :],
                                             start=False, stop=False)

                        def group(e, end, q, free, g):
                            hots = pe.snap(g + 1)
                            left = pe.snap(end - e)
                            with pe.If(left >= SET):
                                pe.reg_add(sets.arrived[q], sets.arrived[q], 16 * SET)
                            with pe.Else():
                                pe.reg_add(sets.arrived[q], sets.arrived[q], 16)
                                for k in range(1, SET):
                                    with pe.If(left > k):
                                        pe.reg_add(sets.arrived[q], sets.arrived[q], 16)
                            arrived = pe.snap(sets.arrived[q], min_val=16, max_val=1 << 24)
                            pe.wait_ge(s_hot, hots)
                            pe.wait_ge(s_got[q], arrived)
                            add(q, 0)
                            with pe.If(left >= SET):
                                for k in range(1, SET):
                                    add(q, k)
                            with pe.Else():
                                for k in range(1, SET):
                                    with pe.If(left > k):
                                        add(q, k)
                            nc.tensor.matmul(cnt[v][:, 0:2], zero16[:, 0:P], zero16[:, 0:2],
                                             start=False, stop=False).then_inc(s_used, 1)

                        nc.tensor.matmul(agg[v][:, :], zero16[:, 0:P], zero16[:, :], start=True, stop=False)
                        nc.tensor.matmul(cnt[v][:, 0:2], zero16[:, 0:P], zero16[:, 0:2],
                                         start=True, stop=False)
                        sets.over_groups(t, v, group)
                        nc.tensor.matmul(agg[v][:, :], zero16[:, 0:P], zero16[:, :], start=False, stop=True)
                        nc.tensor.matmul(cnt[v][:, 0:2], zero16[:, 0:P], zero16[:, 0:2],
                                         start=False, stop=True).then_inc(s_agg, 1)

                    def linear(t):
                        pe.wait_ge(s_xhl, t + 1)
                        if there(t - 1):
                            pe.wait_ge(s_hs, t)
                        for b in range(KD):
                            for a, w in ((b, w_hi), (b, w_lo), (KD + b, w_hi)):
                                nc.tensor.matmul(ps_h[:, :], x_hl[:, a, :], w[:, 1, b, :],
                                                 start=(b == 0 and w is w_hi and a == b), stop=False)
                        pe.wait_ge(s_mlo, t + 1)
                        for b in range(KD):
                            for a, w in ((m_hi, w_hi), (m_hi, w_lo), (m_lo, w_hi)):
                                last = nc.tensor.matmul(ps_h[:, :], a[:, b, :], w[:, 0, b, :],
                                                        start=False, stop=(b == KD - 1 and a is m_lo))
                        last.then_inc(s_h, 1)

                    def turn(t, i, v):
                        pe.wait_ge(s_xt[v], 16 * (i + 1))
                        for b in range(2 * KD):
                            last = nc.tensor.transpose(ps_x[:, b, :], xt[:, v, b * P:(b + 1) * P],
                                                       ident16[:, :])
                        last.then_inc(s_trx, 1)
                        pe.wait_ge(s_mean, t + 1)
                        for b in range(KD):
                            last = nc.tensor.transpose(ps_m[:, b, :], mean[:, v, b * P:(b + 1) * P],
                                                       ident[:, :])
                        last.then_inc(s_trm, 1)

                    def turn_h(t, v):
                        pe.wait_ge(s_hs, t + 1)
                        if there(t - 1):
                            pe.wait_ge(s_bs, t * KD)
                        for b in range(KD):
                            last = nc.tensor.transpose(ps_ht[:, b, :], hs[:, v, b * P:(b + 1) * P],
                                                       ident[:, :])
                        last.then_inc(s_tht, 1)

                    def step(t, i, v):
                        if there(t):
                            gather(t, v)
                        if there(t - 1):
                            linear(t - 1)
                        if there(t):
                            turn(t, i, v)
                        if there(t - 2):
                            turn_h(t - 2, v)
                    over_tiles(pe, step)

        sb, pb, sem = places(nc, whole)
        w_hi = sb("we_hi", [P, WALL], f32r)
        w_lo = sb("we_lo", [P, WALL], f32r)
        scale_r = sb("scale_r", [P, D], f32)
        shift_r = sb("shift_r", [P, D], f32)
        bias_hl = sb("bias_hl", [BR, D], f32r)
        sel = sb("sel", [BR, E], f32r)
        b3_hl = sb("b3_hl", [3 * E, D], f32r)
        wg1_hi = sb("wg1_hi", [P, KD, G], f32r)
        wg1_lo = sb("wg1_lo", [P, KD, G], f32r)
        bg1 = sb("bg1", [G, 1], f32)
        wg2 = sb("wg2", [P, E], f32)
        g1, be1, g2, be2 = (sb(n, [P, E * KH], f32) for n in ("g1", "be1", "g2", "be2"))

        with ExitStack() as stage:
            sb, pb, sem = places(nc, stage)

            CH, RING = 1024, 4
            wst = sb("wst2", [P, RING, CH], f32)
            gb = sb("gb", [P, 2, KD], f32)
            small = sb("small", [P, 8], f32)
            mh = sb("mh2", [P, KD], f32)
            bsc = sb("bsc", [P, 2, KD], f32)
            diag = sb("diag", [P, 2, KD, P], f32)
            bstage, bd, bh2 = ([sb(f"{n}{k}", [r, D], f32) for k, r in enumerate((BR, 3 * E))]
                               for n in ("bstage", "bd", "bh2"))
            bh = [sb(f"bh{k}", [r, D], f32r) for k, r in enumerate((BR, 3 * E))]
            rmask = [sb(f"rmask{k}", [r, 2], f32) for k, r in enumerate((BR, 3 * E))]
            self32 = sb("self32", [BR, E], f32)
            wgst = sb("wgst", [P, KD, G], f32)
            ps_row = [pb(f"ps_row{j}", [P, D], f32) for j in range(2)]
            s_ws = [sem(f"s_ws{j}") for j in range(RING)]
            s_wh, s_wl, s_cin, s_zero = sem("s_wh"), sem("s_wl"), sem("s_cin"), sem("s_zero")
            s_bn, s_bp, s_diag, s_row, s_k = sem("s_bn"), sem("s_bp"), sem("s_diag"), sem("s_row"), sem("s_k")
            s_kh = sem("s_kh")
            NCH = WALL // CH

            block = stage.enter_context(nc.Block())

            @block.sync
            def _(sp):
                for c in range(NCH):
                    if c >= RING:
                        sp.wait_ge(s_wl, c - RING + 1)
                    sp.dma_start(wst[:, c % RING, :], wall[:, c * CH:(c + 1) * CH]
                                 ).then_inc(s_ws[c % RING], 16)

            @block.scalar
            def _(act):
                act.dma_start(gb[:, 0, :], gamma_t).then_inc(s_cin, 16)
                act.dma_start(gb[:, 1, :], beta_t).then_inc(s_cin, 16)
                for k, (rows_of, mask) in enumerate(((bias_rows, row_mask), (b3_rows, b3_mask))):
                    act.dma_start(bstage[k][:, :], rows_of).then_inc(s_cin, 16)
                    act.dma_start(rmask[k][:, :], mask).then_inc(s_cin, 16)
                act.dma_start(self32[:, :], sel_in).then_inc(s_cin, 16)
                act.dma_start(wgst[:, :, :], wg1).then_inc(s_cin, 16)
                act.dma_start(bg1[:, :], bg1_c).then_inc(s_cin, 16)
                for tile, a in ((g1, g1_t), (be1, be1_t), (g2, g2_t), (be2, be2_t)):
                    act.dma_start(tile[:, :], a).then_inc(s_cin, 16)
                act.wait_ge(s_zero, 1)
                act.dma_start(wg2[0:G + 1, :], wg2b).then_inc(s_cin, 16)
                for c in range(NCH):
                    act.wait_ge(s_ws[c % RING], 16 * (c // RING + 1))
                    nc.scalar.activation(w_hi[:, c * CH:(c + 1) * CH], wst[:, c % RING, :], ACT.Copy
                                         ).then_inc(s_wh, 1)

            @block.gpsimd
            def _(pool):
                nc.gpsimd.memset(mh[:, :], -0.5).then_inc(s_bp, 1)
                nc.gpsimd.memset(wg2[:, :], 0.0).then_inc(s_zero, 1)
                pool.wait_ge(s_bn, KD + 1)
                pool.wait_ge(s_bp, 1)
                nc.gpsimd.tensor_tensor(small[:, 0:KD], small[:, KD:2 * KD], mh[:, :], ALU.pow
                                        ).then_inc(s_bp, 1)

            @block.vector
            def _(dve):
                nc.vector.tensor_scalar(small[:, KD:2 * KD], bnmv[:, :, 1], EPS, None, ALU.add
                                        ).then_inc(s_bn, KD + 1)
                dve.wait_ge(s_bp, 2)
                dve.wait_ge(s_cin, 16 * 14)
                nc.vector.tensor_tensor(bsc[:, 0, :], small[:, 0:KD], gb[:, 0, :], ALU.mult).then_inc(s_k, 1)
                dve.wait_ge(s_k, 1)
                nc.vector.tensor_tensor(mh[:, :], bsc[:, 0, :], bnmv[:, :, 0], ALU.mult).then_inc(s_k, 1)
                dve.wait_ge(s_k, 2)
                nc.vector.tensor_tensor(bsc[:, 1, :], gb[:, 1, :], mh[:, :], ALU.subtract).then_inc(s_k, 1)
                dve.wait_ge(s_k, 3)
                for j in range(2):
                    for b in range(KD):
                        nc.vector.tensor_scalar(diag[:, j, b, :], ident[:, :], bsc[:, j, b:b + 1], None,
                                                ALU.mult).then_inc(s_diag, 1)
                for k in range(2):
                    nc.vector.tensor_copy(bh[k][:, :], bstage[k][:, :])
                nc.vector.tensor_copy(sel[:, :], self32[:, :])
                nc.vector.tensor_copy(wg1_hi[:, :, :], wgst[:, :, :]).then_inc(s_k, 1)
                dve.wait_ge(s_k, 4)
                nc.vector.tensor_tensor(wg1_lo[:, :, :], wgst[:, :, :], wg1_hi[:, :, :].bitcast(f32),
                                        ALU.subtract)
                for k in range(2):
                    nc.vector.tensor_tensor(bd[k][:, :], bstage[k][:, :], bh[k][:, :].bitcast(f32),
                                            ALU.subtract)
                    nc.vector.tensor_scalar(bh2[k][:, :], bh[k][:, :].bitcast(f32), rmask[k][:, 0:1],
                                            None, ALU.mult).then_inc(s_k, 1)
                dve.wait_ge(s_k, 6)
                for k, both in enumerate((bias_hl, b3_hl)):
                    nc.vector.scalar_tensor_tensor(out=both[:, :], in0=bd[k][:, :],
                                                   scalar=rmask[k][:, 1:2], in1=bh2[k][:, :],
                                                   op0=ALU.mult, op1=ALU.add).then_inc(s_k, 1)
                for c in range(NCH):
                    dve.wait_ge(s_wh, c + 1)
                    nc.vector.tensor_tensor(w_lo[:, c * CH:(c + 1) * CH], wst[:, c % RING, :],
                                            w_hi[:, c * CH:(c + 1) * CH].bitcast(f32), ALU.subtract
                                            ).then_inc(s_wl, 1)
                dve.wait_ge(s_row, 2)
                nc.vector.tensor_copy(scale_r[:, :], ps_row[0][:, :])
                nc.vector.tensor_copy(shift_r[:, :], ps_row[1][:, :])

            @block.tensor
            def _(pe):
                pe.wait_ge(s_diag, 2 * KD)
                for j in range(2):
                    for b in range(KD):
                        last = nc.tensor.matmul(ps_row[j][:, b * P:(b + 1) * P], ones32[:, :],
                                                diag[:, j, b, :], start=True, stop=True)
                    last.then_inc(s_row, 1)

        with ExitStack() as stage:
            sb, pb, sem = places(nc, stage)

            PAIRS = E // 2
            W = 2 * H
            xa = sb("xa", [P, 2, D], f32)
            ht = sb("ht", [P, D], f32)
            acc = sb("acc", [P, 2, D], f32)
            t_hi = sb("t_hi", [P, 2, KD, P], f32r)
            t_lo = sb("t_lo", [P, 2, KD, P], f32r)
            z = [sb(f"z{y}", [P, W], f32) for y in range(2)]
            gel = [sb(f"gel{y}", [P, 4, P], f32) for y in range(2)]
            a_hi = [sb(f"a_hi{y}", [P, 4, P], f32r) for y in range(2)]
            a_lo = [sb(f"a_lo{y}", [P, 4, P], f32r) for y in range(2)]
            st = [sb(f"st{y}", [P, 2, 6], f32) for y in range(3)]
            mv = [sb(f"mvy{y}", [P, 2, 2], f32) for y in range(3)]
            rs = [sb(f"rs{y}", [P, 2], f32) for y in range(3)]
            ve = [sb(f"ve{y}", [P, 2], f32) for y in range(3)]
            mhalf = sb("mhalf2", [P, 2], f32)
            minus1 = sb("minus1", [P, 2], f32)
            epsilon = sb("epsilon", [P, 2], f32)
            negm = sb("negm", [P, 2], f32)
            shift = sb("shift", [P, 2], f32)
            euler = sb("euler", [P, 2], f32)
            iota8 = sb("iota8", [P, E], f32)
            gt = sb("gt", [G + 1, P], f32)
            cwx = sb("cwx", [P, 3 * E], f32r)
            cwt = sb("cwt", [3 * E, P], f32r)
            top = sb("top", [P, 8], f32)
            topi = sb("topi", [P, 8], u32)
            topf = sb("topf", [P, 8], f32)
            lm, ex, sums = (sb(n, [P, 2], f32) for n in ("lm", "ex", "sums"))
            ca, cb = (sb(n, [P, E], f32) for n in ("ca", "cb"))
            wtop = sb("wtop", [P, 2], f32)
            cw = sb("cw", [P, 2, E], f32)
            ps_1 = [pb(f"ps_1{v}", [P, W], f32) for v in range(2)]
            ps_2 = pb("ps_2", [P, W], f32)
            ps_t = [pb(f"ps_t{y}", [P, 4, P], f32) for y in range(2)]
            ps_3 = [pb(f"ps_3{e}", [P, D], f32) for e in range(2)]
            ps_p = pb("ps_p", [P, 4, P], f32)

            s_c0, s_load, s_loadx = sem("s_c0"), sem("s_load"), [sem("s_lx0"), sem("s_lx1")]
            s_bn1, s_bn2, s_x1, s_pst, s_pmv, s_pve, s_ppow, s_tn, s_ttr, s_thi, s_tlo = (
                sem(f"s_p_{n}") for n in ("bn1", "bn2", "x1", "st", "mv", "ve", "pow", "tn", "ttr", "thi",
                                          "tlo"))
            (s_g1, s_gt, s_g2, s_top, s_lm, s_topi, s_topf, s_ex, s_sum, s_rec, s_wtop, s_cab, s_cw,
             s_cwh, s_cwl, s_cwtr, s_cwt, s_b3, s_bias) = (
                sem(f"s_g_{n}") for n in ("g1", "gt", "g2", "top", "lm", "topi", "topf", "ex", "sum",
                                          "rec", "wtop", "cab", "cw", "cwh", "cwl", "cwtr", "cwt", "b3",
                                          "bias"))
            s_l = [sem(f"s_l{y}") for y in range(3)]
            s_st, s_mv, s_ve, s_pow, s_z, s_tr, s_gl, s_ah, s_al = (
                [sem(f"s_{n}{y}") for y in range(2)]
                for n in ("st", "mv", "ve", "pow", "z", "tr", "gl", "ah", "al"))
            s_shift = sem("s_shift")
            s_cmb = sem("s_cmb")
            s_out = [sem("s_out0"), sem("s_out1")]

            def units(eng, body):
                body(0, 0, 0)
                with eng.Fori(0, (TILES - 5) // 2) as j:
                    body(j * 2 + 1, 1, j)
                    body(j * 2 + 2, 0, j + 1)
                for t in range(TILES - 4, TILES + 1):
                    body(t, t % 2, t // 2)

            def lives(t, p, lag):
                return not isinstance(t, int) or 0 <= t * PAIRS + p - lag < TILES * PAIRS

            def before(t, first):
                return not (isinstance(t, int) and t < first)

            block = stage.enter_context(nc.Block())

            @block.sync
            def _(sp):
                def load(t, v, j):
                    n = LAST if isinstance(t, int) and t == TILES - 1 else P
                    if before(t, 1):
                        sp.wait_ge(s_ttr, t)
                    sp.dma_start(ht[:, :], h_rows[bass.ds(t * P, P), :]).then_inc(s_load, 16)
                    if before(t, 2):
                        sp.wait_ge(s_cmb, t * E - 15)
                    sp.dma_start(xa[0:n, v, :], u_rows[bass.ds(t * P, n), :]).then_inc(s_loadx[v], 16)

                def store(t, v, j, n=P):
                    sp.wait_ge(s_cmb, t * E + E)
                    sp.dma_start(out[bass.ds(t * P, n), :], acc[0:n, v, :]).then_inc(s_out[v], 16)

                load(0, 0, 0)
                load(1, 1, 0)

                def step(t, v, j):
                    if not isinstance(t, int) or t <= TILES - 3:
                        load(t + 2, v, j + 1)
                    if before(t, 1):
                        store(t - 1, 1 - v, j, LAST if isinstance(t, int) and t == TILES else P)
                units(sp, step)
                sp.wait_ge(s_out[0], 16 * (TILES // 2 + 1))
                sp.wait_ge(s_out[1], 16 * (TILES // 2))

            @block.gpsimd
            def _(pool):
                nc.gpsimd.memset(mhalf[:, :], -0.5)
                nc.gpsimd.memset(minus1[:, :], -1.0)
                nc.gpsimd.memset(epsilon[:, :], EPS)
                nc.gpsimd.memset(euler[:, :], 2.718281828459045)
                nc.gpsimd.memset(gt[:, :], 1.0).then_inc(s_c0, 1)
                nc.gpsimd.iota(iota8[:, :], pattern=[[1, E]], base=0, channel_multiplier=0,
                               allow_small_or_imprecise_dtypes=True).then_inc(s_c0, 1)
                pool.wait_ge(s_c0, 2)

                def scales(t, y, p, lag):
                    if not lives(t, p, lag):
                        return
                    n = t * PAIRS + (p - lag)
                    pool.wait_ge(s_mv[y], n + 1)
                    if y == 0 and (before(t, 1) or n >= 1):
                        pool.wait_ge(s_z[0], n)
                    if y == 0:
                        nc.gpsimd.tensor_tensor(negm[:, :], mv[0][:, :, 0], minus1[:, :], ALU.mult)
                    nc.gpsimd.tensor_tensor(ve[y][:, :], mv[y][:, :, 1], epsilon[:, :], ALU.add
                                            ).then_inc(s_ve[y], 1)
                    pool.wait_ge(s_ve[y], n + 1)
                    nc.gpsimd.tensor_tensor(rs[y][:, :], ve[y][:, :], mhalf[:, :], ALU.pow
                                            ).then_inc(s_pow[y], 1)
                    if y == 0:
                        pool.wait_ge(s_pow[0], n + 1)
                        nc.gpsimd.tensor_tensor(shift[:, :], negm[:, :], rs[0][:, :], ALU.mult
                                                ).then_inc(s_shift, 1)

                def split(t, p, y, lag):
                    if not lives(t, p, lag):
                        return
                    n = t * PAIRS + (p - lag)
                    pool.wait_ge(s_ah[y], n + 1)
                    nc.gpsimd.tensor_tensor(a_lo[y][:, :, :], gel[y][:, :, :],
                                            a_hi[y][:, :, :].bitcast(f32), ALU.subtract
                                            ).then_inc(s_al[y], 1)

                def prepare(t):
                    pool.wait_ge(s_pmv, t + 1)
                    nc.gpsimd.tensor_tensor(ve[2][:, 0:1], mv[2][:, 0, 1:2], epsilon[:, 0:1], ALU.add
                                            ).then_inc(s_pve, 1)
                    pool.wait_ge(s_pve, t + 1)
                    nc.gpsimd.tensor_tensor(rs[2][:, 0:1], ve[2][:, 0:1], mhalf[:, 0:1], ALU.pow
                                            ).then_inc(s_ppow, 1)

                prepare(0)

                def step(t, v, j):
                    for p in range(PAIRS):
                        if p == 3 and not (isinstance(t, int) and t == TILES):
                            pool.wait_ge(s_lm, t + 1)
                            nc.gpsimd.tensor_tensor(ex[:, :], euler[:, :], lm[:, :], ALU.pow
                                                    ).then_inc(s_ex, 1)
                        scales(t, 0, p, 0)
                        scales(t, 1, p, 2)
                        if p == 2 and not (isinstance(t, int) and t >= TILES - 1):
                            prepare(t + 1)
                        split(t, p, 0, 1)
                        split(t, p, 1, 3)
                units(pool, step)

            @block.vector
            def _(dve):
                dve.wait_ge(s_c0, 2)

                def sums_of(t, p, y, lag):
                    if not lives(t, p, lag):
                        return
                    n = t * PAIRS + (p - lag)
                    src = ps_1[p % 2] if y == 0 else ps_2
                    dve.wait_ge(s_l[y], n + 1)
                    if y == 0 and (before(t, 1) or n >= 1):
                        dve.wait_ge(s_shift, n)
                    for e in range(2):
                        last = nc.vector.bn_stats(st[y][:, e, :], src[:, e * H:(e + 1) * H])
                    last.then_inc(s_st[y], 1)

                def moments(t, p, y, lag):
                    if not lives(t, p, lag):
                        return
                    n = t * PAIRS + (p - lag)
                    wait_apart(dve, s_c0, 2, s_st[y], n + 1)
                    for e in range(2):
                        last = nc.vector.bn_aggr(mv[y][:, e, :], st[y][:, e, :])
                    last.then_inc(s_mv[y], 1)

                def normal(t, p):
                    if not lives(t, p, 2):
                        return
                    n = t * PAIRS + (p - 2)
                    dve.wait_ge(s_pow[1], n + 1)
                    if before(t, 2) or n >= 1:
                        dve.wait_ge(s_tr[1], n)
                    for e in range(2):
                        last = nc.vector.tensor_scalar(z[1][:, e * H:(e + 1) * H],
                                                       ps_2[:, e * H:(e + 1) * H],
                                                       mv[1][:, e, 0:1], rs[1][:, e:e + 1],
                                                       ALU.subtract, ALU.mult)
                    last.then_inc(s_z[1], 1)

                def combine(t, v, j, p, e):
                    if not lives(t, p, 4):
                        return
                    n = t * E + (2 * p - E)
                    first = p == 0 and e == 0
                    if e == 0:
                        dve.wait_ge(s_l[2], t * PAIRS + (p - 4) + 1)
                    if first:
                        dve.wait_ge(s_cw, t)
                        if before(t, 3):
                            dve.wait_ge(s_out[1 - v], 16 * (j - 1 if v == 0 else j))
                    else:
                        dve.wait_ge(s_cmb, n + e)
                    if p == 3 and e == 0:
                        dve.wait_ge(s_bias, t)
                    nc.vector.scalar_tensor_tensor(
                        out=acc[:, 1 - v, :], in0=ps_3[e][:, :], scalar=cw[:, 1 - v, 2 * p + e:2 * p + e + 1],
                        in1=(xa if first else acc)[:, 1 - v, :], op0=ALU.mult, op1=ALU.add
                    ).then_inc(s_cmb, 1)

                def batch_norm_scale(t):
                    dve.wait_ge(s_load, t * 16 + 16)
                    nc.vector.tensor_tensor(ht[:, :], ht[:, :], scale_r[:, :], ALU.mult).then_inc(s_bn1, 1)

                def batch_norm_shift(t):
                    dve.wait_ge(s_bn1, t + 1)
                    nc.vector.tensor_tensor(ht[:, :], ht[:, :], shift_r[:, :], ALU.add).then_inc(s_bn2, 1)

                def graph_part(t, v, j):
                    dve.wait_ge(s_loadx[v], 16 * (j + 1))
                    dve.wait_ge(s_bn2, t + 1)
                    nc.vector.scalar_tensor_tensor(out=xa[:, v, :], in0=ht[:, :], scalar=0.0,
                                                   in1=xa[:, v, :], op0=ALU.max, op1=ALU.add
                                                   ).then_inc(s_x1, 1)

                def row_sums(t, v):
                    dve.wait_ge(s_x1, t + 1)
                    nc.vector.bn_stats(st[2][:, 0, :], xa[:, v, :]).then_inc(s_pst, 1)

                def row_moments(t):
                    wait_apart(dve, s_c0, 2, s_pst, t + 1)
                    nc.vector.bn_aggr(mv[2][:, 0, :], st[2][:, 0, :]).then_inc(s_pmv, 1)

                def layer_norm(t, v):
                    dve.wait_ge(s_ppow, t + 1)
                    nc.vector.tensor_scalar(ht[:, :], xa[:, v, :], mv[2][:, 0, 0:1], rs[2][:, 0:1],
                                            ALU.subtract, ALU.mult).then_inc(s_tn, 1)

                def low(t, v):
                    dve.wait_ge(s_thi, t + 1)
                    nc.vector.tensor_tensor(t_lo[:, v, :, :], ps_p[:, :, :], t_hi[:, v, :, :].bitcast(f32),
                                            ALU.subtract).then_inc(s_tlo, 1)

                def largest(t):
                    wait_apart(dve, s_c0, 2, s_g2, t + 1)
                    nc.vector.max(top[:, :], ps_p[:, 0, 0:E]).then_inc(s_top, 1)

                def minus_largest(t):
                    wait_apart(dve, s_c0, 2, s_top, t + 1)
                    nc.vector.max_index(topi[:, :], top[:, :], ps_p[:, 0, 0:E]).then_inc(s_topi, 1)
                    nc.vector.tensor_scalar(lm[:, :], top[:, 0:2], top[:, 0:1], None, ALU.subtract
                                            ).then_inc(s_lm, 1)

                def numbers(t):
                    dve.wait_ge(s_topi, t + 1)
                    nc.vector.tensor_copy(topf[:, 0:2], topi[:, 0:2]).then_inc(s_topf, 1)

                def total(t):
                    dve.wait_ge(s_ex, t + 1)
                    nc.vector.tensor_tensor(sums[:, 0:1], ex[:, 0:1], ex[:, 1:2], ALU.add).then_inc(s_sum, 1)

                def inverse(t):
                    dve.wait_ge(s_sum, t + 1)
                    nc.vector.reciprocal(sums[:, 1:2], sums[:, 0:1]).then_inc(s_rec, 1)

                def shares(t):
                    dve.wait_ge(s_rec, t + 1)
                    nc.vector.tensor_scalar(wtop[:, :], ex[:, :], sums[:, 1:2], None, ALU.mult
                                            ).then_inc(s_wtop, 1)

                def by_expert(t):
                    dve.wait_ge(s_topf, t + 1)
                    dve.wait_ge(s_wtop, t + 1)
                    for k, c in enumerate((ca, cb)):
                        last = nc.vector.tensor_scalar(c[:, :], iota8[:, :], topf[:, k:k + 1],
                                                       wtop[:, k:k + 1], ALU.is_equal, ALU.mult)
                    last.then_inc(s_cab, 1)

                def weights(t, v):
                    dve.wait_ge(s_cab, t + 1)
                    nc.vector.tensor_tensor(cw[:, v, :], ca[:, :], cb[:, :], ALU.add).then_inc(s_cw, 1)

                def high_weights(t, v):
                    if before(t, 1):
                        dve.wait_ge(s_cwtr, t)
                    dve.wait_ge(s_cw, t + 1)
                    for at in (0, 2 * E):
                        last = nc.vector.tensor_copy(cwx[:, at:at + E], cw[:, v, :])
                    last.then_inc(s_cwh, 1)

                def low_weights(t, v):
                    dve.wait_ge(s_cwh, t + 1)
                    nc.vector.tensor_tensor(cwx[:, E:2 * E], cw[:, v, :], cwx[:, 0:E].bitcast(f32),
                                            ALU.subtract).then_inc(s_cwl, 1)

                def last_bias(t, v):
                    dve.wait_ge(s_b3, t + 1)
                    dve.wait_ge(s_cmb, t * E + 6)
                    nc.vector.tensor_tensor(acc[:, v, :], ps_p[:, :, :].rearrange("p a b -> p (a b)"),
                                            acc[:, v, :], ALU.add).then_inc(s_bias, 1)

                batch_norm_scale(0)
                batch_norm_shift(0)
                graph_part(0, 0, 0)
                row_sums(0, 0)
                row_moments(0)
                layer_norm(0, 0)
                low(0, 0)

                def step(t, v, j):
                    more = not (isinstance(t, int) and t >= TILES - 1)
                    here = not (isinstance(t, int) and t == TILES)
                    for p in range(PAIRS):
                        sums_of(t, p, 0, 0)
                        if p == 3 and here:
                            numbers(t)
                        moments(t, p, 0, 0)
                        if p == 3 and more:
                            low(t + 1, 1 - v)
                        sums_of(t, p, 1, 2)
                        if p == 3 and here:
                            total(t)
                        if p == 1 and here:
                            largest(t)
                        if p == 2 and more:
                            row_moments(t + 1)
                        moments(t, p, 1, 2)
                        if p == 0 and more:
                            batch_norm_scale(t + 1)
                        if p == 0 and before(t, 1):
                            high_weights(t - 1, 1 - v)
                        if p == 3 and here:
                            inverse(t)
                        normal(t, p)
                        if p == 0 and more:
                            batch_norm_shift(t + 1)
                        if p == 1 and more:
                            graph_part(t + 1, 1 - v, j if v == 0 else j + 1)
                        if p == 0 and before(t, 1):
                            low_weights(t - 1, 1 - v)
                        if p == 1 and here:
                            minus_largest(t)
                        if p == 2 and more:
                            layer_norm(t + 1, 1 - v)
                        if p == 3 and here:
                            shares(t)
                        combine(t, v, j, p, 0)
                        if p == 1 and more:
                            row_sums(t + 1, 1 - v)
                        if p == 3 and here:
                            by_expert(t)
                        combine(t, v, j, p, 1)
                        if p == 2 and before(t, 1):
                            last_bias(t - 1, 1 - v)
                        if p == 3 and here:
                            weights(t, v)
                units(dve, step)

            @block.scalar
            def _(act):
                def gelu(t, p, y, lag):
                    if not lives(t, p, lag):
                        return
                    n = t * PAIRS + (p - lag)
                    pair = (p - lag) % PAIRS
                    act.wait_ge(s_tr[y], n + 1)
                    if before(t, 2) or n >= 1:
                        act.wait_ge(s_al[y], n)
                    for c in range(4):
                        col = pair * 4 + c
                        last = nc.scalar.activation(gel[y][:, c, :], ps_t[y][:, c, :], ACT.Gelu,
                                                    scale=(g1, g2)[y][:, col:col + 1],
                                                    bias=(be1, be2)[y][:, col:col + 1])
                    last.then_inc(s_gl[y], 1)
                    act.wait_ge(s_gl[y], n + 1)
                    if before(t, 2) or n >= 1:
                        act.wait_ge(s_l[y + 1], n)
                    nc.scalar.activation(a_hi[y][:, :, :], gel[y][:, :, :], ACT.Copy).then_inc(s_ah[y], 1)

                def normal(t, p):
                    if not lives(t, p, 0):
                        return
                    n = t * PAIRS + p
                    act.wait_ge(s_shift, n + 1)
                    if before(t, 1) or n >= 1:
                        act.wait_ge(s_tr[0], n)
                    for e in range(2):
                        last = nc.scalar.activation(z[0][:, e * H:(e + 1) * H],
                                                    ps_1[p % 2][:, e * H:(e + 1) * H], ACT.Identity,
                                                    scale=rs[0][:, e:e + 1], bias=shift[:, e:e + 1])
                    last.then_inc(s_z[0], 1)

                def high(t, v):
                    act.wait_ge(s_ttr, t + 1)
                    nc.scalar.activation(t_hi[:, v, :, :], ps_p[:, :, :], ACT.Copy).then_inc(s_thi, 1)

                high(0, 0)

                def step(t, v, j):
                    more = not (isinstance(t, int) and t >= TILES - 1)
                    here = not (isinstance(t, int) and t == TILES)
                    for p in range(PAIRS):
                        if p == 3 and more:
                            high(t + 1, 1 - v)
                        if p == 2 and before(t, 1):
                            act.wait_ge(s_cwtr, t)
                            if before(t, 2):
                                act.wait_ge(s_b3, t - 1)
                            nc.scalar.activation(cwt[:, :], ps_p[0:3 * E, 0, :], ACT.Copy
                                                 ).then_inc(s_cwt, 1)
                        gelu(t, p, 0, 1)
                        normal(t, p)
                        if p == 0 and here:
                            act.wait_ge(s_g1, t + 1)
                            if before(t, 1):
                                act.wait_ge(s_g2, t)
                            nc.scalar.activation(gt[0:G, :], ps_p[0:G, 0, :], ACT.Gelu, bias=bg1[:, 0:1]
                                                 ).then_inc(s_gt, 1)
                        gelu(t, p, 1, 3)
                units(act, step)

            @block.tensor
            def _(pe):
                pe.wait_ge(s_c0, 2)

                def three(out, pairs, start, stop):
                    passes = [(a, w) for ah, al, wh, wl in pairs for a, w in ((ah, wh), (ah, wl), (al, wh))]
                    for k, (a, w) in enumerate(passes):
                        last = nc.tensor.matmul(out, a, w, start=start and k == 0,
                                                stop=stop and k == len(passes) - 1)
                    return last

                def bias(out, row, cols):
                    nc.tensor.matmul(out, sel[:, row:row + 1].to_broadcast([BR, P]), bias_hl[:, cols],
                                     start=True, stop=False)

                def transpose(t, v):
                    pe.wait_ge(s_tn, t + 1)
                    if before(t, 1):
                        pe.wait_ge(s_topi, t)
                    if before(t, 2):
                        pe.wait_ge(s_bias, t - 1)
                    for b in range(KD):
                        last = nc.tensor.transpose(ps_p[:, b, :], ht[:, b * P:(b + 1) * P], ident[:, :])
                    last.then_inc(s_ttr, 1)

                def layer1(t, p, v):
                    if not lives(t, p, 0):
                        return
                    n = t * PAIRS + p
                    if p == 0:
                        pe.wait_ge(s_tlo, t + 1)
                    if before(t, 1) or n >= 2:
                        pe.wait_ge(s_z[0], n - 1)
                    o = ps_1[p % 2][:, :]
                    bias(o, p, slice(0, D))
                    three(o, [(t_hi[:, v, b, :], t_lo[:, v, b, :],
                               w_hi[:, (p * KD + b) * W:(p * KD + b + 1) * W],
                               w_lo[:, (p * KD + b) * W:(p * KD + b + 1) * W]) for b in range(KD)],
                          False, True).then_inc(s_l[0], 1)

                def turn(t, p, y, lag):
                    if not lives(t, p, lag):
                        return
                    n = t * PAIRS + (p - lag)
                    pe.wait_ge(s_z[y], n + 1)
                    if before(t, 2) or n >= 1:
                        pe.wait_ge(s_gl[y], n)
                    for c in range(4):
                        last = nc.tensor.transpose(ps_t[y][:, c, :], z[y][:, c * P:(c + 1) * P], ident[:, :])
                    last.then_inc(s_tr[y], 1)

                def layer2(t, p):
                    if not lives(t, p, 2):
                        return
                    n = t * PAIRS + (p - 2)
                    pair = (p - 2) % PAIRS
                    pe.wait_ge(s_al[0], n + 1)
                    if before(t, 2) or n >= 1:
                        pe.wait_ge(s_z[1], n)
                    nc.tensor.matmul(ps_2[:, :], sel[:, 4 + pair:5 + pair].to_broadcast([BR, P]),
                                     bias_hl[:, :], start=True, stop=False)
                    for e in range(2):
                        at = [W2_AT + ((2 * pair + e) * KH + b) * H for b in range(KH)]
                        last = three(ps_2[:, e * H:(e + 1) * H],
                                     [(a_hi[0][:, 2 * e + b, :], a_lo[0][:, 2 * e + b, :],
                                       w_hi[:, at[b]:at[b] + H], w_lo[:, at[b]:at[b] + H])
                                      for b in range(KH)], False, e == 1)
                    last.then_inc(s_l[1], 1)

                def layer3(t, p):
                    if not lives(t, p, 4):
                        return
                    n = t * PAIRS + (p - 4)
                    pe.wait_ge(s_al[1], n + 1)
                    if before(t, 2) or n >= 1:
                        pe.wait_ge(s_cmb, n * 2)
                    for e in range(2):
                        at = [W3_AT + ((2 * p + e) * KH + b) * D for b in range(KH)]
                        last = three(ps_3[e][:, :],
                                     [(a_hi[1][:, 2 * e + b, :], a_lo[1][:, 2 * e + b, :],
                                       w_hi[:, at[b]:at[b] + D], w_lo[:, at[b]:at[b] + D])
                                      for b in range(KH)], True, True)
                    last.then_inc(s_l[2], 1)

                transpose(0, 0)

                def step(t, v, j):
                    more = not (isinstance(t, int) and t >= TILES - 1)
                    here = not (isinstance(t, int) and t == TILES)
                    for p in range(PAIRS):
                        layer1(t, p, v)
                        if p == 1 and here:
                            pe.wait_ge(s_gt, t + 1)
                            nc.tensor.matmul(ps_p[:, 0, 0:E], gt[:, :], wg2[0:G + 1, :], start=True,
                                             stop=True).then_inc(s_g2, 1)
                        if p == 2 and before(t, 1):
                            pe.wait_ge(s_cwl, t)
                            if here:
                                pe.wait_ge(s_topi, t + 1)
                            nc.tensor.transpose(ps_p[0:3 * E, 0, :], cwx[:, :].bitcast(f32), ident[:, :]
                                                ).then_inc(s_cwtr, 1)
                        if p == 3 and more:
                            transpose(t + 1, 1 - v)
                        layer2(t, p)
                        turn(t, p, 0, 1)
                        turn(t, p, 1, 3)
                        if p == 0 and here:
                            three(ps_p[0:G, 0, :], [(wg1_hi[:, b, :], wg1_lo[:, b, :], t_hi[:, v, b, :],
                                                     t_lo[:, v, b, :]) for b in range(KD)], True, True
                                  ).then_inc(s_g1, 1)
                        if p == 2 and before(t, 1):
                            pe.wait_ge(s_cwt, t)
                            nc.tensor.matmul(ps_p[:, :, :], cwt[:, :], b3_hl[:, :], start=True, stop=True
                                             ).then_inc(s_b3, 1)
                        layer3(t, p)
                units(pe, step)


def kernel(x, src, dst, L0_gnn_W_l, L0_gnn_b_l, L0_gnn_W_r, L0_gnn_gamma, L0_gnn_beta, L0_ffn_Wg1,
           L0_ffn_bg1, L0_ffn_Wg2, L0_ffn_bg2, L0_ffn_W1, L0_ffn_b1, L0_ffn_g1, L0_ffn_be1, L0_ffn_W2,
           L0_ffn_b2, L0_ffn_g2, L0_ffn_be2, L0_ffn_W3, L0_ffn_b3):
    import numpy as np
    import concourse.bacc as bacc
    from concourse.bass_utils import run_bass_kernel_spmd

    def arr(a):
        return np.ascontiguousarray(a)

    def edges(a, fill):
        return np.concatenate([np.asarray(a), np.full(ECOLS * P - EDGES, fill, np.int32)])

    def by_block(w):
        w = np.asarray(w)
        return w.reshape(-1, P, w.shape[-1]).transpose(1, 0, 2)

    def column(a):
        return arr(np.asarray(a).reshape(-1, P).T)

    def experts(w):
        w = np.asarray(w)
        return w.reshape(E, -1, P, w.shape[-1]).transpose(2, 0, 1, 3).reshape(P, -1)

    src_p, dst_p = edges(src, 0), edges(dst, NO_NODE)
    w1 = np.asarray(L0_ffn_W1).reshape(E // 2, 2, KD, P, H).transpose(3, 0, 2, 1, 4).reshape(P, -1)
    b1, b2 = (np.asarray(b).reshape(E // 2, 2 * H) for b in (L0_ffn_b1, L0_ffn_b2))
    b3 = np.asarray(L0_ffn_b3)
    sel = np.zeros((BR, E), np.float32)
    row_mask = np.zeros((BR, 2), np.float32)
    n = E // 2
    for at, col in ((0, 0), (2 * n, n)):
        for j in range(n):
            sel[at + j, col + j] = sel[at + n + j, col + j] = 1.0
            row_mask[at + j, 0] = row_mask[at + n + j, 1] = 1.0
    b3_mask = np.zeros((3 * E, 2), np.float32)
    b3_mask[:2 * E, 0] = b3_mask[2 * E:, 1] = 1.0
    given = {
        "x": arr(x),
        "src_t": arr(np.concatenate([np.zeros((P, LEAD), np.int32), src_p.reshape(ECOLS, P).T], axis=1)),
        "dst_t": arr(dst_p.reshape(ECOLS, P).T),
        "dst_r": arr(dst_p.reshape(ECHUNKS, P, P).transpose(1, 0, 2)),
        "wl_t": arr(by_block(np.asarray(L0_gnn_W_l).T)),
        "wr_t": arr(by_block(np.asarray(L0_gnn_W_r).T)),
        "bl_b": arr(np.broadcast_to(np.asarray(L0_gnn_b_l), (P, D))),
        "gamma_t": column(L0_gnn_gamma),
        "beta_t": column(L0_gnn_beta),
        "wall": arr(np.concatenate([w1, experts(L0_ffn_W2), experts(L0_ffn_W3)], axis=1)),
        "wg1": arr(by_block(L0_ffn_Wg1)),
        "bg1_c": arr(np.asarray(L0_ffn_bg1).reshape(G, 1)),
        "bias_rows": arr(np.concatenate([b1, b1, b2, b2])),
        "row_mask": row_mask,
        "b3_rows": arr(np.concatenate([b3, b3, b3])),
        "b3_mask": b3_mask,
        "sel_in": sel,
        "wg2b": arr(np.concatenate([np.asarray(L0_ffn_Wg2), np.asarray(L0_ffn_bg2)[None, :]])),
        "g1_t": column(L0_ffn_g1), "be1_t": column(L0_ffn_be1),
        "g2_t": column(L0_ffn_g2), "be2_t": column(L0_ffn_be2),
    }
    nc = bacc.Bacc("TRN2", target_bir_lowering=False, num_devices=1)
    args = [nc.dram_tensor(n, a.shape, mybir.dt.from_np(a.dtype), kind="ExternalInput").ap()
            for n, a in given.items()]
    out = nc.dram_tensor("out", (N, D), mybir.dt.float32, kind="ExternalOutput").ap()
    build(nc, *args, out)
    r = run_bass_kernel_spmd(nc, [given], core_ids=[0])
    return r.results[0]["out"]
```
